# Optimizing a Trainium2 kernel written in Bass

```python
import numpy as np
import jax
import jax.numpy as jnp

def _softmax(x, axis=-1):
    return jax.nn.softmax(x, axis=axis)

def _gelu(x):
    return jax.nn.gelu(x, approximate=True)

def _silu(x):
    return jax.nn.silu(x)

def _sigmoid(x):
    return jax.nn.sigmoid(x)

def _layernorm(x, axis=-1, eps=1e-05):
    m = jnp.mean(x, axis=axis, keepdims=True)
    v = jnp.var(x, axis=axis, keepdims=True)
    return (x - m) / jnp.sqrt(v + eps)

def _scatter_add(tgt, idx, src, axis=0):
    return tgt.at[idx].add(src)

def _segment_sum(src, seg, n):
    return jax.ops.segment_sum(src, seg, n)
kernel_name = 'mk_vit_tower_cls_d2_tok_img1024_r4_5b7847'

def setup_inputs(seed: int=0):
    np.random.seed(seed)
    _w = jnp.asarray

    def _rec_inputs():
        import jax
        import jax.numpy as jnp
        _rk = jax.random.key(seed)
        x = -0.00011082 + 0.999858 * jax.random.normal(jax.random.fold_in(_rk, 1), (2, 5, 128, 128), jnp.float32)
        cls_tok = 0.02 * jax.random.normal(jax.random.fold_in(_rk, 5), (1, 1, 256), jnp.float32)
        return (x, cls_tok)
    x, cls_tok = _rec_inputs()

    def _L0_tok_setup():
        import jax, jax.numpy as jnp
        import numpy as np
        PATCH = 8
        EPS = 1e-05

        def _patchify(x):
            B, C, H, Wd = x.shape
            p = PATCH
            x = x.reshape(B, C, H // p, p, Wd // p, p)
            x = x.transpose(0, 2, 4, 1, 3, 5)
            return x.reshape(B, H // p * (Wd // p), C * p * p)
        key = jax.random.key(seed)
        k1, k2 = jax.random.split(key)
        B, C, H, W_ = (32, 5, 128, 128)
        in_feat, embed_dim = (C * PATCH * PATCH, 256)
        x = jax.random.normal(k1, (B, C, H, W_), dtype=jnp.float32)
        W = jax.random.normal(k2, (in_feat, embed_dim), dtype=jnp.float32) * (1.0 / np.sqrt(in_feat))
        gamma = jnp.ones((embed_dim,), dtype=jnp.float32)
        return {'x': x, 'W': W, 'gamma': gamma}
    _L0_tok_all = _L0_tok_setup()
    _L0_tok_in = {k: v for k, v in _L0_tok_all.items() if k in ('W', 'gamma')}
    del _L0_tok_all

    def _L0_attn_setup():
        import jax, jax.numpy as jnp
        import numpy as np
        import math
        D = 256
        key = jax.random.key(seed)
        ks = jax.random.split(key, 5)
        B, S = (4, 512)
        scale = 1.0 / math.sqrt(D)
        x = jax.random.normal(ks[0], (B, S, D), dtype=jnp.float32)
        W_qkv = jax.random.normal(ks[1], (D, 3 * D), dtype=jnp.float32) * scale
        b_qkv = jax.random.normal(ks[2], (3 * D,), dtype=jnp.float32) * 0.01
        W_out = jax.random.normal(ks[3], (D, D), dtype=jnp.float32) * scale
        b_out = jax.random.normal(ks[4], (D,), dtype=jnp.float32) * 0.01
        return {'x': x, 'W_qkv': W_qkv, 'b_qkv': b_qkv, 'W_out': W_out, 'b_out': b_out}
    _L0_attn_all = _L0_attn_setup()
    _L0_attn_in = {k: v for k, v in _L0_attn_all.items() if k in ('W_qkv', 'b_qkv', 'W_out', 'b_out')}
    del _L0_attn_all

    def _L0_ffn_setup():
        import jax, jax.numpy as jnp
        import numpy as np
        TOP_K = 2

        def _route(x2d, gate_w, num_experts, top_k):
            scores = jax.nn.softmax((x2d @ gate_w.T).astype(jnp.float32), axis=1)
            top_scores, sel = jax.lax.top_k(scores, top_k)
            sel_flat = sel.reshape(-1)
            counts = jnp.bincount(sel_flat, length=num_experts)
            order = jnp.argsort(sel_flat, stable=True)
            top_scores_sorted = top_scores.reshape(-1)[order]
            token_idx = order // top_k
            return (top_scores_sorted, token_idx, counts)

        def _grouped_swiglu(xr, w1, w2, w3, eid):
            out = jnp.zeros((xr.shape[0], w2.shape[-1]), dtype=xr.dtype)
            for e in range(w1.shape[0]):
                xe = jnp.where((eid == e)[:, None], xr, 0.0)
                h = jax.nn.silu(xe @ w1[e]) * (xe @ w3[e])
                out = out + h @ w2[e]
            return out
        key = jax.random.key(seed)
        ks = jax.random.split(key, 5)
        bs, slen, dim, hidden, E = (2, 512, 256, 704, 8)
        x = jax.random.normal(ks[0], (bs, slen, dim), dtype=jnp.float32)
        gate_w = jax.random.normal(ks[1], (E, dim), dtype=jnp.float32) * 0.02
        w1 = jax.random.normal(ks[2], (E, dim, hidden), dtype=jnp.float32) * 0.02
        w2 = jax.random.normal(ks[3], (E, hidden, dim), dtype=jnp.float32) * 0.02
        w3 = jax.random.normal(ks[4], (E, dim, hidden), dtype=jnp.float32) * 0.02
        return {'x': x, 'gate_w': gate_w, 'w1': w1, 'w2': w2, 'w3': w3}
    _L0_ffn_all = _L0_ffn_setup()
    _L0_ffn_in = {k: v for k, v in _L0_ffn_all.items() if k in ('gate_w', 'w1', 'w2', 'w3')}
    del _L0_ffn_all

    def _L1_attn_setup():
        import jax, jax.numpy as jnp
        import numpy as np
        key = jax.random.key(seed)
        k1, k2, k3 = jax.random.split(key, 3)
        B, S, D, N = (2, 512, 256, 16)
        H = D // N
        x = jax.random.normal(k1, (B, S, D), dtype=jnp.float32)
        W_qkv = jax.random.normal(k2, (N, D, 3 * H), dtype=jnp.float32) / np.sqrt(D).astype(np.float32)
        W_out = jax.random.normal(k3, (N, H, D), dtype=jnp.float32) / np.sqrt(D).astype(np.float32)
        return {'x': x, 'W_qkv': W_qkv, 'W_out': W_out}
    _L1_attn_all = _L1_attn_setup()
    _L1_attn_in = {k: v for k, v in _L1_attn_all.items() if k in ('W_qkv', 'W_out')}
    del _L1_attn_all

    def _L1_ffn_setup():
        import jax, jax.numpy as jnp
        import numpy as np
        B, S, D = (2, 256, 256)
        E, K, F, FS = (8, 2, 128, 256)
        key = jax.random.key(seed)
        ks = jax.random.split(key, 9)
        s = lambda k, shape, fan: jax.random.normal(k, shape, jnp.float32) * fan ** (-0.5)
        return {'x': jax.random.normal(ks[0], (B, S, D), jnp.float32), 'Wr': s(ks[1], (D, E), D), 'Wg': s(ks[2], (E, D, F), D), 'Wu': s(ks[3], (E, D, F), D), 'Wd': s(ks[4], (E, F, D), F), 'Sg': s(ks[5], (D, FS), D), 'Su': s(ks[6], (D, FS), D), 'Sd': s(ks[7], (FS, D), FS), 'expert_bias': jnp.zeros((E,), jnp.float32)}
    _L1_ffn_all = _L1_ffn_setup()
    _L1_ffn_in = {k: v for k, v in _L1_ffn_all.items() if k in ('Wr', 'Wg', 'Wu', 'Wd', 'Sg', 'Su', 'Sd', 'expert_bias')}
    del _L1_ffn_all
    return {'x': x, 'cls_tok': cls_tok, 'L0_tok_W': _L0_tok_in['W'], 'L0_tok_gamma': _L0_tok_in['gamma'], 'L0_attn_W_qkv': _L0_attn_in['W_qkv'], 'L0_attn_b_qkv': _L0_attn_in['b_qkv'], 'L0_attn_W_out': _L0_attn_in['W_out'], 'L0_attn_b_out': _L0_attn_in['b_out'], 'L0_ffn_gate_w': _L0_ffn_in['gate_w'], 'L0_ffn_w1': _L0_ffn_in['w1'], 'L0_ffn_w2': _L0_ffn_in['w2'], 'L0_ffn_w3': _L0_ffn_in['w3'], 'L1_attn_W_qkv': _L1_attn_in['W_qkv'], 'L1_attn_W_out': _L1_attn_in['W_out'], 'L1_ffn_Wr': _L1_ffn_in['Wr'], 'L1_ffn_Wg': _L1_ffn_in['Wg'], 'L1_ffn_Wu': _L1_ffn_in['Wu'], 'L1_ffn_Wd': _L1_ffn_in['Wd'], 'L1_ffn_Sg': _L1_ffn_in['Sg'], 'L1_ffn_Su': _L1_ffn_in['Su'], 'L1_ffn_Sd': _L1_ffn_in['Sd'], 'L1_ffn_expert_bias': _L1_ffn_in['expert_bias']}

def reference(x, cls_tok, L0_tok_W, L0_tok_gamma, L0_attn_W_qkv, L0_attn_b_qkv, L0_attn_W_out, L0_attn_b_out, L0_ffn_gate_w, L0_ffn_w1, L0_ffn_w2, L0_ffn_w3, L1_attn_W_qkv, L1_attn_W_out, L1_ffn_Wr, L1_ffn_Wg, L1_ffn_Wu, L1_ffn_Wd, L1_ffn_Sg, L1_ffn_Su, L1_ffn_Sd, L1_ffn_expert_bias):
    import jax
    import jax.numpy as jnp

    def _L0_tok_ref(x, W, gamma):
        import jax, jax.numpy as jnp
        import numpy as np
        PATCH = 8
        EPS = 1e-05

        def _patchify(x):
            B, C, H, Wd = x.shape
            p = PATCH
            x = x.reshape(B, C, H // p, p, Wd // p, p)
            x = x.transpose(0, 2, 4, 1, 3, 5)
            return x.reshape(B, H // p * (Wd // p), C * p * p)
        tokens = _patchify(x)
        h = jnp.einsum('bnf,fd->bnd', tokens, W)
        mu = jnp.mean(h, axis=-1, keepdims=True)
        var = jnp.mean(jnp.square(h - mu), axis=-1, keepdims=True)
        out = (h - mu) * jax.lax.rsqrt(var + EPS) * gamma
        return out

    def _L0_attn_ref(x, W_qkv, b_qkv, W_out, b_out):
        import jax, jax.numpy as jnp
        import numpy as np
        import math
        D = 256
        qkv = x @ W_qkv + b_qkv
        q, k, v = jnp.split(qkv, 3, axis=-1)
        inv_sqrt_d = 1.0 / math.sqrt(D)
        scores = jnp.einsum('bqd,bkd->bqk', q, k) * inv_sqrt_d
        attn = jax.nn.softmax(scores, axis=-1)
        ctx = jnp.einsum('bqk,bkd->bqd', attn, v)
        return ctx @ W_out + b_out

    def _L0_ffn_ref(x, gate_w, w1, w2, w3):
        import jax, jax.numpy as jnp
        import numpy as np
        TOP_K = 2

        def _route(x2d, gate_w, num_experts, top_k):
            scores = jax.nn.softmax((x2d @ gate_w.T).astype(jnp.float32), axis=1)
            top_scores, sel = jax.lax.top_k(scores, top_k)
            sel_flat = sel.reshape(-1)
            counts = jnp.bincount(sel_flat, length=num_experts)
            order = jnp.argsort(sel_flat, stable=True)
            top_scores_sorted = top_scores.reshape(-1)[order]
            token_idx = order // top_k
            return (top_scores_sorted, token_idx, counts)

        def _grouped_swiglu(xr, w1, w2, w3, eid):
            out = jnp.zeros((xr.shape[0], w2.shape[-1]), dtype=xr.dtype)
            for e in range(w1.shape[0]):
                xe = jnp.where((eid == e)[:, None], xr, 0.0)
                h = jax.nn.silu(xe @ w1[e]) * (xe @ w3[e])
                out = out + h @ w2[e]
            return out
        bs, slen, dim = x.shape
        E, top_k = (gate_w.shape[0], TOP_K)
        x2d = x.reshape(bs * slen, dim)
        top_scores, token_idx, counts = _route(x2d, gate_w, E, top_k)
        routed_in = (x2d[token_idx].astype(jnp.float32) * top_scores[:, None]).astype(x.dtype)
        Tr = bs * slen * top_k
        eid = jnp.repeat(jnp.arange(E), counts, total_repeat_length=Tr)
        routed_out = _grouped_swiglu(routed_in, w1, w2, w3, eid)
        out = jnp.zeros((bs * slen, dim), dtype=x.dtype).at[token_idx].add(routed_out)
        return out.reshape(bs, slen, dim)

    def _L1_attn_ref(x, W_qkv, W_out):
        import jax, jax.numpy as jnp
        import numpy as np
        B, S, D = x.shape
        head_dim = W_qkv.shape[-1] // 3
        qkv = jnp.einsum('bsd,ndh->bnsh', x, W_qkv)
        q, k, v = jnp.split(qkv, 3, axis=-1)
        scale = jnp.asarray(1.0 / np.sqrt(head_dim), dtype=x.dtype)
        attn = jnp.einsum('bnqh,bnkh->bnqk', q, k) * scale
        mask = jnp.asarray(-10000000000.0, dtype=x.dtype) * (1.0 - jnp.tril(jnp.ones((S, S), dtype=x.dtype)))
        attn = jax.nn.softmax(attn + mask, axis=-1)
        out = jnp.einsum('bnqk,bnkh->bnqh', attn, v)
        out = out.reshape(B, -1, S)
        return jnp.einsum('bds,nhd->bsd', out, W_out)

    def _L1_ffn_ref(x, Wr, Wg, Wu, Wd, Sg, Su, Sd, expert_bias):
        import jax, jax.numpy as jnp
        import numpy as np
        B, S, D = (2, 256, 256)
        E, K, F, FS = (8, 2, 128, 256)
        b, s, d = x.shape
        xf = x.reshape(-1, d)
        T = xf.shape[0]
        logits = xf @ Wr + expert_bias
        top_v, top_i = jax.lax.top_k(logits, K)
        probs = jax.nn.softmax(top_v, axis=-1)
        rw = jnp.zeros_like(logits).at[jnp.arange(T)[:, None], top_i].set(probs)
        gate = jnp.einsum('td,edf->tef', xf, Wg)
        up = jnp.einsum('td,edf->tef', xf, Wu)
        h = jax.nn.silu(gate) * up
        eo = jnp.einsum('tef,efd->ted', h, Wd)
        out = jnp.einsum('te,ted->td', rw, eo)
        out = out + jax.nn.silu(xf @ Sg) * (xf @ Su) @ Sd
        return out.reshape(b, s, d)
    h = _L0_tok_ref(x, L0_tok_W, L0_tok_gamma)
    h = jnp.concatenate([jnp.broadcast_to(cls_tok, (h.shape[0], 1, h.shape[2])), h], axis=1)
    h = h + _L0_attn_ref(_layernorm(h, axis=-1), L0_attn_W_qkv, L0_attn_b_qkv, L0_attn_W_out, L0_attn_b_out)
    h = h + _L0_ffn_ref(_layernorm(h, axis=-1), L0_ffn_gate_w, L0_ffn_w1, L0_ffn_w2, L0_ffn_w3)
    h = h + _L1_attn_ref(_layernorm(h, axis=-1), L1_attn_W_qkv, L1_attn_W_out)
    h = h + _L1_ffn_ref(_layernorm(h, axis=-1), L1_ffn_Wr, L1_ffn_Wg, L1_ffn_Wu, L1_ffn_Wd, L1_ffn_Sg, L1_ffn_Su, L1_ffn_Sd, L1_ffn_expert_bias)
    return h

_drawn_inputs = setup_inputs


def setup_inputs(seed=0):
    import zlib

    import numpy as np

    out = dict(_drawn_inputs(seed))
    spreads = {'L0_tok_gamma': (1.0, 0.2), 'L1_ffn_expert_bias': (0.0, 0.717)}
    factors = {'L0_ffn_gate_w': 6.337, 'L0_ffn_w1': 7.715, 'L0_ffn_w2': 8.0, 'L0_ffn_w3': 8.0}
    for name, (base, spread) in spreads.items():
        noise = np.random.default_rng([zlib.crc32(name.encode()), seed]).standard_normal(out[name].shape)
        drawn = base * np.exp(spread * noise) if base else spread * noise
        out[name] = jnp.asarray(drawn.astype(out[name].dtype))
    for name, factor in factors.items():
        out[name] = (out[name] * factor).astype(out[name].dtype)
    return out
```

```python
from contextlib import ExitStack

import concourse.bass as bass
from concourse import mybir

F32 = mybir.dt.float32
F32R = mybir.dt.float32r
ALU = mybir.AluOpType
ACT = mybir.ActivationFunctionType
AX = mybir.AxisListType.X

P = 128
EPS = 1e-5
HUGE = 1e38


def vit_tower(nc, x, cls_tok, tok_W, tok_gamma, a0_Wqkv, a0_bqkv, a0_Wo, a0_bo, gate_w, w1, w2, w3,
              a1_Wqkv, a1_Wo, Wr, Wg, Wu, Wd, Sg, Su, Sd, ebias, out):
    NB, C, H, W = x.shape
    D = tok_W.shape[1]
    KT = D // P
    PS = 8
    HY, WX = H // PS, W // PS
    NTOK = HY * WX
    S = NTOK + 1
    N = S + 1
    CI = C * PS
    JG = 3
    NJ = (PS + JG - 1) // JG
    E, HID = w1.shape[0], w1.shape[2]
    HC = (HID + P - 1) // P
    HTAIL = HID - (HC - 1) * P
    NH, HD = a1_Wqkv.shape[0], a1_Wqkv.shape[2] // 3
    SLOT = 32
    HT = NH * SLOT // P
    HPT = P // SLOT
    F1 = Wg.shape[2]
    RT = 86
    NR = N // RT
    POS = [(0, P), (P, P), (2 * P, 1)]
    assert NR * RT == N and S == 2 * P + 1 and D == 256 and F1 == P

    WA = KT * HID
    WTOT = 2 * WA + HC * D
    STEPS = 2 * HC
    PIECES = [(i * WA // 4, WA // 4) for i in range(8)]
    PIECES += [(2 * WA + i * HC * D // 4, HC * D // 4) for i in range(4)]
    assert len(PIECES) == STEPS and E % 2 == 0
    CH1 = Sg.shape[1] // F1 + E
    NSH = CH1 - E
    OFF = 4

    ctx = ExitStack()
    with ctx:
        sems = {}

        def sem(name, b=None):
            key = name if b is None else f"{name}_{b}"
            if key not in sems:
                sems[key] = ctx.enter_context(nc.semaphore(key))
            return sems[key]

        def sb(name, shape, dt=F32):
            return ctx.enter_context(nc.sbuf_tensor(name, shape, dt))

        h = sb("h", [P, NB, KT, N])
        y = sb("y", [P, NB, KT, N])
        dev = sb("dev", [P, NB, KT, N])
        sq = sb("sq", [P, NB, KT, N])
        sd = sb("sd", [P, NB, N])
        rstd = sb("rstd", [P, NB, N])
        big = sb("big", [P, E, NB, N])
        ident = sb("ident", [P, P])
        avg = sb("avg", [P, P])
        ones = sb("ones", [P, 2])
        eps_t = sb("eps_t", [P, 1])
        rank8 = sb("rank8", [P, NR, E])
        causal = sb("causal", [P, 3 * P])
        slotmask = sb("slotmask", [P, HT, NH])
        wtok = sb("wtok", [JG * CI, NJ, D])
        gamma_t = sb("gamma_t", [P, KT])
        wqkv0 = sb("wqkv0", [P, KT, 3 * D])
        bqkv0 = sb("bqkv0", [P, 3 * KT])
        wo0 = sb("wo0", [P, KT, D])
        bo0 = sb("bo0", [P, KT])
        gw = sb("gw", [P, KT, E])
        wr1 = sb("wr1", [P, KT, E])
        ebias_t = sb("ebias_t", [RT, E])
        wqkv1 = wqkv0[:, :, :].rearrange("p k (n c) -> p k n c", n=NH)
        wq1 = sb("wq1", [P, KT, NH, SLOT])
        wk1 = sb("wk1", [P, KT, NH, SLOT])
        wo1 = wo0
        wsum = sb("wsum", [P, KT])
        assert 2 * HT == E
        qk = big[:, :, :, :].rearrange("p e b n -> p (e b n)").rearrange("p (b m n) -> p b m n", b=NB, m=2 * HT)
        v = sb("v", [P, NB, 3, D])
        prob = sb("prob", [P, NB, 3, N])
        probT = sb("probT", [P, NB, 3, N])
        cT = dev
        stat = sb("stat", [P, NB, 16])
        logit = sb("logit", [RT, NB, NR, E])
        eq = sb("eq", [RT, NB, NR, E])
        pick1 = sb("pick1", [RT, NB, NR, E])
        pick2 = sb("pick2", [RT, NB, NR, E])
        rest = sb("rest", [RT, NB, NR, E])
        route = sb("route", [RT, NB, NR, E])
        rstat = sb("rstat", [RT, NB, NR, 8])
        raw = sb("raw", [P, WTOT])
        whi = sb("whi", [P, 2, WTOT], F32R)
        wlo = sb("wlo", [P, 2, WTOT], F32R)
        xhi = sb("xhi", [P, 2, NB, KT, N], F32R)
        xlo = sb("xlo", [P, 2, NB, KT, N], F32R)
        sg = sb("sg", [P, NB, N])
        hid = sb("hid", [P, NB, N])
        hidw = sb("hidw", [P, N])
        hhi = sb("hhi", [P, 4, N], F32R)
        hlo = sb("hlo", [P, 4, N], F32R)
        zero = sb("zero", [P, N], F32R)
        two = prob[:, :, :, :].rearrange("p b t n -> p (b t n)")
        scm = two[:, 0:6 * P].rearrange("p (a n) -> p a n", a=2)
        ph = two[:, 6 * P:12 * P].rearrange("p (a n) -> p a n", a=2)
        phT = probT[:, :, :, :].rearrange("p b t n -> p (b t n)")[:, 0:6 * P].rearrange("p (a n) -> p a n", a=2)
        hmx = sb("hmx", [P, 2, 2])
        hnm = sb("hnm", [P, 2, 2])
        hsum = sb("hsum", [P, NB, 2, NH])
        hinv = sb("hinv", [P, NB, 2, NH])
        osb = sb("osb", [P, NB, 2, NH, HD])
        qlast = sb("qlast", [P, NB, HT, NH])
        plast = sb("plast", [NH, NB, N])
        plT = sb("plT", [P, NB, 3, NH])
        olm = sb("olm", [NH, NB, NH, HD])
        ol = sb("ol", [NH, NB, HD])
        ols = sb("ols", [NH, NB, HD])
        lstat = sb("lstat", [NH, NB, 4])
        patches = big[:, :, :, :].rearrange("p e b n -> p (e b n)")[0:JG * CI, 0:NB * HY * W] \
            .rearrange("p (b y w) -> p b y w", b=NB, y=HY)
        whi1 = whi[:, :, :].rearrange("p a n -> p (a n)")
        wlo1 = wlo[:, :, :].rearrange("p a n -> p (a n)")
        GU = KT * F1
        W1 = 2 * GU + D
        HALF1 = CH1 // 2
        assert HALF1 * W1 <= WTOT and CH1 * W1 <= 2 * WTOT

        heads_dram = nc.dram_tensor("heads_dram", (NB, NH, S, HD), F32, kind="Internal").ap()

        bank = [ctx.enter_context(nc.psum_tensor(f"bank{i}", [P, 512], F32)) for i in range(8)]

        def bk(b, i):
            return bank[4 * b + i]

        ctx.enter_context(nc.allow_non_contiguous_dma(reason="small per-feature vectors and one column"))
        block = ctx.enter_context(nc.Block())
        BS = range(NB)

        def f32(ap):
            return ap.bitcast(F32)

        @block.sync
        def _(sp):
            for b in BS:
                for jj in range(JG):
                    for c in range(C):
                        p0 = jj * CI + c * PS
                        sp.dma_start(patches[p0:p0 + PS, b, :, 0:W - jj],
                                     x[b, c].rearrange("(y i) w -> i y w", i=PS)[:, :, jj:W])\
                            .then_inc(sem("patches_in", b), 16)
                if b == 0:
                    wt = tok_W.rearrange("(c j) d -> c j d", j=PS)
                    for jj in range(JG):
                        ng = len(range(jj, PS, JG))
                        sp.dma_start(wtok[jj * CI:(jj + 1) * CI, 0:ng, :], wt[:, jj:PS:JG, :])\
                            .then_inc(sem("wtok_in"), 16)
            for k in range(KT):
                for b in BS:
                    sp.dma_start(h[:, b, k, 0:1], cls_tok[0, 0:1, k * P:(k + 1) * P].rearrange("a p -> p a"))\
                        .then_inc(sem("small_in"), 16)
            sp.dma_start(gamma_t[:, :], tok_gamma.rearrange("(k p) -> p k", p=P)).then_inc(sem("small_in"), 16)
            sp.dma_start(bqkv0[:, :], a0_bqkv.rearrange("(k p) -> p k", p=P)).then_inc(sem("small_in"), 16)
            sp.dma_start(bo0[:, :], a0_bo.rearrange("(k p) -> p k", p=P)).then_inc(sem("small_in"), 16)
            sp.dma_start(wqkv0[:, :, :], a0_Wqkv.rearrange("(k p) n -> p k n", p=P)).then_inc(sem("wqkv0_in"), 16)
            sp.dma_start(wo0[:, :, :], a0_Wo.rearrange("(k p) n -> p k n", p=P)).then_inc(sem("wo0_in"), 16)
            for k in range(KT):
                sp.dma_start(gw[:, k, :], gate_w[:, k * P:(k + 1) * P].rearrange("e p -> p e"))\
                    .then_inc(sem("gw_in"), 16)

            def load_expert(e, before):
                def third(n):
                    if before is not None:
                        sp.wait_ge(sem("whi_done"), before + 4 * (n + 1))
                        sp.wait_ge(sem("wlo_done"), before + 4 * (n + 1))
                for n, w in enumerate((w1, w3)):
                    third(n)
                    sp.dma_start(raw[:, n * WA:(n + 1) * WA].rearrange("p (k n) -> p k n", k=KT),
                                 w[bass.ds(e, 1)].rearrange("a (k p) n -> p (a k) n", p=P))\
                        .then_inc(sem("expert_in", n), 16)
                third(2)
                rd = raw[:, 2 * WA:WTOT].rearrange("p (c n) -> p c n", c=HC)
                sp.dma_start(rd[:, 0:HC - 1, :],
                             w2[bass.ds(e, 1), 0:(HC - 1) * P, :].rearrange("a (c p) n -> p (a c) n", p=P))\
                    .then_inc(sem("expert_in", 2), 16)
                sp.dma_start(rd[0:HTAIL, HC - 1, :], w2[bass.ds(e, 1), (HC - 1) * P:HID, :]
                             .rearrange("a p n -> p (a n)")).then_inc(sem("expert_in", 2), 16)

            sp.wait_ge(sem("tail_zero"), 1)
            load_expert(0, None)
            for k in range(KT):
                sp.dma_start(wr1[:, k, :], Wr[k * P:(k + 1) * P, :]).then_inc(sem("l1_in"), 16)
            sp.dma_start(ebias_t[:, :], ebias.rearrange("(a e) -> a e", a=1).broadcast_to([RT, E])) \
                .then_inc(sem("l1_in"), 16)
            for b in BS:
                sp.wait_ge(sem("v_mm", b), 3)
            for k in range(KT):
                sp.dma_start(wqkv1[:, k, :, :], a1_Wqkv[:, k * P:(k + 1) * P, :].rearrange("n p c -> p n c"))\
                    .then_inc(sem("wqkv1_in"), 16)
            for b in BS:
                sp.wait_ge(sem("op_mm", b), KT)
            sp.dma_start(wo1[:, :, :], a1_Wo.rearrange("n h d -> (n h) d").rearrange("(k p) d -> p k d", p=P))\
                .then_inc(sem("l1_in"), 16)
            with sp.Fori(0, E - 1) as i:
                load_expert(i + 1, STEPS * i)

            sp.wait_ge(sem("whi_done"), STEPS * E)
            sp.wait_ge(sem("wlo_done"), STEPS * E)

            def load1(at, src):
                n = src.shape[1] * src.shape[2]
                sp.dma_start(raw[:, at:at + n].rearrange("p (k n) -> p k n", k=src.shape[1]), src)\
                    .then_inc(sem("experts1_in"), 16)

            for c in range(CH1):
                at = c % HALF1 * W1
                if c == HALF1:
                    sp.wait_ge(sem("w1split_done"), HALF1)
                if c < NSH:
                    for n, m in enumerate((Sg, Su)):
                        load1(at + n * GU, m.rearrange("(k p) f -> p k f", p=P)[:, :, c * F1:(c + 1) * F1])
                    load1(at + 2 * GU, Sd[c * F1:(c + 1) * F1, :].rearrange("p (a d) -> p a d", a=1))
                else:
                    for n, m in enumerate((Wg, Wu)):
                        load1(at + n * GU, m[c - NSH].rearrange("(k p) f -> p k f", p=P))
                    load1(at + 2 * GU, Wd[c - NSH].rearrange("p (a d) -> p a d", a=1))
            for b in BS:
                sp.wait_ge(sem("osb_done", b), 2)
                for t in range(2):
                    sp.dma_start(heads_dram[b].rearrange("n s c -> s n c")[t * P:(t + 1) * P],
                                 osb[:, b, t, :, :]).then_inc(sem("heads_out", b), 16)
                sp.dma_start(heads_dram[b, :, S - 1, :], ols[:, b, :]).then_inc(sem("heads_out", b), 16)
                sp.wait_ge(sem("heads_out", b), 48)
                sp.dma_start(cT[:, b, :, 0:S],
                             heads_dram[b].rearrange("n s c -> (n s c)").rearrange("(k p s) -> p k s", k=KT, p=P))\
                    .then_inc(sem("heads_in", b), 16)
            for b in BS:
                for t, (s0, rows) in enumerate(POS):
                    sp.wait_ge(sem("y_out_ready", b), t + 1)
                    sp.dma_start(out[b, s0:s0 + rows, :], v[0:rows, b, t, :]).then_inc(sem("stored"), 16)
            sp.wait_ge(sem("stored"), 16 * 3 * NB)

        @block.gpsimd
        def _(pool):
            cnt = [0]

            def link(ins):
                cnt[0] += 1
                ins.then_inc(sem("pool_chain"), 1)
                pool.wait_ge(sem("pool_chain"), cnt[0])

            pool.memset(avg[:, :], 1.0 / D).then_inc(sem("const"), 1)
            pool.memset(eps_t[:, :], EPS).then_inc(sem("const"), 1)
            pool.memset(h[:, :, :, S:N], 0.0).then_inc(sem("const"), 1)
            pool.memset(raw[:, WTOT - D:WTOT], 0.0).then_inc(sem("tail_zero"), 1)
            link(pool.memset(ident[:, :], 0.0))
            pool.affine_select(out=ident[:, :], in_=ident[:, :], compare_op=ALU.not_equal, fill=1.0, base=0,
                               pattern=[[-1, P]], channel_multiplier=1).then_inc(sem("const"), 1)
            pool.memset(ones[:, :], 1.0).then_inc(sem("const"), 1)
            for j in range(E):
                pool.memset(rank8[:, :, j:j + 1], float(E - j)).then_inc(sem("const"), 1)
            link(pool.memset(causal[:, :], 0.0))
            for t in (0, 2):
                pool.affine_select(out=causal[:, t * P:(t + 1) * P], in_=causal[:, t * P:(t + 1) * P],
                                   compare_op=ALU.is_ge, fill=-1e10 * HD ** 0.5, base=0,
                                   pattern=[[-1, P]], channel_multiplier=1).then_inc(sem("const"), 1)
            link(pool.memset(slotmask[:, :, :], 1.0))
            link(pool.affine_select(out=slotmask[:, :, :], in_=slotmask[:, :, :], compare_op=ALU.is_ge, fill=0.0,
                                    base=0, pattern=[[P, HT], [-SLOT, NH]], channel_multiplier=1))
            pool.affine_select(out=slotmask[:, :, :], in_=slotmask[:, :, :], compare_op=ALU.is_ge, fill=0.0,
                               base=SLOT - 1, pattern=[[-P, HT], [SLOT, NH]], channel_multiplier=-1)\
                .then_inc(sem("const"), 1)
            link(pool.memset(wq1[:, :, :, :], 0.0))
            link(pool.memset(wk1[:, :, :, :], 0.0))

            def low_part(par, n, hi_count):
                at, size = PIECES[n]
                pool.wait_ge(sem("whi_done"), hi_count)
                pool.tensor_tensor(wlo[:, par, at:at + size], raw[:, at:at + size],
                                   f32(whi[:, par, at:at + size]), ALU.subtract).then_inc(sem("wlo_done"), 1)

            for n in range(STEPS):
                low_part(0, n, n + 1)
            pool.wait_ge(sem("wqkv1_in"), 32)
            pool.tensor_copy(wq1[:, :, :, 0:HD], wqkv1[:, :, :, 0:HD]).then_inc(sem("wqk1_ready"), 1)
            pool.tensor_copy(wk1[:, :, :, 0:HD], wqkv1[:, :, :, HD:2 * HD]).then_inc(sem("wqk1_ready"), 1)

            def expert(i, par, prep):
                if prep:
                    e = 2 * i + par
                    pool.wait_ge(sem("down_done"), STEPS * e + OFF)
                    for n in range(STEPS):
                        low_part(1 - par, n, STEPS * (e + 1) + n + 1)

            with pool.Fori(0, E // 2 - 1) as i:
                for par in range(2):
                    expert(i, par, True)
            expert(E // 2 - 1, 0, True)

            pool.wait_ge(sem("down_done"), STEPS * E + OFF)
            for n in range(CH1):
                if n % HALF1 == 0:
                    pool.wait_ge(sem("experts1_in"), 16 * 3 * HALF1 * (n // HALF1 + 1))
                at, r = n * W1, raw[:, n % HALF1 * W1:(n % HALF1 + 1) * W1]
                link(pool.tensor_copy(whi1[:, at:at + W1], r))
                pool.tensor_tensor(wlo1[:, at:at + W1], r, f32(whi1[:, at:at + W1]), ALU.subtract)\
                    .then_inc(sem("w1split_done"), 1)

        CONST = 3 + 1 + 1 + E + 2 + 1

        @block.scalar
        def _(act):
            act.wait_ge(sem("const"), CONST)

            def norm(n, b, cols):
                a, z = cols
                act.wait_ge(sem("ln_dev", b), n + 1)
                act.activation(sq[:, b, :, a:z], dev[:, b, :, a:z], ACT.Square).then_inc(sem("ln_sq", b), 1)

            def norm2(n, b, cols):
                a, z = cols
                act.wait_ge(sem("ln_var", b), n + 1)
                act.activation(sd[:, b, a:z], bk(b, 3)[:, a:z], ACT.Sqrt, bias=eps_t[:, 0:1])\
                    .then_inc(sem("ln_sd", b), 1)

            for b in BS:
                for m in range(KT):
                    act.wait_ge(sem("tok_mm", b), m + 1)
                    act.activation(y[:, b, m, 1:S], bk(b, m)[:, 0:NTOK], ACT.Copy).then_inc(sem("tok_sb", b), 1)
            for n in range(2):
                cols = (1, S) if n == 0 else (0, N)
                for b in BS:
                    norm(n, b, cols)
                for b in BS:
                    norm2(n, b, cols)
            act.wait_ge(sem("small_in"), 16 * (KT * NB + 3))
            for b in BS:
                for m in range(2 * KT):
                    act.wait_ge(sem("qk_mm", b), m + 1)
                    act.activation(qk[:, b, m, :], bk(b, m)[:, 0:N], ACT.Identity, bias=bqkv0[:, m:m + 1])\
                        .then_inc(sem("qk_sb", b), 1)
            for t, (_s0, rows) in enumerate(POS):
                for b in BS:
                    act.wait_ge(sem("sc_nm", b), t + 1)
                    act.activation(prob[0:rows, b, t, 0:S], bk(b, (3 + t) % 4)[0:rows, 0:S], ACT.Exp,
                                   bias=stat[0:rows, b, t:t + 1], scale=D ** -0.5,
                                   accum_out=stat[0:rows, b, 4 + t:5 + t]).then_inc(sem("sc_exp", b), 1)
            for b in BS:
                for j, (_s0, rows) in enumerate(POS):
                    act.wait_ge(sem("pt_mm", b), j + 1)
                    act.activation(probT[0:rows, b, j, 0:S], bk(b, (2 + j) % 4)[0:rows, 0:S], ACT.Copy)\
                        .then_inc(sem("pt_sb", b), 1)
            for b in BS:
                for m in range(KT):
                    act.wait_ge(sem("cx_mm", b), m + 1)
                    act.activation(cT[:, b, m, 0:S], bk(b, 1 + m)[:, 0:S], ACT.Identity,
                                   bias=bqkv0[:, 2 * KT + m:2 * KT + m + 1]).then_inc(sem("cx_sb", b), 1)

            def norms(n):
                for b in BS:
                    norm(n, b, (0, N))
                for b in BS:
                    norm2(n, b, (0, N))

            norms(2)

            def high_part(par, n, e):
                at, size = PIECES[n]
                if n % 4 == 0:
                    act.wait_ge(sem("expert_in", n // 4), (16 if n < 8 else 32) * (e + 1))
                act.activation(whi[:, par, at:at + size], raw[:, at:at + size], ACT.Copy)\
                    .then_inc(sem("whi_done"), 1)

            for n in range(STEPS):
                high_part(0, n, 0)
            for b in BS:
                act.wait_ge(sem("rt_shift", b), 1)
                act.activation(route[:, b, :, :], logit[:, b, :, :], ACT.Exp).then_inc(sem("rt_exp", b), 1)

            def copy_weights(layer):
                for e in range(E):
                    for b in BS:
                        act.wait_ge(sem("rb_mm", b), layer * E + e + 1)
                        act.activation(big[:, e, b, :], bk(b, e % 4)[:, 0:N], ACT.Copy)\
                            .then_inc(sem("rb_sb", b), 1)

            copy_weights(0)

            def x_high(par, count):
                for b in BS:
                    act.wait_ge(sem("xs_done"), count + b + 1)
                    act.activation(xhi[:, par, b, :, :], sq[:, b, :, :], ACT.Copy).then_inc(sem("xhi_done"), 1)

            x_high(0, 0)
            act.nop().then_inc(sem("silu_done"), OFF)
            act.nop().then_inc(sem("hhi_done"), OFF)

            def act_expert(i, par, prep):
                e = 2 * i + par
                if prep:
                    act.wait_ge(sem("down_done"), STEPS * e + OFF)
                for s in range(STEPS):
                    c, b = divmod(s, 2)
                    rows = P if c < HC - 1 else HTAIL
                    k = STEPS * e + s
                    act.wait_ge(sem("up_done"), k + 1)
                    act.wait_ge(sem("hmul_done"), k - 1 + OFF)
                    act.activation(sg[0:rows, b, :], bk(b, 0)[0:rows, 0:N], ACT.Silu).then_inc(sem("silu_done"), 1)
                    if prep:
                        high_part(1 - par, s, e + 1)
                        if s == 4:
                            x_high(1 - par, 2 * (e + 1))
                    act.wait_ge(sem("hmul_done"), k + 1 + OFF)
                    act.wait_ge(sem("down_done"), k - 3 + OFF)
                    act.activation(hhi[0:rows, s % 4, :], hid[0:rows, b, :], ACT.Copy)\
                        .then_inc(sem("hhi_done"), 1)

            with act.Fori(0, E // 2 - 1) as i:
                for par in range(2):
                    act_expert(i, par, True)
            act_expert(E // 2 - 1, 0, True)
            act_expert(E // 2 - 1, 1, False)

            norms(3)
            for m in range(2 * HT):
                for b in BS:
                    act.wait_ge(sem("qk1_mm", b), m + 1)
                    act.activation(qk[:, b, m, :], bk(b, m % 4)[:, 0:N], ACT.Copy).then_inc(sem("qk1_sb", b), 1)
            for b in BS:
                act.wait_ge(sem("last_nm", b), 1)
                act.activation(plast[:, b, 0:S], bank[6 + b][0:NH, 0:S], ACT.Exp, bias=lstat[:, b, 1:2],
                               scale=HD ** -0.5, accum_out=lstat[:, b, 2:3]).then_inc(sem("last_exp", b), 1)

            def head_exp(g):
                b, n = divmod(g, NH)
                act.wait_ge(sem("hs_nm"), g + 1)
                if g >= 2:
                    act.wait_ge(sem("hp_mm"), g - 1)
                for t, (a, z) in enumerate(((0, P), (P, 3 * P))):
                    act.activation(ph[:, g % 2, a:z], scm[:, g % 2, a:z], ACT.Exp, bias=hnm[:, g % 2, t:t + 1],
                                   scale=HD ** -0.5, accum_out=hsum[:, b, t, n:n + 1]).then_inc(sem("hs_exp"), 1)

            def head_evac(g):
                act.wait_ge(sem("hp_mm"), g + 1)
                if g >= 2:
                    act.wait_ge(sem("av_mm"), g - 1)
                act.activation(phT[:, g % 2, :], bank[2 + g % 2][:, 0:3 * P], ACT.Copy).then_inc(sem("hp_sb"), 1)

            for g in range(NB * NH + 1):
                if g < NB * NH:
                    head_exp(g)
                if g >= 1:
                    head_evac(g - 1)

            norms(4)
            for b in BS:
                act.wait_ge(sem("ln_y", b), 4)
                act.activation(xhi[:, 0, b, :, :], y[:, b, :, :], ACT.Copy).then_inc(sem("xhi_done"), 1)
            for b in BS:
                act.wait_ge(sem("rt_shift", b), 2)
                act.activation(rstat[:, b, :, 3:4], rstat[:, b, :, 2:3], ACT.Exp).then_inc(sem("rt_exp", b), 1)
            copy_weights(1)
            K0 = STEPS * E
            for k in range(2 * CH1):
                c, b = divmod(k, 2)
                act.wait_ge(sem("up_done"), K0 + k + 1)
                act.wait_ge(sem("hmul_done"), K0 + k - 1 + OFF)
                act.activation(sg[:, b, :], bk(b, 0)[:, 0:N], ACT.Silu).then_inc(sem("silu_done"), 1)
                act.wait_ge(sem("hmul_done"), K0 + k + 1 + OFF)
                act.wait_ge(sem("down_done"), K0 + k - 3 + OFF)
                act.activation(hhi[:, k % 4, :], hid[:, b, :], ACT.Copy).then_inc(sem("hhi_done"), 1)
            for t, (_s0, rows) in enumerate(POS):
                for b in BS:
                    act.wait_ge(sem("ot_mm", b), t + 1)
                    act.activation(v[0:rows, b, t, :], bk(b, t % 2)[0:rows, 0:D], ACT.Copy)\
                        .then_inc(sem("y_out_ready", b), 1)

        @block.vector
        def _(dve):
            cnt = [0]

            def link(ins):
                cnt[0] += 1
                ins.then_inc(sem("dve_chain"), 1)
                dve.wait_ge(sem("dve_chain"), cnt[0])

            link(dve.memset(f32(zero[:, :]), 0.0))
            dve.nop().then_inc(sem("zero_ready"), 1)
            dve.wait_ge(sem("const"), CONST)
            dve.wait_ge(sem("small_in"), 16 * (KT * NB + 3))

            def norm_dev(n, b, src, cols):
                a, z = cols
                dve.wait_ge(sem("ln_mean", b), n + 1)
                mean = bk(b, 2)[:, a:z].unsqueeze(1).to_broadcast([P, KT, z - a])
                dve.tensor_tensor(dev[:, b, :, a:z], src[:, b, :, a:z], mean, ALU.subtract)\
                    .then_inc(sem("ln_dev", b), 1)

            def norm_out(n, b, cols):
                a, z = cols
                dve.wait_ge(sem("ln_sd", b), n + 1)
                link(dve.reciprocal(rstd[:, b, a:z], sd[:, b, a:z]))
                if n == 0:
                    for k in range(KT):
                        dve.scalar_tensor_tensor(out=h[:, b, k, a:z], in0=dev[:, b, k, a:z],
                                                 scalar=gamma_t[:, k:k + 1], in1=rstd[:, b, a:z],
                                                 op0=ALU.mult, op1=ALU.mult).then_inc(sem("h_done", b), 1)
                else:
                    r = rstd[:, b, a:z].unsqueeze(1).to_broadcast([P, KT, z - a])
                    dve.tensor_tensor(y[:, b, :, a:z], dev[:, b, :, a:z], r, ALU.mult).then_inc(sem("ln_y", b), 1)

            def norms(n):
                for b in BS:
                    norm_dev(n, b, h, (0, N))
                for b in BS:
                    norm_out(n, b, (0, N))

            for b in BS:
                norm_dev(0, b, y, (1, S))
            for b in BS:
                norm_out(0, b, (1, S))
            for b in BS:
                dve.wait_ge(sem("h_done", b), KT)
            norms(1)
            for t, (_s0, rows) in enumerate(POS):
                for b in BS:
                    dve.wait_ge(sem("v_mm", b), t + 1)
                    dve.tensor_copy(v[0:rows, b, t, :], bk(b, t)[0:rows, 0:D]).then_inc(sem("v_sb", b), 1)
            for t, (_s0, rows) in enumerate(POS):
                for b in BS:
                    dve.wait_ge(sem("sc_mm", b), t + 1)
                    link(dve.tensor_reduce(stat[0:rows, b, 8 + t:9 + t], bk(b, (3 + t) % 4)[0:rows, 0:S], AX,
                                           ALU.max))
                    dve.tensor_scalar(stat[0:rows, b, t:t + 1], stat[0:rows, b, 8 + t:9 + t], -D ** -0.5, None,
                                      ALU.mult).then_inc(sem("sc_nm", b), 1)
            for t, (_s0, rows) in enumerate(POS):
                for b in BS:
                    dve.wait_ge(sem("sc_exp", b), t + 1)
                    link(dve.reciprocal(stat[0:rows, b, 12 + t:13 + t], stat[0:rows, b, 4 + t:5 + t]))
                    dve.tensor_scalar(prob[0:rows, b, t, 0:S], prob[0:rows, b, t, 0:S],
                                      stat[0:rows, b, 12 + t:13 + t], None, ALU.mult).then_inc(sem("prob_ok", b), 1)
            for m in range(KT):
                for b in BS:
                    dve.wait_ge(sem("op_mm", b), m + 1)
                    dve.scalar_tensor_tensor(out=h[:, b, m, 0:S], in0=bk(b, (3 + m) % 4)[:, 0:S],
                                             scalar=bo0[:, m:m + 1], in1=h[:, b, m, 0:S],
                                             op0=ALU.add, op1=ALU.add).then_inc(sem("h_done", b), 1)
            for b in BS:
                dve.wait_ge(sem("h_done", b), 2 * KT)
            norms(2)

            def top(src, pick, top_at, b, guard):
                def wide(ap):
                    return ap.to_broadcast([RT, NR, E])
                m, r = rstat[:, b, :, top_at:top_at + 1], rstat[:, b, :, 4:5]
                link(dve.tensor_reduce(m, src, AX, ALU.max))
                link(dve.tensor_tensor(eq[:, b], src, wide(m), ALU.is_equal))
                link(dve.tensor_tensor(eq[:, b], eq[:, b], rank8[0:RT, :, :], ALU.mult))
                link(dve.tensor_reduce(r, eq[:, b], AX, ALU.max))
                link(dve.tensor_tensor(pick, eq[:, b], wide(r), ALU.is_equal))

            def top2(src, b):
                top(src, pick1[:, b], 0, b, 0)
                link(dve.scalar_tensor_tensor(out=rest[:, b].rearrange("p r e -> p (r e)"),
                                              in0=pick1[:, b].rearrange("p r e -> p (r e)"), scalar=-HUGE,
                                              in1=src.rearrange("p r e -> p (r e)"), op0=ALU.mult, op1=ALU.add))
                top(rest[:, b], pick2[:, b], 1, b, 0)

            def wide(ap):
                return ap.to_broadcast([RT, NR, E])

            def router0(b):
                dve.wait_ge(sem("rt_mm", b), 1)
                lps = bk(b, 0)[0:RT, 0:NR * E].rearrange("p (r e) -> p r e", e=E)
                link(dve.tensor_reduce(rstat[:, b, :, 0:1], lps, AX, ALU.max))
                dve.tensor_tensor(logit[:, b], lps, wide(rstat[:, b, :, 0:1]), ALU.subtract)\
                    .then_inc(sem("rt_shift", b), 1)

            def router0b(b):
                dve.wait_ge(sem("rt_exp", b), 1)
                link(dve.tensor_reduce(rstat[:, b, :, 5:6], route[:, b], AX, ALU.add))
                link(dve.reciprocal(rstat[:, b, :, 6:7], rstat[:, b, :, 5:6]))
                link(dve.tensor_tensor(logit[:, b], route[:, b], wide(rstat[:, b, :, 6:7]), ALU.mult))
                top2(logit[:, b], b)
                link(dve.tensor_tensor(eq[:, b], pick1[:, b], pick2[:, b], ALU.add))
                dve.tensor_tensor(route[:, b], eq[:, b], logit[:, b], ALU.mult).then_inc(sem("rt_done", b), 1)

            for b in BS:
                router0(b)
            for b in BS:
                router0b(b)

            def scaled_x(e, count):
                for b in BS:
                    dve.tensor_tensor(sq[:, b, :, :], y[:, b, :, :],
                                      big[:, bass.ds(e, 1), b, :].to_broadcast([P, KT, N]) if not isinstance(e, int)
                                      else big[:, e:e + 1, b, :].to_broadcast([P, KT, N]), ALU.mult)\
                        .then_inc(sem("xs_done"), 1)

            def x_low(par, count):
                for b in BS:
                    dve.wait_ge(sem("xhi_done"), count + b + 1)
                    dve.tensor_tensor(xlo[:, par, b, :, :], sq[:, b, :, :], f32(xhi[:, par, b, :, :]), ALU.subtract)\
                        .then_inc(sem("xlo_done"), 1)

            for b in BS:
                dve.wait_ge(sem("rb_sb", b), E)
            scaled_x(0, 0)
            x_low(0, 0)
            for name in ("hmul_done", "hlo_done"):
                dve.nop().then_inc(sem(name), OFF)

            def hidden_low(k, s, b, rows):
                dve.wait_ge(sem("hhi_done"), k + 1 + OFF)
                dve.tensor_tensor(hlo[0:rows, s % 4, :], hid[0:rows, b, :], f32(hhi[0:rows, s % 4, :]),
                                  ALU.subtract).then_inc(sem("hlo_done"), 1)

            def dve_expert(i, par, prep):
                e = 2 * i + par
                for s in range(STEPS):
                    c, b = divmod(s, 2)
                    rows = P if c < HC - 1 else HTAIL
                    k = STEPS * e + s
                    dve.wait_ge(sem("silu_done"), k + 1 + OFF)
                    dve.wait_ge(sem("hlo_done"), k - 1 + OFF)
                    dve.tensor_tensor(hid[0:rows, b, :], sg[0:rows, b, :], bk(b, 1)[0:rows, 0:N], ALU.mult)\
                        .then_inc(sem("hmul_done"), 1)
                    if prep and s == 2:
                        dve.wait_ge(sem("xlo_done"), 2 * (e + 1))
                        scaled_x(e + 1, 0)
                    if prep and s == 6:
                        x_low(1 - par, 2 * (e + 1))
                    hidden_low(k, s, b, rows)

            with dve.Fori(0, E // 2 - 1) as i:
                for par in range(2):
                    dve_expert(i, par, True)
            dve_expert(E // 2 - 1, 0, True)
            dve_expert(E // 2 - 1, 1, False)
            for b in BS:
                for m in range(KT):
                    dve.wait_ge(sem("down_done"), STEPS * E + OFF)
                    dve.tensor_tensor(h[:, b, m, :], h[:, b, m, :], bk(b, 2 + m)[:, 0:N], ALU.add)\
                        .then_inc(sem("h_done", b), 1)
            for b in BS:
                dve.wait_ge(sem("h_done", b), 3 * KT)
            norms(3)
            for k in range(KT):
                dve.wait_ge(sem("wsum_mm"), 1)
                dve.tensor_copy(wsum[:, k:k + 1], bank[1][:, 256 + 2 * k:257 + 2 * k]).then_inc(sem("wsum_sb"), 1)
            for t, (_s0, rows) in enumerate(POS):
                for b in BS:
                    dve.wait_ge(sem("v1_mm", b), t + 1)
                    dve.tensor_copy(v[0:rows, b, t, :], bk(b, t)[0:rows, 0:D]).then_inc(sem("v1_sb", b), 1)
            for b in BS:
                dve.wait_ge(sem("qk1_sb", b), HT)
                dve.tensor_tensor(qlast[:, b], slotmask[:, :, :],
                                  qk[:, b, 0:HT, S - 1:S].to_broadcast([P, HT, NH]), ALU.mult)\
                    .then_inc(sem("qlast_done", b), 1)
            for b in BS:
                dve.wait_ge(sem("last_mm", b), 1)
                link(dve.tensor_reduce(lstat[:, b, 0:1], bank[6 + b][0:NH, 0:S], AX, ALU.max))
                dve.tensor_scalar(lstat[:, b, 1:2], lstat[:, b, 0:1], -HD ** -0.5, None, ALU.mult)\
                    .then_inc(sem("last_nm", b), 1)
            for b in BS:
                dve.wait_ge(sem("last_mm", b), 2)
                for j, (_s0, rows) in enumerate(POS):
                    dve.tensor_copy(plT[0:rows, b, j, :], bank[6 + b][0:rows, 16 * j:16 * j + NH])\
                        .then_inc(sem("plT_sb", b), 1)
            for b in BS:
                dve.wait_ge(sem("last_mm", b), 3)
                link(dve.tensor_tensor(olm[:, b], bank[6 + b][0:NH, 0:D].rearrange("p (n c) -> p n c", c=HD),
                                       ident[0:NH, 0:NH].unsqueeze(2).to_broadcast([NH, NH, HD]), ALU.mult))
                link(dve.tensor_reduce(ol[:, b, :], olm[:, b].rearrange("p n c -> p c n"), AX, ALU.add))
                link(dve.reciprocal(lstat[:, b, 3:4], lstat[:, b, 2:3]))
                dve.tensor_scalar(ols[:, b, :], ol[:, b, :], lstat[:, b, 3:4], None, ALU.mult)\
                    .then_inc(sem("osb_done", b), 1)
            def head_max(g):
                dve.wait_ge(sem("hs_mm"), g + 1)
                if g >= 2:
                    dve.wait_ge(sem("hs_exp"), 2 * (g - 1))
                for t, (a, z) in enumerate(((0, P), (P, 3 * P))):
                    dve.tensor_tensor_reduce(scm[:, g % 2, a:z], bank[g % 2][:, a:z], causal[:, a:z], 1.0, -HUGE,
                                             ALU.add, ALU.max, hmx[:, g % 2, t:t + 1]).then_inc(sem("hs_max"), 1)
                dve.wait_ge(sem("hs_max"), 2 * (g + 1))
                dve.tensor_scalar(hnm[:, g % 2, :], hmx[:, g % 2, :], -HD ** -0.5, None, ALU.mult)\
                    .then_inc(sem("hs_nm"), 1)

            def heads_out(b):
                dve.wait_ge(sem("hs_exp"), 2 * NH * (b + 1))
                link(dve.reciprocal(hinv[:, b], hsum[:, b]))
                dve.wait_ge(sem("av_mm"), NH * (b + 1))
                dve.tensor_tensor(osb[:, b].rearrange("p t n c -> p (t n) c"),
                                  bank[4 + b][:, :].rearrange("p (n c) -> p n c", c=HD),
                                  hinv[:, b].rearrange("p t n -> p (t n)").unsqueeze(2)
                                  .to_broadcast([P, 2 * NH, HD]), ALU.mult).then_inc(sem("osb_done", b), 1)

            for g in range(NB * NH + 2):
                if g < NB * NH:
                    head_max(g)
                if g >= 2 and (g - 2) % NH == NH - 1:
                    heads_out((g - 2) // NH)
            dve.wait_ge(sem("wsum_sb"), KT)
            for b in BS:
                dve.wait_ge(sem("heads_in", b), 16)
                for k in range(KT):
                    dve.scalar_tensor_tensor(out=h[:, b, k, 0:S], in0=cT[:, b, k, 0:S], scalar=wsum[:, k:k + 1],
                                             in1=h[:, b, k, 0:S], op0=ALU.mult, op1=ALU.add)\
                        .then_inc(sem("h_done", b), 1)
            for b in BS:
                dve.wait_ge(sem("h_done", b), 4 * KT)
            norms(4)
            for b in BS:
                dve.wait_ge(sem("xhi_done"), 2 * E + b + 1)
                dve.tensor_tensor(xlo[:, 0, b, :, :], y[:, b, :, :], f32(xhi[:, 0, b, :, :]), ALU.subtract)\
                    .then_inc(sem("xlo_done"), 1)
            dve.wait_ge(sem("l1_in"), 64)
            for b in BS:
                dve.wait_ge(sem("rt_mm", b), 2)
                lps = bk(b, 0)[0:RT, 0:NR * E].rearrange("p (r e) -> p r e", e=E)
                link(dve.tensor_tensor(logit[:, b], lps, ebias_t[:, :].unsqueeze(1).to_broadcast([RT, NR, E]),
                                       ALU.add))
                top2(logit[:, b], b)
                dve.tensor_tensor(rstat[:, b, :, 2:3], rstat[:, b, :, 1:2], rstat[:, b, :, 0:1], ALU.subtract)\
                    .then_inc(sem("rt_shift", b), 1)
            for b in BS:
                dve.wait_ge(sem("rt_exp", b), 2)
                link(dve.tensor_scalar(rstat[:, b, :, 5:6], rstat[:, b, :, 3:4], 1.0, None, ALU.add))
                link(dve.reciprocal(rstat[:, b, :, 6:7], rstat[:, b, :, 5:6]))
                link(dve.tensor_tensor(eq[:, b], pick2[:, b], wide(rstat[:, b, :, 3:4]), ALU.mult))
                link(dve.tensor_tensor(rest[:, b], eq[:, b], pick1[:, b], ALU.add))
                dve.tensor_tensor(route[:, b], rest[:, b], wide(rstat[:, b, :, 6:7]), ALU.mult)\
                    .then_inc(sem("rt_done", b), 1)
            for b in BS:
                dve.wait_ge(sem("rb_sb", b), 2 * E)
            K0 = STEPS * E
            for k in range(2 * CH1):
                c, b = divmod(k, 2)
                dve.wait_ge(sem("silu_done"), K0 + k + 1 + OFF)
                dve.wait_ge(sem("hlo_done"), K0 + k - 1 + OFF)
                if c < NSH:
                    dve.tensor_tensor(hid[:, b, :], sg[:, b, :], bk(b, 1)[:, 0:N], ALU.mult)\
                        .then_inc(sem("hmul_done"), 1)
                else:
                    link(dve.tensor_tensor(hidw[:, :], sg[:, b, :], bk(b, 1)[:, 0:N], ALU.mult))
                    dve.tensor_tensor(hid[:, b, :], hidw[:, :], big[:, c - NSH, b, :], ALU.mult)\
                        .then_inc(sem("hmul_done"), 1)
                hidden_low(K0 + k, k, b, P)
            for b in BS:
                for m in range(KT):
                    dve.wait_ge(sem("down_done"), STEPS * E + 2 * CH1 + OFF)
                    dve.tensor_tensor(h[:, b, m, :], h[:, b, m, :], bk(b, 2 + m)[:, 0:N], ALU.add)\
                        .then_inc(sem("h_done", b), 1)

        @block.tensor
        def _(pe):
            pe.wait_ge(sem("const"), CONST)

            def mm(o, w, m, start, stop, **kw):
                return pe.matmul(o, w, m, start=start, stop=stop, **kw)

            def norm_mean(n, b, src, cols):
                a, z = cols
                for k in range(KT):
                    last = mm(bk(b, 2)[:, a:z], avg[:, :], src[:, b, k, a:z], k == 0, k == KT - 1)
                last.then_inc(sem("ln_mean", b), 1)

            def norm_var(n, b, cols):
                a, z = cols
                pe.wait_ge(sem("ln_sq", b), n + 1)
                for k in range(KT):
                    last = mm(bk(b, 3)[:, a:z], avg[:, :], sq[:, b, k, a:z], k == 0, k == KT - 1)
                last.then_inc(sem("ln_var", b), 1)

            pe.wait_ge(sem("wtok_in"), 16 * JG)
            for b in BS:
                pe.wait_ge(sem("patches_in", b), 16 * JG * C)
                for m in range(KT):
                    for g in range(NJ):
                        rows = min(JG, PS - JG * g) * CI
                        last = mm(bk(b, m)[:, 0:NTOK], wtok[0:rows, g, m * P:(m + 1) * P],
                                  patches[0:rows, b, :, JG * g:W:PS], g == 0, g == NJ - 1)
                    last.then_inc(sem("tok_mm", b), 1)
            for b in BS:
                pe.wait_ge(sem("tok_sb", b), KT)
                norm_mean(0, b, y, (1, S))
            for b in BS:
                norm_var(0, b, (1, S))

            def norms(n):
                for b in BS:
                    pe.wait_ge(sem("h_done", b), n * KT)
                    norm_mean(n, b, h, (0, N))
                for b in BS:
                    norm_var(n, b, (0, N))

            pe.wait_ge(sem("small_in"), 16 * (KT * NB + 3))
            norms(1)
            pe.wait_ge(sem("wqkv0_in"), 16)
            for b in BS:
                pe.wait_ge(sem("ln_y", b), 1)
                for m in range(2 * KT):
                    for k in range(KT):
                        last = mm(bk(b, m)[:, 0:N], wqkv0[:, k, m * P:(m + 1) * P], y[:, b, k, :], k == 0, k == KT - 1)
                    last.then_inc(sem("qk_mm", b), 1)
            for t, (s0, rows) in enumerate(POS):
                for b in BS:
                    pe.wait_ge(sem("qk_sb", b), t + 1)
                    for k in range(KT):
                        last = mm(bk(b, t)[0:rows, 0:D], y[:, b, k, s0:s0 + rows], wqkv0[:, k, 2 * D:3 * D],
                                  k == 0, k == KT - 1)
                    last.then_inc(sem("v_mm", b), 1)
            for t, (s0, rows) in enumerate(POS):
                for b in BS:
                    pe.wait_ge(sem("qk_sb", b), 2 * KT)
                    if t:
                        pe.wait_ge(sem("v_sb", b), t)
                    for k in range(KT):
                        last = mm(bk(b, (3 + t) % 4)[0:rows, 0:S], qk[:, b, k, s0:s0 + rows],
                                  qk[:, b, KT + k, 0:S], k == 0, k == KT - 1)
                    last.then_inc(sem("sc_mm", b), 1)
            for j, (k0, kn) in enumerate(POS):
                for b in BS:
                    pe.wait_ge(sem("v_sb", b), 3)
                    pe.wait_ge(sem("prob_ok", b), 3)
                    for t, (s0, rows) in enumerate(POS):
                        last = pe.transpose(bk(b, (2 + j) % 4)[0:kn, s0:s0 + rows], prob[0:rows, b, t, k0:k0 + kn],
                                            ident[0:rows, 0:rows])
                    last.then_inc(sem("pt_mm", b), 1)
            for m in range(KT):
                for b in BS:
                    pe.wait_ge(sem("pt_sb", b), 3)
                    for j, (k0, kn) in enumerate(POS):
                        last = mm(bk(b, 1 + m)[:, 0:S], v[0:kn, b, j, m * P:(m + 1) * P], probT[0:kn, b, j, 0:S],
                                  j == 0, j == 2)
                    last.then_inc(sem("cx_mm", b), 1)
            pe.wait_ge(sem("wo0_in"), 16)
            for m in range(KT):
                for b in BS:
                    pe.wait_ge(sem("cx_sb", b), KT)
                    for k in range(KT):
                        last = mm(bk(b, (3 + m) % 4)[:, 0:S], wo0[:, k, m * P:(m + 1) * P], cT[:, b, k, 0:S],
                                  k == 0, k == KT - 1)
                    last.then_inc(sem("op_mm", b), 1)
            norms(2)

            def logits(layer, w):
                for b in BS:
                    pe.wait_ge(sem("ln_y", b), 2 if layer == 0 else 4)
                    for r in range(NR):
                        for k in range(KT):
                            last = mm(bk(b, 0)[0:RT, r * E:(r + 1) * E], y[:, b, k, r * RT:(r + 1) * RT], w[:, k, :],
                                      k == 0, k == KT - 1)
                    last.then_inc(sem("rt_mm", b), 1)

            def spread_weights(layer):
                for b in BS:
                    pe.wait_ge(sem("rt_done", b), layer + 1)
                for e in range(E):
                    for b in BS:
                        if e >= 4:
                            pe.wait_ge(sem("rb_sb", b), layer * E + e - 3)
                        for r in range(NR):
                            last = mm(bk(b, e % 4)[:, r * RT:(r + 1) * RT],
                                      route[:, b, r, e:e + 1].to_broadcast([RT, P]), ident[0:RT, 0:RT], True, True)
                        last.then_inc(sem("rb_mm", b), 1)

            pe.wait_ge(sem("gw_in"), 16 * KT)
            logits(0, gw)
            spread_weights(0)

            def clear_sums(layer):
                for b in BS:
                    pe.wait_ge(sem("rb_sb", b), (layer + 1) * E)
                for b in BS:
                    for m in range(KT):
                        mm(bk(b, 2 + m)[:, 0:N], zero[:, 0:P], zero[:, :], True, False, skip_group_check=True)

            def split_mm(o, whi_, wlo_, mhi, mlo, start, stop):
                kw = dict(skip_group_check=True)
                mm(o, whi_, mhi, start, False, **kw)
                mm(o, whi_, mlo, False, False, **kw)
                return mm(o, wlo_, mhi, False, stop, **kw)

            def up(k, s, e_par, ready=None):
                c, b = divmod(s, 2)
                cols = P if c < HC - 1 else HTAIL
                pe.wait_ge(sem("hmul_done"), k - 1 + OFF)
                for n in range(2):
                    for kt in range(KT):
                        at = n * WA + kt * HID + c * P
                        last = split_mm(bk(b, n)[0:cols, 0:N], whi[:, e_par, at:at + cols], wlo[:, e_par, at:at + cols],
                                        xhi[:, e_par, b, kt, :], xlo[:, e_par, b, kt, :], kt == 0, kt == KT - 1)
                last.then_inc(sem("up_done"), 1)

            def down(k, s, e_par, final):
                c, b = divmod(s, 2)
                rows = P if c < HC - 1 else HTAIL
                pe.wait_ge(sem("hhi_done"), k + 1 + OFF)
                pe.wait_ge(sem("hlo_done"), k + 1 + OFF)
                for m in range(KT):
                    at = 2 * WA + c * D + m * P
                    last = split_mm(bk(b, 2 + m)[:, 0:N], whi[0:rows, e_par, at:at + P], wlo[0:rows, e_par, at:at + P],
                                    hhi[0:rows, s % 4, :], hlo[0:rows, s % 4, :], False, final)
                last.then_inc(sem("down_done"), 1)

            def expert_ready(e):
                pe.wait_ge(sem("wlo_done"), STEPS * (e + 1))
                pe.wait_ge(sem("whi_done"), STEPS * (e + 1))
                pe.wait_ge(sem("xlo_done"), 2 * (e + 1))

            pe.wait_ge(sem("zero_ready"), 1)
            clear_sums(0)
            pe.nop().then_inc(sem("down_done"), OFF)
            expert_ready(0)
            up(0, 0, 0)
            up(1, 1, 0)

            def pe_expert(i, par, more):
                e = 2 * i + par
                for s in range(STEPS):
                    k = STEPS * e + s
                    if s + 2 < STEPS:
                        up(k + 2, s + 2, par)
                    elif more:
                        if s + 2 == STEPS:
                            expert_ready(e + 1)
                        up(k + 2, s + 2 - STEPS, 1 - par)
                    down(k, s, par, (not more) and s >= STEPS - 2)

            with pe.Fori(0, E // 2 - 1) as i:
                for par in range(2):
                    pe_expert(i, par, True)
            pe_expert(E // 2 - 1, 0, True)
            pe_expert(E // 2 - 1, 1, False)

            norms(3)
            pe.wait_ge(sem("wqk1_ready"), 2)
            for m in range(2 * HT):
                w = (wq1 if m < HT else wk1)[:, :, (m % HT) * HPT:(m % HT + 1) * HPT, :]\
                    .rearrange("p k n c -> p k (n c)")
                for b in BS:
                    if m == 0:
                        pe.wait_ge(sem("ln_y", b), 3)
                    if m >= 4:
                        pe.wait_ge(sem("qk1_sb", b), m - 3)
                    for k in range(KT):
                        last = mm(bk(b, m % 4)[:, 0:N], w[:, k, :], y[:, b, k, :], k == 0, k == KT - 1)
                    last.then_inc(sem("qk1_mm", b), 1)
            pe.wait_ge(sem("l1_in"), 64)
            for t, (s0, rows) in enumerate(POS):
                for b in BS:
                    pe.wait_ge(sem("qk1_sb", b), 4 + t + 1)
                    if t == 1 and b == 0:
                        for m in range(KT):
                            for k in range(KT):
                                last = mm(bank[1][:, 256 + 2 * m:257 + 2 * m], wo1[:, k, m * P:(m + 1) * P],
                                          ones[:, 0:1], k == 0, k == KT - 1)
                        last.then_inc(sem("wsum_mm"), 1)
                        pe.wait_ge(sem("wsum_sb"), KT)
                    for k in range(KT):
                        last = mm(bk(b, t)[0:rows, 0:D], y[:, b, k, s0:s0 + rows],
                                  wqkv1[:, k, :, 2 * HD:3 * HD], k == 0, k == KT - 1)
                    last.then_inc(sem("v1_mm", b), 1)
            for b in BS:
                pe.wait_ge(sem("qk1_sb", b), 2 * HT)
                pe.wait_ge(sem("v1_sb", b), 3)
            for b in BS:
                pe.wait_ge(sem("qlast_done", b), 1)
                for t in range(HT):
                    last = mm(bank[6 + b][0:NH, 0:S], qlast[:, b, t, :], qk[:, b, HT + t, 0:S], t == 0, t == HT - 1)
                last.then_inc(sem("last_mm", b), 1)
            for b in BS:
                pe.wait_ge(sem("last_exp", b), 1)
                for j, (k0, kn) in enumerate(POS):
                    last = pe.transpose(bank[6 + b][0:kn, 16 * j:16 * j + NH], plast[:, b, k0:k0 + kn],
                                        ident[0:NH, 0:NH])
                last.then_inc(sem("last_mm", b), 1)
            for b in BS:
                pe.wait_ge(sem("plT_sb", b), 3)
                for j, (k0, kn) in enumerate(POS):
                    last = mm(bank[6 + b][0:NH, 0:D], plT[0:kn, b, j, :], v[0:kn, b, j, :], j == 0, j == 2)
                last.then_inc(sem("last_mm", b), 1)

            def head_scores(g):
                b, n = divmod(g, NH)
                t, p0 = n // HPT, (n % HPT) * SLOT
                if g >= 2:
                    pe.wait_ge(sem("hs_max"), 2 * (g - 1))
                q, kk = qk[p0:p0 + HD, b, t, :], qk[p0:p0 + HD, b, HT + t, :]
                mm(bank[g % 2][:, 0:P], q[:, 0:P], kk[:, 0:P], True, True)
                mm(bank[g % 2][:, P:3 * P], q[:, P:2 * P], kk[:, 0:2 * P], True, True)\
                    .then_inc(sem("hs_mm"), 1)

            def head_turn(g):
                pe.wait_ge(sem("hs_exp"), 2 * (g + 1))
                if g >= 2:
                    pe.wait_ge(sem("hp_sb"), g - 1)
                for j in range(3):
                    last = pe.transpose(bank[2 + g % 2][:, j * P:(j + 1) * P], ph[:, g % 2, j * P:(j + 1) * P],
                                        ident[:, :])
                last.then_inc(sem("hp_mm"), 1)

            def head_out(g):
                b, n = divmod(g, NH)
                pe.wait_ge(sem("hp_sb"), g + 1)
                vn = v[:, b, :, n * HD:(n + 1) * HD]
                o = bank[4 + b]
                mm(o[:, n * HD:(n + 1) * HD], phT[:, g % 2, 0:P], vn[:, 0, :], True, True)
                mm(o[:, D + n * HD:D + (n + 1) * HD], phT[:, g % 2, P:2 * P], vn[:, 0, :], True, False)
                mm(o[:, D + n * HD:D + (n + 1) * HD], phT[:, g % 2, 2 * P:3 * P], vn[:, 1, :], False, True)\
                    .then_inc(sem("av_mm"), 1)

            for g in range(NB * NH + 2):
                if g < NB * NH:
                    head_scores(g)
                if 1 <= g <= NB * NH:
                    head_turn(g - 1)
                if g >= 2:
                    head_out(g - 2)

            norms(4)
            logits(1, wr1)
            spread_weights(1)
            clear_sums(1)
            pe.wait_ge(sem("w1split_done"), CH1)
            pe.wait_ge(sem("xlo_done"), 2 * E + 2)
            K0 = STEPS * E

            def up1(k):
                c, b = divmod(k, 2)
                pe.wait_ge(sem("hmul_done"), K0 + k - 1 + OFF)
                for n in range(2):
                    for kt in range(KT):
                        at = c * W1 + n * GU + kt * F1
                        last = split_mm(bk(b, n)[:, 0:N], whi1[:, at:at + F1], wlo1[:, at:at + F1],
                                        xhi[:, 0, b, kt, :], xlo[:, 0, b, kt, :], kt == 0, kt == KT - 1)
                last.then_inc(sem("up_done"), 1)

            def down1(k):
                c, b = divmod(k, 2)
                pe.wait_ge(sem("hhi_done"), K0 + k + 1 + OFF)
                pe.wait_ge(sem("hlo_done"), K0 + k + 1 + OFF)
                for m in range(KT):
                    at = c * W1 + 2 * GU + m * P
                    last = split_mm(bk(b, 2 + m)[:, 0:N], whi1[:, at:at + P], wlo1[:, at:at + P],
                                    hhi[:, k % 4, :], hlo[:, k % 4, :], False, c == CH1 - 1)
                last.then_inc(sem("down_done"), 1)

            for k in range(2 * CH1 + 2):
                if k < 2 * CH1:
                    up1(k)
                if k >= 2:
                    down1(k - 2)
            for t, (s0, rows) in enumerate(POS):
                for b in BS:
                    pe.wait_ge(sem("h_done", b), 5 * KT)
                    if t == 2:
                        pe.wait_ge(sem("y_out_ready", b), 1)
                    for k in range(KT):
                        last = pe.transpose(bk(b, t % 2)[0:rows, k * P:(k + 1) * P], h[:, b, k, s0:s0 + rows],
                                            ident[:, :])
                    last.then_inc(sem("ot_mm", b), 1)


_INS = ['x', 'cls_tok', 'L0_tok_W', 'L0_tok_gamma', 'L0_attn_W_qkv', 'L0_attn_b_qkv', 'L0_attn_W_out',
        'L0_attn_b_out', 'L0_ffn_gate_w', 'L0_ffn_w1', 'L0_ffn_w2', 'L0_ffn_w3', 'L1_attn_W_qkv', 'L1_attn_W_out',
        'L1_ffn_Wr', 'L1_ffn_Wg', 'L1_ffn_Wu', 'L1_ffn_Wd', 'L1_ffn_Sg', 'L1_ffn_Su', 'L1_ffn_Sd',
        'L1_ffn_expert_bias']
_OUTS = [((2, 257, 256), 'float32')]


def kernel(**inputs):
    import numpy as _np
    import concourse.bacc as _bacc
    from concourse import mybir as _mybir
    from concourse.bass_utils import run_bass_kernel_spmd as _run

    nc = _bacc.Bacc("TRN2", target_bir_lowering=False, num_devices=1)
    arrays, args = {}, []
    for name in _INS:
        a = _np.ascontiguousarray(inputs[name])
        arrays[f"in_{name}_dram"] = a
        args.append(nc.dram_tensor(f"in_{name}_dram", a.shape, _mybir.dt.from_np(a.dtype), kind="ExternalInput").ap())
    for i, (shape, dtype) in enumerate(_OUTS):
        dt = _mybir.dt.from_np(_np.dtype(dtype))
        args.append(nc.dram_tensor(f"out_{i}_dram", shape, dt, kind="ExternalOutput").ap())
    vit_tower(nc, *args)
    r = _run(nc, [arrays], core_ids=[0])
    got = tuple(r.results[0][f"out_{i}_dram"] for i in range(len(_OUTS)))
    return got[0]
```

```python
from contextlib import ExitStack

import concourse.bass as bass
from concourse import mybir

F32 = mybir.dt.float32
F32R = mybir.dt.float32r
ALU = mybir.AluOpType
ACT = mybir.ActivationFunctionType
AX = mybir.AxisListType.X

P = 128
EPS = 1e-5
HUGE = 1e38


def vit_tower(nc, x, cls_tok, tok_W, tok_gamma, a0_Wqkv, a0_bqkv, a0_Wo, a0_bo, gate_w, w1, w2, w3,
              a1_Wqkv, a1_Wo, Wr, Wg, Wu, Wd, Sg, Su, Sd, ebias, out):
    NB, C, H, W = x.shape
    D = tok_W.shape[1]
    KT = D // P
    PS = 8
    HY, WX = H // PS, W // PS
    NTOK = HY * WX
    S = NTOK + 1
    N = S + 1
    CI = C * PS
    JG = 3
    NJ = (PS + JG - 1) // JG
    E, HID = w1.shape[0], w1.shape[2]
    HC = (HID + P - 1) // P
    HTAIL = HID - (HC - 1) * P
    NH, HD = a1_Wqkv.shape[0], a1_Wqkv.shape[2] // 3
    PAIR = 2 * HD
    HPT = P // HD
    NQ = 3 * KT
    F1 = Wg.shape[2]
    RT = 86
    NR = N // RT
    POS = [(0, P), (P, P), (2 * P, 1)]
    assert NR * RT == N and S == 2 * P + 1 and D == 256 and F1 == P

    WA = KT * HID
    WTOT = 2 * WA + HC * D
    STEPS = 2 * HC
    PIECES = [(i * WA // 4, WA // 4) for i in range(8)]
    PIECES += [(2 * WA + i * HC * D // 4, HC * D // 4) for i in range(4)]
    assert len(PIECES) == STEPS and E % 2 == 0
    PREP = [(0, 0)] * 2 + [(2 * s, 2 * s + 2) for s in range(6)] + [(12, 12)] * (STEPS - 8)
    CH1 = Sg.shape[1] // F1 + E
    NSH = CH1 - E
    LAG = 4
    OFF = 4

    ctx = ExitStack()
    with ctx:
        sems = {}

        def sem(name, b=None):
            key = name if b is None else f"{name}_{b}"
            if key not in sems:
                sems[key] = ctx.enter_context(nc.semaphore(key))
            return sems[key]

        def sb(name, shape, dt=F32):
            return ctx.enter_context(nc.sbuf_tensor(name, shape, dt))

        h = sb("h", [P, NB, KT, N])
        y = sb("y", [P, NB, KT, N])
        dev = sb("dev", [P, NB, KT, N])
        sq = sb("sq", [P, NB, KT, N])
        tmp = sb("tmp", [1, 1])
        sd = sb("sd", [P, NB, N])
        rstd = sb("rstd", [P, NB, N])
        big = sb("big", [P, NB, N, E])
        ident = sb("ident", [P, P])
        avg = sb("avg", [P, P])
        ones = sb("ones", [P, 2])
        eps_t = sb("eps_t", [P, 1])
        rank8 = sb("rank8", [P, NB * NR, E])
        causal = sb("causal", [P, 3 * P])
        headmask = sb("headmask", [P, KT, NH])
        qscale = sb("qscale", [P, 2])
        wtok = sb("wtok", [JG * CI, NJ, D])
        gamma_t = sb("gamma_t", [P, KT])
        wqkv0 = sb("wqkv0", [P, KT, 3 * D])
        bqkv0 = sb("bqkv0", [P, 3 * KT])
        wo0 = sb("wo0", [P, KT, D])
        bo0 = sb("bo0", [P, KT])
        gw = sb("gw", [P, KT, E])
        wr1 = sb("wr1", [P, KT, E])
        ebias_t = sb("ebias_t", [RT, E])
        wqkv1 = wqkv0[:, :, :].rearrange("p k (q n) -> p k q n", q=3)
        wo1 = wo0
        wsum = sb("wsum", [P, KT])
        qk = big[:, :, :, :].rearrange("p b n e -> p (b n e)")[:, 0:NB * NQ * N]\
            .rearrange("p (b m n) -> p b m n", b=NB, m=NQ)
        v = sb("v", [P, NB, 3, D])
        prob = sb("prob", [P, NB, 3, N])
        probT = sb("probT", [P, NB, 3, N])
        cT = dev
        stat = sb("stat", [P, NB, 16])
        logit = sb("logit", [RT, NB, NR, E])
        eq = sb("eq", [RT, NB, NR, E])
        pick1 = sb("pick1", [RT, NB, NR, E])
        pick2 = sb("pick2", [RT, NB, NR, E])
        rest = sb("rest", [RT, NB, NR, E])
        route = sb("route", [RT, NB, NR, E])
        rstat = sb("rstat", [RT, NB, NR, 8])
        raw = sb("raw", [P, WTOT])
        whi = sb("whi", [P, 2, WTOT], F32R)
        wlo = sb("wlo", [P, 2, WTOT], F32R)
        xhi = sb("xhi", [P, 2, NB, KT, N], F32R)
        xlo = sb("xlo", [P, 2, NB, KT, N], F32R)
        sg = sb("sg", [P, NB, N])
        hid = sb("hid", [P, NB, N])
        hidw = sb("hidw", [P, N])
        hhi = sb("hhi", [P, 4, N], F32R)
        hlo = sb("hlo", [P, 4, N], F32R)
        zero = sb("zero", [P, N], F32R)
        scm = prob[:, :, :, :].rearrange("p b t n -> p (b t n)")[:, 0:12 * P]\
            .rearrange("p (a n) -> p a n", a=4)
        ph = probT[:, :, :, :].rearrange("p b t n -> p (b t n)")[:, 0:12 * P].rearrange("p (a n) -> p a n", a=4)
        phT = sb("phT", [P, 3, 3 * P])
        hnm = sb("hnm", [P, 4, 2])
        hsum = sb("hsum", [P, NB, 2, NH])
        hinv = sb("hinv", [P, NB, 2, NH])
        osb = sb("osb", [P, NB, 2, NH, HD])
        qlast = sb("qlast", [P, NB, KT, NH])
        plast = sb("plast", [NH, NB, N])
        plT = sb("plT", [P, NB, 3, NH])
        olm = hid[0:NH, :, 0:NH * HD].rearrange("p b (n c) -> p b n c", n=NH)
        ol = sb("ol", [NH, NB, HD])
        ols = sb("ols", [NH, NB, HD])
        lstat = sb("lstat", [NH, NB, 4])
        patches = big[:, :, :, :].rearrange("p b n e -> p (b n e)")[0:JG * CI, 0:NB * HY * W] \
            .rearrange("p (b y w) -> p b y w", b=NB, y=HY)
        whi1 = whi[:, :, :].rearrange("p a n -> p (a n)")
        wlo1 = wlo[:, :, :].rearrange("p a n -> p (a n)")
        GU = KT * F1
        W1 = 2 * GU + D
        HALF1 = CH1 // 2
        assert HALF1 * W1 <= WTOT and CH1 * W1 <= 2 * WTOT

        route_dram = nc.dram_tensor("route_dram", (2, NB, N, E), F32, kind="Internal").ap()
        heads_dram = nc.dram_tensor("heads_dram", (NB, NH, S, HD), F32, kind="Internal").ap()

        def merged(t):
            return t[:, :, :, :].rearrange("p b r e -> p (b r) e")

        bank = [ctx.enter_context(nc.psum_tensor(f"bank{i}", [P, 512], F32)) for i in range(8)]

        def bk(b, i):
            return bank[4 * b + i]

        ctx.enter_context(nc.allow_non_contiguous_dma(reason="small per-feature vectors and one column"))
        block = ctx.enter_context(nc.Block())
        BS = range(NB)

        def f32(ap):
            return ap.bitcast(F32)

        def head_evac(eng, g):
            eng.wait_ge(sem("hp_mm"), g + 1)
            if g >= 3:
                eng.wait_ge(sem("av_mm"), g - 2)
            if g % 2 == 0:
                nc.scalar.activation(phT[:, g % 3, :], turn_bank(g)[:, 0:3 * P], ACT.Copy)\
                    .then_inc(sem("hp_even"), 1)
            else:
                nc.vector.tensor_copy(phT[:, g % 3, :], turn_bank(g)[:, 0:3 * P]).then_inc(sem("hp_odd"), 1)

        def wait_evac(eng, g):
            eng.wait_ge(sem("hp_even" if g % 2 == 0 else "hp_odd"), g // 2 + 1)

        def turn_bank(g):
            return bank[3 if g % 2 == 0 else 6]

        @block.sync
        def _(sp):
            for b in BS:
                for jj in range(JG):
                    for c in range(C):
                        p0 = jj * CI + c * PS
                        eng = (sp, sp)[c % 2]
                        eng.dma_start(patches[p0:p0 + PS, b, :, 0:W - jj],
                                      x[b, c].rearrange("(y i) w -> i y w", i=PS)[:, :, jj:W])\
                            .then_inc(sem("patches_in", b), 16)
                if b == 0:
                    wt = tok_W.rearrange("(c j) d -> c j d", j=PS)
                    for jj in range(JG):
                        ng = len(range(jj, PS, JG))
                        sp.dma_start(wtok[jj * CI:(jj + 1) * CI, 0:ng, :], wt[:, jj:PS:JG, :])\
                            .then_inc(sem("wtok_in"), 16)
            for k in range(KT):
                for b in BS:
                    sp.dma_start(h[:, b, k, 0:1], cls_tok[0, 0:1, k * P:(k + 1) * P].rearrange("a p -> p a"))\
                        .then_inc(sem("small_in"), 16)
            sp.dma_start(gamma_t[:, :], tok_gamma.rearrange("(k p) -> p k", p=P)).then_inc(sem("small_in"), 16)
            sp.dma_start(bqkv0[:, :], a0_bqkv.rearrange("(k p) -> p k", p=P)).then_inc(sem("small_in"), 16)
            sp.dma_start(bo0[:, :], a0_bo.rearrange("(k p) -> p k", p=P)).then_inc(sem("small_in"), 16)
            sp.dma_start(wqkv0[:, :, :], a0_Wqkv.rearrange("(k p) n -> p k n", p=P)).then_inc(sem("wqkv0_in"), 16)
            sp.dma_start(wo0[:, :, :], a0_Wo.rearrange("(k p) n -> p k n", p=P)).then_inc(sem("wo0_in"), 16)
            for k in range(KT):
                sp.dma_start(gw[:, k, :], gate_w[:, k * P:(k + 1) * P].rearrange("e p -> p e"))\
                    .then_inc(sem("gw_in"), 16)

            def load_expert(e, before):
                def third(n):
                    if before is not None:
                        sp.wait_ge(sem("whi_done"), before + 4 * (n + 1))
                        sp.wait_ge(sem("wlo_done"), before + 4 * (n + 1))
                for n, w in enumerate((w1, w3)):
                    third(n)
                    sp.dma_start(raw[:, n * WA:(n + 1) * WA].rearrange("p (k n) -> p k n", k=KT),
                                 w[bass.ds(e, 1)].rearrange("a (k p) n -> p (a k) n", p=P))\
                        .then_inc(sem("expert_in", n), 16)
                third(2)
                rd = raw[:, 2 * WA:WTOT].rearrange("p (c n) -> p c n", c=HC)
                sp.dma_start(rd[:, 0:HC - 1, :],
                             w2[bass.ds(e, 1), 0:(HC - 1) * P, :].rearrange("a (c p) n -> p (a c) n", p=P))\
                    .then_inc(sem("expert_in", 2), 16)
                sp.dma_start(rd[0:HTAIL, HC - 1, :], w2[bass.ds(e, 1), (HC - 1) * P:HID, :]
                             .rearrange("a p n -> p (a n)")).then_inc(sem("expert_in", 2), 16)

            def spread_routing(layer):
                for b in BS:
                    sp.wait_ge(sem("rt_done"), layer + 1)
                    sp.dma_start(route_dram[layer, b].rearrange("(r p) e -> p r e", p=RT), route[:, b, :, :])\
                        .then_inc(sem("rt_out", b), 16)
                for b in BS:
                    sp.wait_ge(sem("rt_out", b), 16 * (layer + 1))
                    sp.dma_start(big[:, b, :, :].rearrange("p n e -> p (n e)"),
                                 route_dram[layer, b].rearrange("n e -> (n e)").rearrange("(a n) -> a n", a=1)
                                 .broadcast_to([P, N * E])).then_inc(sem("rt_in", b), 16)

            sp.wait_ge(sem("tail_zero"), 1)
            load_expert(0, None)
            for k in range(KT):
                sp.dma_start(wr1[:, k, :], Wr[k * P:(k + 1) * P, :]).then_inc(sem("l1_in"), 16)
            sp.dma_start(ebias_t[:, :], ebias.rearrange("(a e) -> a e", a=1).broadcast_to([RT, E])) \
                .then_inc(sem("l1_in"), 16)
            for b in BS:
                sp.wait_ge(sem("v_mm", b), 3)
            for q in range(3):
                for k in range(KT):
                    sp.dma_start(wqkv1[:, k, q, :].rearrange("p (n c) -> p n c", n=NH),
                                 a1_Wqkv[:, k * P:(k + 1) * P, q * HD:(q + 1) * HD].rearrange("n p c -> p n c"))\
                        .then_inc(sem("wqkv1_in"), 16)
            for b in BS:
                sp.wait_ge(sem("op_mm", b), KT)
            sp.dma_start(wo1[:, :, :], a1_Wo.rearrange("n h d -> (n h) d").rearrange("(k p) d -> p k d", p=P))\
                .then_inc(sem("l1_in"), 16)
            spread_routing(0)
            with sp.Fori(0, E - 1) as i:
                load_expert(i + 1, STEPS * i)

            sp.wait_ge(sem("whi_done"), STEPS * E)
            sp.wait_ge(sem("wlo_done"), STEPS * E)

            def load1(at, src):
                n = src.shape[1] * src.shape[2]
                sp.dma_start(raw[:, at:at + n].rearrange("p (k n) -> p k n", k=src.shape[1]), src)\
                    .then_inc(sem("experts1_in"), 16)

            for c in range(CH1):
                at = c % HALF1 * W1
                if c == HALF1:
                    sp.wait_ge(sem("w1split_done"), HALF1)
                if c < NSH:
                    for n, m in enumerate((Sg, Su)):
                        load1(at + n * GU, m.rearrange("(k p) f -> p k f", p=P)[:, :, c * F1:(c + 1) * F1])
                    load1(at + 2 * GU, Sd[c * F1:(c + 1) * F1, :].rearrange("p (a d) -> p a d", a=1))
                else:
                    for n, m in enumerate((Wg, Wu)):
                        load1(at + n * GU, m[c - NSH].rearrange("(k p) f -> p k f", p=P))
                    load1(at + 2 * GU, Wd[c - NSH].rearrange("p (a d) -> p a d", a=1))
            for b in BS:
                sp.wait_ge(sem("osb_done", b), 2)
                for t in range(2):
                    sp.dma_start(heads_dram[b].rearrange("n s c -> s n c")[t * P:(t + 1) * P],
                                 osb[:, b, t, :, :]).then_inc(sem("heads_out", b), 16)
                sp.dma_start(heads_dram[b, :, S - 1, :], ols[:, b, :]).then_inc(sem("heads_out", b), 16)
                sp.wait_ge(sem("heads_out", b), 48)
                sp.dma_start(cT[:, b, :, 0:S],
                             heads_dram[b].rearrange("n s c -> (n s c)").rearrange("(k p s) -> p k s", k=KT, p=P))\
                    .then_inc(sem("heads_in", b), 16)
            spread_routing(1)
            for b in BS:
                for t, (s0, rows) in enumerate(POS):
                    sp.wait_ge(sem("y_out_ready", b), t + 1)
                    sp.dma_start(out[b, s0:s0 + rows, :], v[0:rows, b, t, :]).then_inc(sem("stored"), 16)
            sp.wait_ge(sem("stored"), 16 * 3 * NB)

        @block.gpsimd
        def _(pool):
            cnt = [0]

            def link(ins):
                cnt[0] += 1
                ins.then_inc(sem("pool_chain"), 1)
                pool.wait_ge(sem("pool_chain"), cnt[0])

            pool.memset(avg[:, :], 1.0 / D).then_inc(sem("const"), 1)
            pool.memset(eps_t[:, :], EPS).then_inc(sem("const"), 1)
            pool.memset(h[:, :, :, S:N], 0.0).then_inc(sem("const"), 1)
            pool.memset(raw[:, WTOT - D:WTOT], 0.0).then_inc(sem("tail_zero"), 1)
            link(pool.memset(ident[:, :], 0.0))
            pool.affine_select(out=ident[:, :], in_=ident[:, :], compare_op=ALU.not_equal, fill=1.0, base=0,
                               pattern=[[-1, P]], channel_multiplier=1).then_inc(sem("const"), 1)
            pool.memset(ones[:, :], 1.0).then_inc(sem("const"), 1)
            for j in range(E):
                pool.memset(rank8[:, :, j:j + 1], float(E - j)).then_inc(sem("const"), 1)
            link(pool.memset(causal[:, :], 0.0))
            for t in (0, 2):
                pool.affine_select(out=causal[:, t * P:(t + 1) * P], in_=causal[:, t * P:(t + 1) * P],
                                   compare_op=ALU.is_ge, fill=1e10, base=0,
                                   pattern=[[-1, P]], channel_multiplier=1).then_inc(sem("const"), 1)
            link(pool.memset(headmask[:, :, :], 1.0))
            link(pool.affine_select(out=headmask[:, :, :], in_=headmask[:, :, :], compare_op=ALU.is_ge, fill=0.0,
                                    base=0, pattern=[[P, KT], [-HD, NH]], channel_multiplier=1))
            link(pool.affine_select(out=headmask[:, :, :], in_=headmask[:, :, :], compare_op=ALU.is_ge, fill=0.0,
                                    base=HD - 1, pattern=[[-P, KT], [HD, NH]], channel_multiplier=-1))
            for par in range(2):
                link(pool.tensor_copy(qscale[:, par:par + 1], headmask[:, 0, par:par + 1]))
                for n in range(par + 2, HPT, 2):
                    link(pool.tensor_tensor(qscale[:, par:par + 1], qscale[:, par:par + 1], headmask[:, 0, n:n + 1],
                                            ALU.add))
            pool.tensor_scalar(qscale[:, :], qscale[:, :], -HD ** -0.5, None, ALU.mult).then_inc(sem("const"), 1)

            def low_part(par, n, hi_count):
                at, size = PIECES[n]
                pool.wait_ge(sem("whi_done"), hi_count)
                pool.tensor_tensor(wlo[:, par, at:at + size], raw[:, at:at + size],
                                   f32(whi[:, par, at:at + size]), ALU.subtract).then_inc(sem("wlo_done"), 1)

            for n in range(STEPS):
                low_part(0, n, n + 1)

            def expert(i, par, prep):
                if prep:
                    e = 2 * i + par
                    pool.wait_ge(sem("down_done"), STEPS * e + OFF)
                    for n in range(STEPS):
                        low_part(1 - par, n, STEPS * (e + 1) + n + 1)

            with pool.Fori(0, E // 2 - 1) as i:
                for par in range(2):
                    expert(i, par, True)
            expert(E // 2 - 1, 0, True)

            pool.wait_ge(sem("down_done"), STEPS * E + OFF)
            for n in range(CH1):
                if n % HALF1 == 0:
                    pool.wait_ge(sem("experts1_in"), 16 * 3 * HALF1 * (n // HALF1 + 1))
                at, r = n * W1, raw[:, n % HALF1 * W1:(n % HALF1 + 1) * W1]
                link(pool.tensor_copy(whi1[:, at:at + W1], r))
                pool.tensor_tensor(wlo1[:, at:at + W1], r, f32(whi1[:, at:at + W1]), ALU.subtract)\
                    .then_inc(sem("w1split_done"), 1)

        CONST = 3 + 1 + 1 + E + 2 + 1

        @block.scalar
        def _(act):
            act.wait_ge(sem("const"), CONST)

            def preload(func):
                cnt[0] += 1
                act.activation(tmp[:, :], eps_t[0:1, :], func).then_inc(sem("act_preload"), 1)
                act.wait_ge(sem("act_preload"), cnt[0])

            cnt = [0]
            preload(ACT.Sqrt)

            def norm(n, b, cols):
                a, z = cols
                act.wait_ge(sem("ln_dev", b), n + 1)
                act.activation(sq[:, b, :, a:z], dev[:, b, :, a:z], ACT.Square).then_inc(sem("ln_sq", b), 1)

            def norm2(n, b, cols):
                a, z = cols
                act.wait_ge(sem("ln_var", b), n + 1)
                act.activation(sd[:, b, a:z], bk(b, 3)[:, a:z], ACT.Sqrt, bias=eps_t[:, 0:1])\
                    .then_inc(sem("ln_sd", b), 1)

            for b in BS:
                for m in range(KT):
                    act.wait_ge(sem("tok_mm", b), m + 1)
                    act.activation(y[:, b, m, 1:S], bk(b, m)[:, 0:NTOK], ACT.Copy).then_inc(sem("tok_sb", b), 1)
            for n in range(2):
                cols = (1, S) if n == 0 else (0, N)
                for b in BS:
                    norm(n, b, cols)
                for b in BS:
                    norm2(n, b, cols)
            def high_part(par, n, e):
                at, size = PIECES[n]
                if n % 4 == 0:
                    act.wait_ge(sem("expert_in", n // 4), (16 if n < 8 else 32) * (e + 1))
                act.activation(whi[:, par, at:at + size], raw[:, at:at + size], ACT.Copy)\
                    .then_inc(sem("whi_done"), 1)

            act.wait_ge(sem("small_in"), 16 * (KT * NB + 3))
            for b in BS:
                for m in range(2 * KT):
                    act.wait_ge(sem("qk_mm", b), m + 1)
                    act.activation(qk[:, b, m, :], bk(b, m)[:, 0:N], ACT.Identity, bias=bqkv0[:, m:m + 1])\
                        .then_inc(sem("qk_sb", b), 1)
            preload(ACT.Exp)
            for n in range(STEPS):
                high_part(0, n, 0)
            for t, (_s0, rows) in enumerate(POS):
                for b in BS:
                    act.wait_ge(sem("sc_nm", b), t + 1)
                    act.activation(prob[0:rows, b, t, 0:S], bk(b, (3 + t) % 4)[0:rows, 0:S], ACT.Exp,
                                   bias=stat[0:rows, b, t:t + 1], scale=D ** -0.5,
                                   accum_out=stat[0:rows, b, 4 + t:5 + t]).then_inc(sem("sc_exp", b), 1)
            for b in BS:
                for j, (_s0, rows) in enumerate(POS):
                    act.wait_ge(sem("pt_mm", b), j + 1)
                    act.activation(probT[0:rows, b, j, 0:S], bk(b, (2 + j) % 4)[0:rows, 0:S], ACT.Copy)\
                        .then_inc(sem("pt_sb", b), 1)
            for b in BS:
                for m in range(KT):
                    act.wait_ge(sem("cx_mm", b), m + 1)
                    act.activation(cT[:, b, m, 0:S], bk(b, 1 + m)[:, 0:S], ACT.Identity,
                                   bias=bqkv0[:, 2 * KT + m:2 * KT + m + 1]).then_inc(sem("cx_sb", b), 1)

            def norms(n):
                for b in BS:
                    norm(n, b, (0, N))
                for b in BS:
                    norm2(n, b, (0, N))

            preload(ACT.Sqrt)
            norms(2)
            preload(ACT.Exp)
            act.wait_ge(sem("rt_shift"), 1)
            act.activation(merged(route), merged(logit), ACT.Exp).then_inc(sem("rt_exp"), 1)
            preload(ACT.Silu)

            def x_high(par, count):
                for b in BS:
                    act.wait_ge(sem("xs_done"), count + b + 1)
                    act.activation(xhi[:, par, b, :, :], sq[:, b, :, :], ACT.Copy).then_inc(sem("xhi_done"), 1)

            x_high(0, 0)
            act.nop().then_inc(sem("silu_done"), OFF)
            act.nop().then_inc(sem("hhi_done"), OFF)

            def act_expert(i, par, prep):
                e = 2 * i + par
                for s in range(STEPS):
                    c, b = divmod(s, 2)
                    rows = P if c < HC - 1 else HTAIL
                    k = STEPS * e + s
                    act.wait_ge(sem("up_done"), k + 1)
                    act.wait_ge(sem("hmul_done"), k - 1 + OFF)
                    act.activation(sg[0:rows, b, :], bk(b, 0)[0:rows, 0:N], ACT.Silu).then_inc(sem("silu_done"), 1)
                    if prep:
                        if s == 2:
                            act.wait_ge(sem("down_done"), STEPS * e + OFF)
                        for n in range(*PREP[s]):
                            high_part(1 - par, n, e + 1)
                        if s == 4:
                            x_high(1 - par, 2 * (e + 1))
                    act.wait_ge(sem("hmul_done"), k + 1 + OFF)
                    act.wait_ge(sem("down_done"), k - 3 + OFF)
                    act.activation(hhi[0:rows, s % 4, :], hid[0:rows, b, :], ACT.Copy)\
                        .then_inc(sem("hhi_done"), 1)

            with act.Fori(0, E // 2 - 1) as i:
                for par in range(2):
                    act_expert(i, par, True)
            act_expert(E // 2 - 1, 0, True)
            act_expert(E // 2 - 1, 1, False)

            preload(ACT.Sqrt)
            norms(3)
            preload(ACT.Exp)
            for m in range(2 * KT):
                for b in BS:
                    act.wait_ge(sem("qk1_mm", b), m + 1)
                    for par in range(2 if m < KT else 1):
                        at = par * KT + m if m < KT else KT + m
                        ins = act.activation(qk[:, b, at, :], bk(b, m)[:, 0:N], ACT.Copy,
                                             scale=qscale[:, par:par + 1] if m < KT else 1.0)
                    ins.then_inc(sem("qk1_sb", b), 1)
            for b in BS:
                act.wait_ge(sem("last_nm", b), 1)
                act.activation(plast[:, b, 0:S], bank[6 + b][0:NH, 0:S], ACT.Exp, bias=lstat[:, b, 1:2],
                               scale=-1.0, accum_out=lstat[:, b, 2:3]).then_inc(sem("last_exp", b), 1)

            def head_exp(g):
                b, n = divmod(g, NH)
                if g >= 3:
                    act.wait_ge(sem("hp_mm"), g - 2)
                for t, (a, z) in enumerate(((0, P), (P, 3 * P))):
                    act.wait_ge(sem("hs_max"), 2 * g + t + 1)
                    act.activation(ph[:, g % 3, a:z], scm[:, g % 3, a:z], ACT.Exp, bias=hnm[:, g % 3, t:t + 1],
                                   scale=-1.0, accum_out=hsum[:, b, t, n:n + 1]).then_inc(sem("hs_exp"), 1)

            for g in range(NB * NH + 2):
                if g < NB * NH:
                    head_exp(g)
                if g >= 2 and g % 2 == 0:
                    head_evac(act, g - 2)

            preload(ACT.Sqrt)
            norms(4)
            preload(ACT.Exp)
            for b in BS:
                act.wait_ge(sem("ln_y", b), 4)
                act.activation(xhi[:, 0, b, :, :], y[:, b, :, :], ACT.Copy).then_inc(sem("xhi_done"), 1)
            act.wait_ge(sem("rt_shift"), 2)
            act.activation(rstat[:, :, :, 3:4].rearrange("p b r a -> p (b r) a"),
                           rstat[:, :, :, 2:3].rearrange("p b r a -> p (b r) a"), ACT.Exp).then_inc(sem("rt_exp"), 1)
            preload(ACT.Silu)
            K0 = STEPS * E
            for k in range(2 * CH1):
                c, b = divmod(k, 2)
                act.wait_ge(sem("up_done"), K0 + k + 1)
                act.wait_ge(sem("hmul_done"), K0 + k - 1 + OFF)
                act.activation(sg[:, b, :], bk(b, 0)[:, 0:N], ACT.Silu).then_inc(sem("silu_done"), 1)
                act.wait_ge(sem("hmul_done"), K0 + k + 1 + OFF)
                act.wait_ge(sem("down_done"), K0 + k - 3 + OFF)
                act.activation(hhi[:, k % 4, :], hid[:, b, :], ACT.Copy).then_inc(sem("hhi_done"), 1)
            for t, (_s0, rows) in enumerate(POS):
                for b in BS:
                    act.wait_ge(sem("ot_mm", b), t + 1)
                    act.activation(v[0:rows, b, t, :], bk(b, t % 2)[0:rows, 0:D], ACT.Copy)\
                        .then_inc(sem("y_out_ready", b), 1)

        @block.vector
        def _(dve):
            cnt = [0]

            def link(ins):
                cnt[0] += 1
                ins.then_inc(sem("dve_chain"), 1)
                dve.wait_ge(sem("dve_chain"), cnt[0])

            link(dve.memset(f32(zero[:, :]), 0.0))
            dve.nop().then_inc(sem("zero_ready"), 1)
            dve.wait_ge(sem("const"), CONST)
            dve.wait_ge(sem("small_in"), 16 * (KT * NB + 3))

            def norm_dev(n, b, src, cols):
                a, z = cols
                dve.wait_ge(sem("ln_mean", b), n + 1)
                mean = bk(b, 2)[:, a:z].unsqueeze(1).to_broadcast([P, KT, z - a])
                dve.tensor_tensor(dev[:, b, :, a:z], src[:, b, :, a:z], mean, ALU.subtract)\
                    .then_inc(sem("ln_dev", b), 1)

            def norm_out(n, b, cols):
                a, z = cols
                dve.wait_ge(sem("ln_sd", b), n + 1)
                link(dve.reciprocal(rstd[:, b, a:z], sd[:, b, a:z]))
                if n == 0:
                    for k in range(KT):
                        dve.scalar_tensor_tensor(out=h[:, b, k, a:z], in0=dev[:, b, k, a:z],
                                                 scalar=gamma_t[:, k:k + 1], in1=rstd[:, b, a:z],
                                                 op0=ALU.mult, op1=ALU.mult).then_inc(sem("h_done", b), 1)
                else:
                    r = rstd[:, b, a:z].unsqueeze(1).to_broadcast([P, KT, z - a])
                    dve.tensor_tensor(y[:, b, :, a:z], dev[:, b, :, a:z], r, ALU.mult).then_inc(sem("ln_y", b), 1)

            def norms(n):
                for b in BS:
                    norm_dev(n, b, h, (0, N))
                for b in BS:
                    norm_out(n, b, (0, N))

            for b in BS:
                norm_dev(0, b, y, (1, S))
            for b in BS:
                norm_out(0, b, (1, S))
            for b in BS:
                dve.wait_ge(sem("h_done", b), KT)
            norms(1)
            for t, (_s0, rows) in enumerate(POS):
                for b in BS:
                    dve.wait_ge(sem("v_mm", b), t + 1)
                    dve.tensor_copy(v[0:rows, b, t, :], bk(b, t)[0:rows, 0:D]).then_inc(sem("v_sb", b), 1)
            for t, (_s0, rows) in enumerate(POS):
                for b in BS:
                    dve.wait_ge(sem("sc_mm", b), t + 1)
                    link(dve.tensor_reduce(stat[0:rows, b, 8 + t:9 + t], bk(b, (3 + t) % 4)[0:rows, 0:S], AX,
                                           ALU.max))
                    dve.tensor_scalar(stat[0:rows, b, t:t + 1], stat[0:rows, b, 8 + t:9 + t], -D ** -0.5, None,
                                      ALU.mult).then_inc(sem("sc_nm", b), 1)
            for t, (_s0, rows) in enumerate(POS):
                for b in BS:
                    dve.wait_ge(sem("sc_exp", b), t + 1)
                    link(dve.reciprocal(stat[0:rows, b, 12 + t:13 + t], stat[0:rows, b, 4 + t:5 + t]))
                    dve.tensor_scalar(prob[0:rows, b, t, 0:S], prob[0:rows, b, t, 0:S],
                                      stat[0:rows, b, 12 + t:13 + t], None, ALU.mult).then_inc(sem("prob_ok", b), 1)
            for m in range(KT):
                for b in BS:
                    dve.wait_ge(sem("op_mm", b), m + 1)
                    dve.scalar_tensor_tensor(out=h[:, b, m, 0:S], in0=bk(b, (3 + m) % 4)[:, 0:S],
                                             scalar=bo0[:, m:m + 1], in1=h[:, b, m, 0:S],
                                             op0=ALU.add, op1=ALU.add).then_inc(sem("h_done", b), 1)
            for b in BS:
                dve.wait_ge(sem("h_done", b), 2 * KT)
            norms(2)

            R = NB * NR

            def wide(ap):
                return ap.to_broadcast([RT, R, E])

            def col(n):
                return rstat[:, :, :, n:n + 1].rearrange("p b r a -> p (b r) a")

            lg, eq_, p1, p2, rs, rt = (merged(t) for t in (logit, eq, pick1, pick2, rest, route))

            def top(src, pick, n):
                link(dve.tensor_reduce(col(n), src, AX, ALU.max))
                link(dve.tensor_tensor(eq_, src, wide(col(n)), ALU.is_equal))
                link(dve.tensor_tensor(eq_, eq_, rank8[0:RT, :, :], ALU.mult))
                link(dve.tensor_reduce(col(4), eq_, AX, ALU.max))
                link(dve.tensor_tensor(pick, eq_, wide(col(4)), ALU.is_equal))

            def top2(src):
                top(src, p1, 0)
                link(dve.scalar_tensor_tensor(out=rs, in0=p1, scalar=-HUGE, in1=src, op0=ALU.mult, op1=ALU.add))
                top(rs, p2, 1)

            def logits_in(b):
                return bk(b, 0)[0:RT, 0:NR * E].rearrange("p (r e) -> p r e", e=E)

            for b in BS:
                dve.wait_ge(sem("rt_mm", b), 1)
                link(dve.tensor_copy(rest[:, b], logits_in(b)))
            link(dve.tensor_reduce(col(0), rs, AX, ALU.max))
            dve.tensor_tensor(lg, rs, wide(col(0)), ALU.subtract).then_inc(sem("rt_shift"), 1)
            dve.wait_ge(sem("rt_exp"), 1)
            link(dve.tensor_reduce(col(5), rt, AX, ALU.add))
            link(dve.reciprocal(col(6), col(5)))
            link(dve.tensor_tensor(lg, rt, wide(col(6)), ALU.mult))
            top2(lg)
            link(dve.tensor_tensor(eq_, p1, p2, ALU.add))
            dve.tensor_tensor(rt, eq_, lg, ALU.mult).then_inc(sem("rt_done"), 1)

            def scaled_x(e):
                for b in BS:
                    w = big[:, b, :, bass.ds(e, 1)].rearrange("p n a -> p (a n)").unsqueeze(1)
                    dve.tensor_tensor(sq[:, b, :, :], y[:, b, :, :], w.to_broadcast([P, KT, N]), ALU.mult)\
                        .then_inc(sem("xs_done"), 1)

            def x_low(par, count):
                for b in BS:
                    dve.wait_ge(sem("xhi_done"), count + b + 1)
                    dve.tensor_tensor(xlo[:, par, b, :, :], sq[:, b, :, :], f32(xhi[:, par, b, :, :]), ALU.subtract)\
                        .then_inc(sem("xlo_done"), 1)

            for b in BS:
                dve.wait_ge(sem("rb_mm", b), 1)
                dve.tensor_tensor(sq[:, b, :, :], y[:, b, :, :],
                                  bk(b, 1)[:, 0:N].unsqueeze(1).to_broadcast([P, KT, N]), ALU.mult)\
                    .then_inc(sem("xs_done"), 1)
            x_low(0, 0)
            for name in ("hmul_done", "hlo_done"):
                dve.nop().then_inc(sem(name), OFF)

            def hidden_low(k, s, b, rows):
                dve.wait_ge(sem("hhi_done"), k + 1 + OFF)
                dve.tensor_tensor(hlo[0:rows, s % 4, :], hid[0:rows, b, :], f32(hhi[0:rows, s % 4, :]),
                                  ALU.subtract).then_inc(sem("hlo_done"), 1)

            def dve_expert(i, par, prep):
                e = 2 * i + par
                for s in range(STEPS):
                    c, b = divmod(s, 2)
                    rows = P if c < HC - 1 else HTAIL
                    k = STEPS * e + s
                    dve.wait_ge(sem("silu_done"), k + 1 + OFF)
                    dve.wait_ge(sem("hlo_done"), k - 1 + OFF)
                    dve.tensor_tensor(hid[0:rows, b, :], sg[0:rows, b, :], bk(b, 1)[0:rows, 0:N], ALU.mult)\
                        .then_inc(sem("hmul_done"), 1)
                    if prep and s == 2:
                        dve.wait_ge(sem("xlo_done"), 2 * (e + 1))
                        scaled_x(e + 1)
                    if prep and s == 6:
                        x_low(1 - par, 2 * (e + 1))
                    hidden_low(k, s, b, rows)

            for b in BS:
                dve.wait_ge(sem("rt_in", b), 16)
            with dve.Fori(0, E // 2 - 1) as i:
                for par in range(2):
                    dve_expert(i, par, True)
            dve_expert(E // 2 - 1, 0, True)
            dve_expert(E // 2 - 1, 1, False)
            for b in BS:
                for m in range(KT):
                    dve.wait_ge(sem("down_done"), STEPS * E + OFF)
                    dve.tensor_tensor(h[:, b, m, :], h[:, b, m, :], bk(b, 2 + m)[:, 0:N], ALU.add)\
                        .then_inc(sem("h_done", b), 1)
            for b in BS:
                dve.wait_ge(sem("h_done", b), 3 * KT)
            norms(3)
            for k in range(KT):
                dve.wait_ge(sem("wsum_mm"), 1)
                dve.tensor_copy(wsum[:, k:k + 1], bank[1][:, 256 + 2 * k:257 + 2 * k]).then_inc(sem("wsum_sb"), 1)
            for t, (_s0, rows) in enumerate(POS):
                for b in BS:
                    dve.wait_ge(sem("v1_mm", b), t + 1)
                    dve.tensor_copy(v[0:rows, b, t, :], bk(b, t)[0:rows, 0:D]).then_inc(sem("v1_sb", b), 1)
            for b in BS:
                dve.wait_ge(sem("qk1_sb", b), KT)
                for par in range(2):
                    dve.tensor_tensor(qlast[:, b, :, par:NH:2], headmask[:, :, par:NH:2],
                                      qk[:, b, par * KT:(par + 1) * KT, S - 1:S].to_broadcast([P, KT, NH // 2]),
                                      ALU.mult).then_inc(sem("qlast_done", b), 1)
            for b in BS:
                dve.wait_ge(sem("last_mm", b), 1)
                dve.tensor_reduce(lstat[:, b, 1:2], bank[6 + b][0:NH, 0:S], AX, ALU.min)\
                    .then_inc(sem("last_nm", b), 1)
            for b in BS:
                dve.wait_ge(sem("last_mm", b), 2)
                for j, (_s0, rows) in enumerate(POS):
                    dve.tensor_copy(plT[0:rows, b, j, :], bank[6 + b][0:rows, 16 * j:16 * j + NH])\
                        .then_inc(sem("plT_sb", b), 1)
            for b in BS:
                dve.wait_ge(sem("last_mm", b), 3)
                link(dve.tensor_tensor(olm[:, b], bank[6 + b][0:NH, 0:D].rearrange("p (n c) -> p n c", c=HD),
                                       ident[0:NH, 0:NH].unsqueeze(2).to_broadcast([NH, NH, HD]), ALU.mult))
                link(dve.tensor_reduce(ol[:, b, :], olm[:, b].rearrange("p n c -> p c n"), AX, ALU.add))
                link(dve.reciprocal(lstat[:, b, 3:4], lstat[:, b, 2:3]))
                dve.tensor_scalar(ols[:, b, :], ol[:, b, :], lstat[:, b, 3:4], None, ALU.mult)\
                    .then_inc(sem("osb_done", b), 1)
            def head_max(g):
                dve.wait_ge(sem("hs_mm"), g + 1)
                if g >= 3:
                    dve.wait_ge(sem("hs_exp"), 2 * (g - 2))
                for t, (a, z) in enumerate(((0, P), (P, 3 * P))):
                    dve.tensor_tensor_reduce(scm[:, g % 3, a:z], bank[g % 3][:, a:z], causal[:, a:z], 1.0, HUGE,
                                             ALU.add, ALU.min, hnm[:, g % 3, t:t + 1]).then_inc(sem("hs_max"), 1)

            def heads_out(b):
                dve.wait_ge(sem("hs_exp"), 2 * NH * (b + 1))
                link(dve.reciprocal(hinv[:, b], hsum[:, b]))
                dve.wait_ge(sem("av_mm"), NH * (b + 1))
                dve.tensor_tensor(osb[:, b].rearrange("p t n c -> p (t n) c"),
                                  bank[4 + b][:, :].rearrange("p (n c) -> p n c", c=HD),
                                  hinv[:, b].rearrange("p t n -> p (t n)").unsqueeze(2)
                                  .to_broadcast([P, 2 * NH, HD]), ALU.mult).then_inc(sem("osb_done", b), 1)

            for g in range(NB * NH + LAG):
                if g < NB * NH:
                    head_max(g)
                if 2 <= g < NB * NH + 2 and g % 2 == 1:
                    head_evac(dve, g - 2)
                if g >= LAG and (g - LAG) % NH == NH - 1:
                    heads_out((g - LAG) // NH)
            dve.wait_ge(sem("wsum_sb"), KT)
            for b in BS:
                dve.wait_ge(sem("heads_in", b), 16)
                for k in range(KT):
                    dve.scalar_tensor_tensor(out=h[:, b, k, 0:S], in0=cT[:, b, k, 0:S], scalar=wsum[:, k:k + 1],
                                             in1=h[:, b, k, 0:S], op0=ALU.mult, op1=ALU.add)\
                        .then_inc(sem("h_done", b), 1)
            for b in BS:
                dve.wait_ge(sem("h_done", b), 4 * KT)
            norms(4)
            for b in BS:
                dve.wait_ge(sem("xhi_done"), 2 * E + b + 1)
                dve.tensor_tensor(xlo[:, 0, b, :, :], y[:, b, :, :], f32(xhi[:, 0, b, :, :]), ALU.subtract)\
                    .then_inc(sem("xlo_done"), 1)
            dve.wait_ge(sem("l1_in"), 64)
            for b in BS:
                dve.wait_ge(sem("rt_mm", b), 2)
                dve.tensor_tensor(logit[:, b], logits_in(b), ebias_t[:, :].unsqueeze(1).to_broadcast([RT, NR, E]),
                                  ALU.add).then_inc(sem("rt_read", b), 1)
            for b in BS:
                dve.wait_ge(sem("rt_read", b), 1)
            top2(lg)
            dve.tensor_tensor(col(2), col(1), col(0), ALU.subtract).then_inc(sem("rt_shift"), 1)
            dve.wait_ge(sem("rt_exp"), 2)
            link(dve.tensor_scalar(col(5), col(3), 1.0, None, ALU.add))
            link(dve.reciprocal(col(6), col(5)))
            link(dve.tensor_tensor(eq_, p2, wide(col(3)), ALU.mult))
            link(dve.tensor_tensor(rs, eq_, p1, ALU.add))
            dve.wait_ge(sem("rt_out", 1), 16)
            dve.tensor_tensor(rt, rs, wide(col(6)), ALU.mult).then_inc(sem("rt_done"), 1)
            K0 = STEPS * E
            for k in range(2 * CH1):
                c, b = divmod(k, 2)
                dve.wait_ge(sem("silu_done"), K0 + k + 1 + OFF)
                dve.wait_ge(sem("hlo_done"), K0 + k - 1 + OFF)
                if c < NSH:
                    dve.tensor_tensor(hid[:, b, :], sg[:, b, :], bk(b, 1)[:, 0:N], ALU.mult)\
                        .then_inc(sem("hmul_done"), 1)
                else:
                    dve.wait_ge(sem("rt_in", b), 32)
                    link(dve.tensor_tensor(hidw[:, :], sg[:, b, :], bk(b, 1)[:, 0:N], ALU.mult))
                    dve.tensor_tensor(hid[:, b, :], hidw[:, :], big[:, b, :, c - NSH], ALU.mult)\
                        .then_inc(sem("hmul_done"), 1)
                hidden_low(K0 + k, k, b, P)
            for b in BS:
                for m in range(KT):
                    dve.wait_ge(sem("down_done"), STEPS * E + 2 * CH1 + OFF)
                    dve.tensor_tensor(h[:, b, m, :], h[:, b, m, :], bk(b, 2 + m)[:, 0:N], ALU.add)\
                        .then_inc(sem("h_done", b), 1)

        @block.tensor
        def _(pe):
            pe.wait_ge(sem("const"), CONST)

            def mm(o, w, m, start, stop, **kw):
                return pe.matmul(o, w, m, start=start, stop=stop, **kw)

            def norm_mean(n, b, src, cols):
                a, z = cols
                for k in range(KT):
                    last = mm(bk(b, 2)[:, a:z], avg[:, :], src[:, b, k, a:z], k == 0, k == KT - 1)
                last.then_inc(sem("ln_mean", b), 1)

            def norm_var(n, b, cols):
                a, z = cols
                pe.wait_ge(sem("ln_sq", b), n + 1)
                for k in range(KT):
                    last = mm(bk(b, 3)[:, a:z], avg[:, :], sq[:, b, k, a:z], k == 0, k == KT - 1)
                last.then_inc(sem("ln_var", b), 1)

            pe.wait_ge(sem("wtok_in"), 16 * JG)
            for b in BS:
                pe.wait_ge(sem("patches_in", b), 16 * JG * C)
                for m in range(KT):
                    for g in range(NJ):
                        rows = min(JG, PS - JG * g) * CI
                        last = mm(bk(b, m)[:, 0:NTOK], wtok[0:rows, g, m * P:(m + 1) * P],
                                  patches[0:rows, b, :, JG * g:W:PS], g == 0, g == NJ - 1)
                    last.then_inc(sem("tok_mm", b), 1)
            for b in BS:
                pe.wait_ge(sem("tok_sb", b), KT)
                norm_mean(0, b, y, (1, S))
            for b in BS:
                norm_var(0, b, (1, S))

            def norms(n):
                for b in BS:
                    pe.wait_ge(sem("h_done", b), n * KT)
                    norm_mean(n, b, h, (0, N))
                for b in BS:
                    norm_var(n, b, (0, N))

            pe.wait_ge(sem("small_in"), 16 * (KT * NB + 3))
            norms(1)
            pe.wait_ge(sem("wqkv0_in"), 16)
            for b in BS:
                pe.wait_ge(sem("ln_y", b), 1)
                for m in range(2 * KT):
                    for k in range(KT):
                        last = mm(bk(b, m)[:, 0:N], wqkv0[:, k, m * P:(m + 1) * P], y[:, b, k, :], k == 0, k == KT - 1)
                    last.then_inc(sem("qk_mm", b), 1)
            for t, (s0, rows) in enumerate(POS):
                for b in BS:
                    pe.wait_ge(sem("qk_sb", b), t + 1)
                    for k in range(KT):
                        last = mm(bk(b, t)[0:rows, 0:D], y[:, b, k, s0:s0 + rows], wqkv0[:, k, 2 * D:3 * D],
                                  k == 0, k == KT - 1)
                    last.then_inc(sem("v_mm", b), 1)
            for t, (s0, rows) in enumerate(POS):
                for b in BS:
                    pe.wait_ge(sem("qk_sb", b), 2 * KT)
                    if t:
                        pe.wait_ge(sem("v_sb", b), t)
                    for k in range(KT):
                        last = mm(bk(b, (3 + t) % 4)[0:rows, 0:S], qk[:, b, k, s0:s0 + rows],
                                  qk[:, b, KT + k, 0:S], k == 0, k == KT - 1)
                    last.then_inc(sem("sc_mm", b), 1)
            for j, (k0, kn) in enumerate(POS):
                for b in BS:
                    pe.wait_ge(sem("v_sb", b), 3)
                    pe.wait_ge(sem("prob_ok", b), 3)
                    for t, (s0, rows) in enumerate(POS):
                        last = pe.transpose(bk(b, (2 + j) % 4)[0:kn, s0:s0 + rows], prob[0:rows, b, t, k0:k0 + kn],
                                            ident[0:rows, 0:rows])
                    last.then_inc(sem("pt_mm", b), 1)
            for m in range(KT):
                for b in BS:
                    pe.wait_ge(sem("pt_sb", b), 3)
                    for j, (k0, kn) in enumerate(POS):
                        last = mm(bk(b, 1 + m)[:, 0:S], v[0:kn, b, j, m * P:(m + 1) * P], probT[0:kn, b, j, 0:S],
                                  j == 0, j == 2)
                    last.then_inc(sem("cx_mm", b), 1)
            pe.wait_ge(sem("wo0_in"), 16)
            for m in range(KT):
                for b in BS:
                    pe.wait_ge(sem("cx_sb", b), KT)
                    for k in range(KT):
                        last = mm(bk(b, (3 + m) % 4)[:, 0:S], wo0[:, k, m * P:(m + 1) * P], cT[:, b, k, 0:S],
                                  k == 0, k == KT - 1)
                    last.then_inc(sem("op_mm", b), 1)
            norms(2)

            def logits(layer, w):
                for b in BS:
                    pe.wait_ge(sem("ln_y", b), 2 if layer == 0 else 4)
                    for r in range(NR):
                        for k in range(KT):
                            last = mm(bk(b, 0)[0:RT, r * E:(r + 1) * E], y[:, b, k, r * RT:(r + 1) * RT], w[:, k, :],
                                      k == 0, k == KT - 1)
                    last.then_inc(sem("rt_mm", b), 1)

            pe.wait_ge(sem("gw_in"), 16 * KT)
            logits(0, gw)
            pe.wait_ge(sem("rt_done"), 1)
            for b in BS:
                for r in range(NR):
                    last = mm(bk(b, 1)[:, r * RT:(r + 1) * RT], route[:, b, r, 0:1].to_broadcast([RT, P]),
                              ident[0:RT, 0:RT], True, True)
                last.then_inc(sem("rb_mm", b), 1)

            def clear_sums(layer):
                for b in BS:
                    for m in range(KT):
                        mm(bk(b, 2 + m)[:, 0:N], zero[:, 0:P], zero[:, :], True, False, skip_group_check=True)

            def split_mm(o, whi_, wlo_, mhi, mlo, start, stop):
                kw = dict(skip_group_check=True)
                mm(o, whi_, mhi, start, False, **kw)
                mm(o, whi_, mlo, False, False, **kw)
                return mm(o, wlo_, mhi, False, stop, **kw)

            def up(k, s, e_par, ready=None):
                c, b = divmod(s, 2)
                cols = P if c < HC - 1 else HTAIL
                pe.wait_ge(sem("hmul_done"), k - 1 + OFF)
                for n in range(2):
                    for kt in range(KT):
                        at = n * WA + kt * HID + c * P
                        last = split_mm(bk(b, n)[0:cols, 0:N], whi[:, e_par, at:at + cols], wlo[:, e_par, at:at + cols],
                                        xhi[:, e_par, b, kt, :], xlo[:, e_par, b, kt, :], kt == 0, kt == KT - 1)
                last.then_inc(sem("up_done"), 1)

            def down(k, s, e_par, final):
                c, b = divmod(s, 2)
                rows = P if c < HC - 1 else HTAIL
                pe.wait_ge(sem("hhi_done"), k + 1 + OFF)
                pe.wait_ge(sem("hlo_done"), k + 1 + OFF)
                for m in range(KT):
                    at = 2 * WA + c * D + m * P
                    last = split_mm(bk(b, 2 + m)[:, 0:N], whi[0:rows, e_par, at:at + P], wlo[0:rows, e_par, at:at + P],
                                    hhi[0:rows, s % 4, :], hlo[0:rows, s % 4, :], False, final)
                last.then_inc(sem("down_done"), 1)

            def expert_ready(e):
                pe.wait_ge(sem("wlo_done"), STEPS * (e + 1))
                pe.wait_ge(sem("whi_done"), STEPS * (e + 1))
                pe.wait_ge(sem("xlo_done"), 2 * (e + 1))

            pe.wait_ge(sem("zero_ready"), 1)
            clear_sums(0)
            pe.nop().then_inc(sem("down_done"), OFF)
            expert_ready(0)
            up(0, 0, 0)
            up(1, 1, 0)

            def pe_expert(i, par, more):
                e = 2 * i + par
                for s in range(STEPS):
                    k = STEPS * e + s
                    if s + 2 < STEPS:
                        up(k + 2, s + 2, par)
                    elif more:
                        if s + 2 == STEPS:
                            expert_ready(e + 1)
                        up(k + 2, s + 2 - STEPS, 1 - par)
                    down(k, s, par, (not more) and s >= STEPS - 2)

            with pe.Fori(0, E // 2 - 1) as i:
                for par in range(2):
                    pe_expert(i, par, True)
            pe_expert(E // 2 - 1, 0, True)
            pe_expert(E // 2 - 1, 1, False)

            norms(3)
            pe.wait_ge(sem("wqkv1_in"), 16 * 3 * KT)
            for m in range(2 * KT):
                w = wqkv1[:, :, m // KT, m % KT * P:(m % KT + 1) * P]
                for b in BS:
                    if m == 0:
                        pe.wait_ge(sem("ln_y", b), 3)
                    for k in range(KT):
                        last = mm(bk(b, m)[:, 0:N], w[:, k, :], y[:, b, k, :], k == 0, k == KT - 1)
                    last.then_inc(sem("qk1_mm", b), 1)
            pe.wait_ge(sem("l1_in"), 64)
            for t, (s0, rows) in enumerate(POS):
                for b in BS:
                    pe.wait_ge(sem("qk1_sb", b), t + 1)
                    if t == 1 and b == 0:
                        for m in range(KT):
                            for k in range(KT):
                                last = mm(bank[1][:, 256 + 2 * m:257 + 2 * m], wo1[:, k, m * P:(m + 1) * P],
                                          ones[:, 0:1], k == 0, k == KT - 1)
                        last.then_inc(sem("wsum_mm"), 1)
                        pe.wait_ge(sem("wsum_sb"), KT)
                    for k in range(KT):
                        last = mm(bk(b, t)[0:rows, 0:D], y[:, b, k, s0:s0 + rows],
                                  wqkv1[:, k, 2, :], k == 0, k == KT - 1)
                    last.then_inc(sem("v1_mm", b), 1)
            for b in BS:
                pe.wait_ge(sem("qk1_sb", b), 2 * KT)
                pe.wait_ge(sem("v1_sb", b), 3)
            for b in BS:
                pe.wait_ge(sem("qlast_done", b), 2)
                for t in range(KT):
                    last = mm(bank[6 + b][0:NH, 0:S], qlast[:, b, t, :], qk[:, b, 2 * KT + t, 0:S], t == 0,
                              t == KT - 1)
                last.then_inc(sem("last_mm", b), 1)
            for b in BS:
                pe.wait_ge(sem("last_exp", b), 1)
                for j, (k0, kn) in enumerate(POS):
                    last = pe.transpose(bank[6 + b][0:kn, 16 * j:16 * j + NH], plast[:, b, k0:k0 + kn],
                                        ident[0:NH, 0:NH])
                last.then_inc(sem("last_mm", b), 1)
            for b in BS:
                pe.wait_ge(sem("plT_sb", b), 3)
                for j, (k0, kn) in enumerate(POS):
                    last = mm(bank[6 + b][0:NH, 0:D], plT[0:kn, b, j, :], v[0:kn, b, j, :], j == 0, j == 2)
                last.then_inc(sem("last_mm", b), 1)

            def head_scores(g):
                b, n = divmod(g, NH)
                t, p0 = n // HPT, n % HPT // 2 * PAIR
                if g >= 3:
                    pe.wait_ge(sem("hs_max"), 2 * (g - 2))
                q, kk = qk[p0:p0 + PAIR, b, n % 2 * KT + t, :], qk[p0:p0 + PAIR, b, 2 * KT + t, :]
                mm(bank[g % 3][:, 0:P], q[:, 0:P], kk[:, 0:P], True, True)
                mm(bank[g % 3][:, P:3 * P], q[:, P:2 * P], kk[:, 0:2 * P], True, True)\
                    .then_inc(sem("hs_mm"), 1)

            def head_turn(g):
                pe.wait_ge(sem("hs_exp"), 2 * (g + 1))
                if g >= 2:
                    wait_evac(pe, g - 2)
                if g == 1:
                    pe.wait_ge(sem("osb_done", 1), 1)
                for j in range(3):
                    last = pe.transpose(turn_bank(g)[:, j * P:(j + 1) * P], ph[:, g % 3, j * P:(j + 1) * P],
                                        ident[:, :])
                last.then_inc(sem("hp_mm"), 1)

            def head_out(g):
                b, n = divmod(g, NH)
                wait_evac(pe, g)
                vn = v[:, b, :, n * HD:(n + 1) * HD]
                o = bank[4 + b]
                mm(o[:, n * HD:(n + 1) * HD], phT[:, g % 3, 0:P], vn[:, 0, :], True, True)
                mm(o[:, D + n * HD:D + (n + 1) * HD], phT[:, g % 3, P:2 * P], vn[:, 0, :], True, False)
                mm(o[:, D + n * HD:D + (n + 1) * HD], phT[:, g % 3, 2 * P:3 * P], vn[:, 1, :], False, True)\
                    .then_inc(sem("av_mm"), 1)

            for g in range(NB * NH + LAG):
                if g < NB * NH:
                    head_scores(g)
                if 2 <= g < NB * NH + 2:
                    head_turn(g - 2)
                if g >= LAG:
                    head_out(g - LAG)

            norms(4)
            logits(1, wr1)
            clear_sums(1)
            pe.wait_ge(sem("w1split_done"), CH1)
            for b in BS:
                pe.wait_ge(sem("rt_read", b), 1)
            pe.wait_ge(sem("xlo_done"), 2 * E + 2)
            K0 = STEPS * E

            def up1(k):
                c, b = divmod(k, 2)
                pe.wait_ge(sem("hmul_done"), K0 + k - 1 + OFF)
                for n in range(2):
                    for kt in range(KT):
                        at = c * W1 + n * GU + kt * F1
                        last = split_mm(bk(b, n)[:, 0:N], whi1[:, at:at + F1], wlo1[:, at:at + F1],
                                        xhi[:, 0, b, kt, :], xlo[:, 0, b, kt, :], kt == 0, kt == KT - 1)
                last.then_inc(sem("up_done"), 1)

            def down1(k):
                c, b = divmod(k, 2)
                pe.wait_ge(sem("hhi_done"), K0 + k + 1 + OFF)
                pe.wait_ge(sem("hlo_done"), K0 + k + 1 + OFF)
                for m in range(KT):
                    at = c * W1 + 2 * GU + m * P
                    last = split_mm(bk(b, 2 + m)[:, 0:N], whi1[:, at:at + P], wlo1[:, at:at + P],
                                    hhi[:, k % 4, :], hlo[:, k % 4, :], False, c == CH1 - 1)
                last.then_inc(sem("down_done"), 1)

            for k in range(2 * CH1 + 2):
                if k < 2 * CH1:
                    up1(k)
                if k >= 2:
                    down1(k - 2)
            for t, (s0, rows) in enumerate(POS):
                for b in BS:
                    pe.wait_ge(sem("h_done", b), 5 * KT)
                    if t == 2:
                        pe.wait_ge(sem("y_out_ready", b), 1)
                    for k in range(KT):
                        last = pe.transpose(bk(b, t % 2)[0:rows, k * P:(k + 1) * P], h[:, b, k, s0:s0 + rows],
                                            ident[:, :])
                    last.then_inc(sem("ot_mm", b), 1)


_INS = ['x', 'cls_tok', 'L0_tok_W', 'L0_tok_gamma', 'L0_attn_W_qkv', 'L0_attn_b_qkv', 'L0_attn_W_out',
        'L0_attn_b_out', 'L0_ffn_gate_w', 'L0_ffn_w1', 'L0_ffn_w2', 'L0_ffn_w3', 'L1_attn_W_qkv', 'L1_attn_W_out',
        'L1_ffn_Wr', 'L1_ffn_Wg', 'L1_ffn_Wu', 'L1_ffn_Wd', 'L1_ffn_Sg', 'L1_ffn_Su', 'L1_ffn_Sd',
        'L1_ffn_expert_bias']
_OUTS = [((2, 257, 256), 'float32')]


def kernel(**inputs):
    import numpy as _np
    import concourse.bacc as _bacc
    from concourse import mybir as _mybir
    from concourse.bass_utils import run_bass_kernel_spmd as _run

    nc = _bacc.Bacc("TRN2", target_bir_lowering=False, num_devices=1)
    arrays, args = {}, []
    for name in _INS:
        a = _np.ascontiguousarray(inputs[name])
        arrays[f"in_{name}_dram"] = a
        args.append(nc.dram_tensor(f"in_{name}_dram", a.shape, _mybir.dt.from_np(a.dtype), kind="ExternalInput").ap())
    for i, (shape, dtype) in enumerate(_OUTS):
        dt = _mybir.dt.from_np(_np.dtype(dtype))
        args.append(nc.dram_tensor(f"out_{i}_dram", shape, dt, kind="ExternalOutput").ap())
    vit_tower(nc, *args)
    r = _run(nc, [arrays], core_ids=[0])
    got = tuple(r.results[0][f"out_{i}_dram"] for i in range(len(_OUTS)))
    return got[0]
```

```python
from contextlib import ExitStack

import concourse.bass as bass
from concourse import mybir

F32 = mybir.dt.float32
F32R = mybir.dt.float32r
ALU = mybir.AluOpType
ACT = mybir.ActivationFunctionType
AX = mybir.AxisListType.X

P = 128
EPS = 1e-5
HUGE = 1e38


def vit_tower(nc, x, cls_tok, tok_W, tok_gamma, a0_Wqkv, a0_bqkv, a0_Wo, a0_bo, gate_w, w1, w2, w3,
              a1_Wqkv, a1_Wo, Wr, Wg, Wu, Wd, Sg, Su, Sd, ebias, out):
    NB, C, H, W = x.shape
    D = tok_W.shape[1]
    KT = D // P
    PS = 8
    HY, WX = H // PS, W // PS
    NTOK = HY * WX
    NTT = NTOK // P
    S = NTOK + 1
    N = S + 1
    CI = C * PS
    JG = 3
    NJ = (PS + JG - 1) // JG
    E, HID = w1.shape[0], w1.shape[2]
    HC = (HID + P - 1) // P
    HTAIL = HID - (HC - 1) * P
    NH, HD = a1_Wqkv.shape[0], a1_Wqkv.shape[2] // 3
    PAIR = 2 * HD
    HPQ = P // PAIR
    NQ = NH // HPQ
    NG = NH // HPQ
    F1 = Wg.shape[2]
    RT = 86
    NR = N // RT
    POS = [(0, P), (P, P), (2 * P, 1)]
    assert NR * RT == N and S == 2 * P + 1 and D == 256 and F1 == P

    MAIN = (HC - 1) * P
    WA = 2 * HID
    WTOT = KT * WA + HC * D
    STEPS = 2 * HC
    PIECES = [(i * WA // 4, WA // 4) for i in range(4 * KT)]
    PIECES += [(KT * WA + i * HC * D // 4, HC * D // 4) for i in range(4)]
    assert len(PIECES) == STEPS and E % 2 == 0 and HTAIL == P // 2 and KT == 2
    PREP = [(0, 0)] * 2 + [(2 * s, 2 * s + 2) for s in range(6)] + [(12, 12)] * (STEPS - 8)
    CH1 = Sg.shape[1] // F1 + E
    NSH = CH1 - E
    LAG = 4
    LAST = 1
    GEND = NB * NH + LAG + 3
    OFF = 4

    ctx = ExitStack()
    with ctx:
        sems = {}

        def sem(name, b=None):
            key = name if b is None else f"{name}_{b}"
            if key not in sems:
                sems[key] = ctx.enter_context(nc.semaphore(key))
            return sems[key]

        def sb(name, shape, dt=F32):
            return ctx.enter_context(nc.sbuf_tensor(name, shape, dt))

        h = sb("h", [P, NB, KT, N])
        y = sb("y", [P, NB, KT, N])
        dev = sb("dev", [P, NB, KT, N])
        sq = sb("sq", [P, NB, KT, N])
        tmp = sb("tmp", [1, 1])
        sd = sb("sd", [P, NB, N])
        rstd = sb("rstd", [P, NB, N])
        big = sb("big", [P, NB, N, E])
        ident = sb("ident", [P, P])
        avg = sb("avg", [P, P])
        ones = sb("ones", [P, 2])
        eps_t = sb("eps_t", [P, 1])
        rank8 = sb("rank8", [P, NB * NR, E])
        causal = sb("causal", [P, 3 * P])
        headmask = sb("headmask", [P, NQ, NH])
        odd = sb("odd", [P, P // HD])
        qscale = sb("qscale", [P, 2])
        wtok = sb("wtok", [JG * CI, NJ, D])
        gamma_t = sb("gamma_t", [P, KT])
        wqkv0 = sb("wqkv0", [P, KT, 3 * D])
        bqkv0 = sb("bqkv0", [P, 3 * KT])
        wo0 = sb("wo0", [P, KT, D])
        bo0 = sb("bo0", [P, KT])
        gw = sb("gw", [P, KT, E])
        wr1 = sb("wr1", [P, KT, E])
        ebias_t = sb("ebias_t", [RT, E])
        wo1 = wo0
        wsum = sb("wsum", [P, KT])
        qk = big[:, :, :, :].rearrange("p b n e -> p (b n e)")[:, 0:NB * 2 * KT * N]\
            .rearrange("p (b m n) -> p b m n", b=NB, m=2 * KT)
        v = sb("v", [P, NB, 3, D])
        prob = sb("prob", [P, NB, 3, N])
        probT = sb("probT", [P, NB, 3, N])
        wq1, wk1 = (t[:, :, :, :].rearrange("p b t n -> p (b t n)")[:, 0:KT * 2 * D]
                    .rearrange("p (k n) -> p k n", k=KT) for t in (prob, probT))
        wv1 = wqkv0[:, :, 0:D]
        cT = dev
        stat = sb("stat", [P, NB, 16])
        logit = sb("logit", [RT, NB, NR, E])
        eq = sb("eq", [RT, NB, NR, E])
        pick1 = sb("pick1", [RT, NB, NR, E])
        pick2 = sb("pick2", [RT, NB, NR, E])
        rest = sb("rest", [RT, NB, NR, E])
        route = sb("route", [RT, NB, NR, E])
        rstat = sb("rstat", [RT, NB, NR, 8])
        raw = sb("raw", [P, WTOT])
        whi = sb("whi", [P, 2, WTOT], F32R)
        wlo = sb("wlo", [P, 2, WTOT], F32R)
        xhi = sb("xhi", [P, 2, NB, KT, N], F32R)
        xlo = sb("xlo", [P, 2, NB, KT, N], F32R)
        sg = sb("sg", [P, NB, N])
        hid = sb("hid", [P, NB, N])
        hidw = sb("hidw", [P, N])
        hhi = sb("hhi", [P, 4, N], F32R)
        hlo = sb("hlo", [P, 4, N], F32R)
        hhi_tail = sb("hhi_tail", [P, NB, N], F32R)
        hlo_tail = sb("hlo_tail", [P, NB, N], F32R)
        zero = sb("zero", [P, N], F32R)
        scm = prob[:, :, :, :].rearrange("p b t n -> p (b t n)")[:, 0:12 * P]\
            .rearrange("p (a n) -> p a n", a=4)
        ph = probT[:, :, :, :].rearrange("p b t n -> p (b t n)")[:, 0:12 * P].rearrange("p (a n) -> p a n", a=4)
        phT = sb("phT", [P, 3, 3 * P])
        hnm = sb("hnm", [P, 4, 2])
        hsum = sb("hsum", [P, NB, NG, 2, HPQ])
        hinv = sb("hinv", [P, NB, NG, 2, HPQ])
        osb = sb("osb", [P, NB, NG, 2, HPQ, HD])
        qlast = sb("qlast", [P, NB, NQ, NH], F32R)
        plast = sb("plast", [NH, NB, N])
        plT = sb("plT", [P, NB, 3, NH])
        oT = sg
        olm = hid[0:NH, :, 0:NH * HD].rearrange("p b (n c) -> p b n c", n=NH)
        ol = sb("ol", [NH, NB, HD])
        ols = sb("ols", [NH, NB, HD])
        lstat = sb("lstat", [NH, NB, 4])
        patches = big[:, :, :, :].rearrange("p b n e -> p (b n e)")[0:JG * CI, 0:NB * HY * W] \
            .rearrange("p (b n) -> p b n", b=NB)
        whi1 = whi[:, :, :].rearrange("p a n -> p (a n)")
        wlo1 = wlo[:, :, :].rearrange("p a n -> p (a n)")
        GU = KT * F1
        W1 = 2 * GU + D
        HALF1 = CH1 // 2
        assert HALF1 * W1 <= WTOT and CH1 * W1 <= 2 * WTOT

        route_dram = nc.dram_tensor("route_dram", (2, NB, N, E), F32, kind="Internal").ap()
        heads_dram = nc.dram_tensor("heads_dram", (NB, NH, S, HD), F32, kind="Internal").ap()

        def merged(t):
            return t[:, :, :, :].rearrange("p b r e -> p (b r) e")

        bank = [ctx.enter_context(nc.psum_tensor(f"bank{i}", [P, 512], F32)) for i in range(8)]

        def bk(b, i):
            return bank[4 * b + i]

        ctx.enter_context(nc.allow_non_contiguous_dma(reason="small per-feature vectors and one column"))
        block = ctx.enter_context(nc.Block())
        BS = range(NB)

        def last_scored(b, cols):
            return bank[(7, 5)[b]][0:NH, 0:cols]

        def last_valued(b):
            return bank[7][0:NH, b * D:(b + 1) * D]

        def hidden(c, par):
            return slice(0, P) if c < HC - 1 else (slice(0, HTAIL), slice(HTAIL, P))[par]

        def gates(c, par):
            return slice(0, P) if c < HC - 1 else (slice(HTAIL, P), slice(0, HTAIL))[par]

        def hslot(t, s):
            return t[0][:, s % 4, :] if s < STEPS - 2 else t[1][:, s % 2, :]

        def f32(ap):
            return ap.bitcast(F32)

        assert NQ == 2 * KT == 4

        def khi(b, t):
            return xhi[:, t // KT, b, t % KT, :]

        def qsplit(b, t):
            return (hhi, hlo)[b][:, t, :]

        def klo(b, t):
            return xlo[:, t // KT, b, t % KT, :]

        def head_evac(eng, g):
            eng.wait_ge(sem("hp_mm"), g + 1)
            if g >= 3:
                eng.wait_ge(sem("av_mm"), g - 2)
            if g % 2 == 0:
                nc.scalar.activation(phT[:, g % 3, :], turn_bank(g)[:, 0:3 * P], ACT.Copy)\
                    .then_inc(sem("hp_even"), 1)
            else:
                nc.vector.tensor_copy(phT[:, g % 3, :], turn_bank(g)[:, 0:3 * P]).then_inc(sem("hp_odd"), 1)

        def wait_evac(eng, g):
            eng.wait_ge(sem("hp_even" if g % 2 == 0 else "hp_odd"), g // 2 + 1)

        def turn_bank(g):
            return bank[3 if g % 2 == 0 else 6]

        def load_patches(eng, b, channels):
            for jj in range(JG):
                for c in channels:
                    p0 = jj * CI + c * PS
                    eng.dma_start(patches[p0:p0 + PS, b, :].rearrange("p (y w) -> p y w", y=HY)[:, :, 0:W - jj],
                                  x[b, c].rearrange("(y i) w -> i y w", i=PS)[:, :, jj:W])\
                        .then_inc(sem("patches_in" if eng is not nc.gpsimd else "patches_in_sw", b), 16)

        @block.sync
        def _(sp):
            wt = tok_W.rearrange("(c j) d -> c j d", j=PS)
            for jj in range(JG):
                ng = len(range(jj, PS, JG))
                sp.dma_start(wtok[jj * CI:(jj + 1) * CI, 0:ng, :], wt[:, jj:PS:JG, :])\
                    .then_inc(sem("wtok_in"), 16)
            load_patches(sp, 0, range(0, C, 2))
            sp.dma_start(gamma_t[:, :], tok_gamma.rearrange("(k p) -> p k", p=P)).then_inc(sem("gamma_in"), 16)

            def load_class_token(b):
                for k in range(KT):
                    sp.dma_start(h[:, b, k, 0:1], cls_tok[0, 0:1, k * P:(k + 1) * P].rearrange("a p -> p a"))\
                        .then_inc(sem("cls_in", b), 16)

            load_class_token(0)
            load_patches(sp, 1, range(C - 1))
            load_class_token(1)
            sp.dma_start(bqkv0[:, :], a0_bqkv.rearrange("(k p) -> p k", p=P)).then_inc(sem("small_in"), 16)
            sp.dma_start(bo0[:, :], a0_bo.rearrange("(k p) -> p k", p=P)).then_inc(sem("small_in"), 16)
            sp.dma_start(wqkv0[:, :, :], a0_Wqkv.rearrange("(k p) n -> p k n", p=P)).then_inc(sem("wqkv0_in"), 16)
            sp.dma_start(wo0[:, :, :], a0_Wo.rearrange("(k p) n -> p k n", p=P)).then_inc(sem("wo0_in"), 16)
            for k in range(KT):
                sp.dma_start(gw[:, k, :], gate_w[:, k * P:(k + 1) * P].rearrange("e p -> p e"))\
                    .then_inc(sem("gw_in"), 16)

            def load_expert(e, par, before):
                def third(n):
                    if before is not None:
                        sp.wait_ge(sem("whi_done"), before + 4 * (n + 1))
                        sp.wait_ge(sem("wlo_done"), before + 4 * (n + 1))
                tails = ((w3, w1), (w1, w3))[par]
                for k in range(KT):
                    third(k)
                    for at, w, c0, c1 in ((0, w1, 0, MAIN), (MAIN, tails[0], MAIN, HID), (HID, tails[1], MAIN, HID),
                                          (P + MAIN, w3, 0, MAIN)):
                        sp.dma_start(raw[:, k * WA + at:k * WA + at + c1 - c0],
                                     w[bass.ds(e, 1), k * P:(k + 1) * P, c0:c1].rearrange("a p n -> p (a n)"))\
                            .then_inc(sem("expert_in", k), 16)
                third(2)
                rd = raw[:, KT * WA:WTOT].rearrange("p (c n) -> p c n", c=HC)
                sp.dma_start(rd[:, 0:HC - 1, :],
                             w2[bass.ds(e, 1), 0:MAIN, :].rearrange("a (c p) n -> p (a c) n", p=P))\
                    .then_inc(sem("expert_in", 2), 16)
                if par:
                    for t in range(2):
                        sp.dma_start(rd[t * HTAIL:(t + 1) * HTAIL, HC - 1, :],
                                     w2[bass.ds(e - 1 + t, 1), MAIN:HID, :].rearrange("a p n -> p (a n)"))\
                            .then_inc(sem("expert_in", 2), 16)

            def spread_routing(layer):
                for b in BS:
                    sp.wait_ge(sem("rt_done"), layer + 1)
                    sp.dma_start(route_dram[layer, b].rearrange("(r p) e -> p r e", p=RT), route[:, b, :, :])\
                        .then_inc(sem("rt_out", b), 16)
                for b in BS:
                    sp.wait_ge(sem("rt_out", b), 16 * (layer + 1))
                    sp.dma_start(big[:, b, :, :].rearrange("p n e -> p (n e)"),
                                 route_dram[layer, b].rearrange("n e -> (n e)").rearrange("(a n) -> a n", a=1)
                                 .broadcast_to([P, N * E])).then_inc(sem("rt_in", b), 16)

            sp.wait_ge(sem("tail_zero"), 1)
            load_expert(0, 0, None)
            for k in range(KT):
                sp.dma_start(wr1[:, k, :], Wr[k * P:(k + 1) * P, :]).then_inc(sem("l1_in"), 16)
            sp.dma_start(ebias_t[:, :], ebias.rearrange("(a e) -> a e", a=1).broadcast_to([RT, E])) \
                .then_inc(sem("l1_in"), 16)
            for b in BS:
                sp.wait_ge(sem("op_mm", b), KT)
            sp.dma_start(wo1[:, :, :], a1_Wo.rearrange("n h d -> (n h) d").rearrange("(k p) d -> p k d", p=P))\
                .then_inc(sem("l1_in"), 16)
            load_expert(1, 1, 0)
            spread_routing(0)
            with sp.Fori(1, E // 2) as i:
                for par in range(2):
                    load_expert(2 * i + par, par, STEPS * (2 * i + par - 1))
            for q, (w, copies) in enumerate(((wq1, 2), (wk1, 2), (wv1, 1))):
                for k in range(KT):
                    for d in range(copies):
                        sp.dma_start(w[:, k, :].rearrange("p (n d c) -> p n d c", n=NH, d=copies)[:, :, d, :],
                                     a1_Wqkv[:, k * P:(k + 1) * P, q * HD:(q + 1) * HD]
                                     .rearrange("n p c -> p n c")).then_inc(sem("wqkv1_in"), 16)

            sp.wait_ge(sem("whi_done"), STEPS * E)
            sp.wait_ge(sem("wlo_done"), STEPS * E)

            def load1(at, src):
                n = src.shape[1] * src.shape[2]
                sp.dma_start(raw[:, at:at + n].rearrange("p (k n) -> p k n", k=src.shape[1]), src)\
                    .then_inc(sem("experts1_in"), 16)

            for c in range(CH1):
                at = c % HALF1 * W1
                if c == HALF1:
                    sp.wait_ge(sem("w1split_done"), HALF1)
                if c < NSH:
                    for n, m in enumerate((Sg, Su)):
                        load1(at + n * GU, m.rearrange("(k p) f -> p k f", p=P)[:, :, c * F1:(c + 1) * F1])
                    load1(at + 2 * GU, Sd[c * F1:(c + 1) * F1, :].rearrange("p (a d) -> p a d", a=1))
                else:
                    for n, m in enumerate((Wg, Wu)):
                        load1(at + n * GU, m[c - NSH].rearrange("(k p) f -> p k f", p=P))
                    load1(at + 2 * GU, Wd[c - NSH].rearrange("p (a d) -> p a d", a=1))
            for b in BS:
                sp.wait_ge(sem("ols_done", b), 1)
                sp.dma_start(heads_dram[b, :, S - 1, :], ols[:, b, :]).then_inc(sem("heads_out", b), 16)
            for b in BS:
                for gr in range(NG):
                    n0, f0 = gr * HPQ, gr * HPQ * HD
                    sp.wait_ge(sem("osb_done", b), gr + 1)
                    for t in range(2):
                        sp.dma_start(heads_dram[b, n0:n0 + HPQ, t * P:(t + 1) * P, :].rearrange("n s c -> s n c"),
                                     osb[:, b, gr, t, :, :]).then_inc(sem("heads_out", b), 16)
                    sp.wait_ge(sem("heads_out", b), 16 * (2 * gr + 3))
                    sp.dma_start(cT[f0 % P:f0 % P + HPQ * HD, b, f0 // P, 0:S],
                                 heads_dram[b, n0:n0 + HPQ].rearrange("n s c -> (n s c)")
                                 .rearrange("(p s) -> p s", s=S)).then_inc(sem("heads_in", b), 16)
            spread_routing(1)
            for b in BS:
                for t, (s0, rows) in enumerate(POS):
                    if t == 1:
                        sp.wait_ge(sem("y_odd_ready", b), 1)
                    else:
                        sp.wait_ge(sem("y_out_ready", b), t // 2 + 1)
                    sp.dma_start(out[b, s0:s0 + rows, :], v[0:rows, b, t, :]).then_inc(sem("stored"), 16)
            sp.wait_ge(sem("stored"), 16 * 3 * NB)

        @block.gpsimd
        def _(pool):
            cnt = [0]

            def link(ins):
                cnt[0] += 1
                ins.then_inc(sem("pool_chain"), 1)
                pool.wait_ge(sem("pool_chain"), cnt[0])

            load_patches(pool, 1, range(C - 1, C))
            pool.memset(avg[:, :], 1.0 / D).then_inc(sem("const"), 1)
            pool.memset(eps_t[:, :], EPS).then_inc(sem("const"), 1)
            pool.memset(h[:, :, :, S:N], 0.0).then_inc(sem("const"), 1)
            pool.memset(raw[:, WTOT - D:WTOT], 0.0).then_inc(sem("tail_zero"), 1)
            link(pool.memset(ident[:, :], 0.0))
            pool.affine_select(out=ident[:, :], in_=ident[:, :], compare_op=ALU.not_equal, fill=1.0, base=0,
                               pattern=[[-1, P]], channel_multiplier=1).then_inc(sem("const"), 1)
            pool.memset(ones[:, :], 1.0).then_inc(sem("const"), 1)
            for j in range(E):
                pool.memset(rank8[:, :, j:j + 1], float(E - j)).then_inc(sem("const"), 1)
            link(pool.memset(causal[:, :], 0.0))
            for t in (0, 2):
                pool.affine_select(out=causal[:, t * P:(t + 1) * P], in_=causal[:, t * P:(t + 1) * P],
                                   compare_op=ALU.is_ge, fill=1e10, base=0,
                                   pattern=[[-1, P]], channel_multiplier=1).then_inc(sem("const"), 1)

            def blocks(t, width):
                n = t.shape[-1]
                k = t.shape[1] if len(t.shape) == 3 else 1
                pat = [[P, k], [-width, n]] if len(t.shape) == 3 else [[-width, n]]
                back = [[-a, c] for a, c in pat]
                link(pool.memset(t, 1.0))
                link(pool.affine_select(out=t, in_=t, compare_op=ALU.is_ge, fill=0.0, base=0, pattern=pat,
                                        channel_multiplier=1))
                link(pool.affine_select(out=t, in_=t, compare_op=ALU.is_ge, fill=0.0, base=width - 1,
                                        pattern=back, channel_multiplier=-1))

            blocks(headmask[:, :, :], PAIR)
            blocks(odd[:, :], HD)
            link(pool.tensor_copy(odd[:, 0:1], odd[:, 1:2]))
            for n in range(3, P // HD, 2):
                link(pool.tensor_tensor(odd[:, 0:1], odd[:, 0:1], odd[:, n:n + 1], ALU.add))
            root = HD ** -0.5
            link(pool.tensor_scalar(qscale[:, 0:1], odd[:, 0:1], 2 * root, -root, ALU.mult, ALU.add))
            pool.tensor_scalar(qscale[:, 1:2], odd[:, 0:1], -root, None, ALU.mult).then_inc(sem("const"), 1)

            def low_part(par, n, hi_count):
                at, size = PIECES[n]
                pool.wait_ge(sem("whi_done"), hi_count)
                pool.tensor_tensor(wlo[:, par, at:at + size], raw[:, at:at + size],
                                   f32(whi[:, par, at:at + size]), ALU.subtract).then_inc(sem("wlo_done"), 1)

            for n in range(STEPS):
                low_part(0, n, n + 1)

            def expert(i, par, prep):
                if prep:
                    e = 2 * i + par
                    pool.wait_ge(sem("down_done"), STEPS * e + OFF)
                    for n in range(STEPS):
                        low_part(1 - par, n, STEPS * (e + 1) + n + 1)

            with pool.Fori(0, E // 2 - 1) as i:
                for par in range(2):
                    expert(i, par, True)
            expert(E // 2 - 1, 0, True)

            pool.wait_ge(sem("down_done"), STEPS * E + OFF)
            for n in range(CH1):
                if n % HALF1 == 0:
                    pool.wait_ge(sem("experts1_in"), 16 * 3 * HALF1 * (n // HALF1 + 1))
                at, r = n * W1, raw[:, n % HALF1 * W1:(n % HALF1 + 1) * W1]
                link(pool.tensor_copy(whi1[:, at:at + W1], r))
                pool.tensor_tensor(wlo1[:, at:at + W1], r, f32(whi1[:, at:at + W1]), ALU.subtract)\
                    .then_inc(sem("w1split_done"), 1)

        CONST = 3 + 1 + 1 + E + 2 + 1

        @block.scalar
        def _(act):
            load_patches(act, 0, range(1, C, 2))
            act.wait_ge(sem("const"), CONST)

            def preload(func):
                cnt[0] += 1
                act.activation(tmp[:, :], eps_t[0:1, :], func).then_inc(sem("act_preload"), 1)
                act.wait_ge(sem("act_preload"), cnt[0])

            cnt = [0]
            preload(ACT.Sqrt)

            def norm(n, b, cols):
                a, z = cols
                act.wait_ge(sem("ln_dev", b), n)
                act.activation(sq[:, b, :, a:z], dev[:, b, :, a:z], ACT.Square).then_inc(sem("ln_sq", b), 1)

            def norm2(n, b, cols):
                a, z = cols
                act.wait_ge(sem("ln_var", b), n)
                act.activation(sd[:, b, a:z], bk(b, 3)[:, a:z], ACT.Sqrt, bias=eps_t[:, 0:1])\
                    .then_inc(sem("ln_sd", b), 1)

            def norms(n):
                for b in BS:
                    norm(n, b, (0, N))
                for b in BS:
                    norm2(n, b, (0, N))

            def tokens(b):
                for t in range(NTT):
                    act.wait_ge(sem("tok_nm", b), t + 1)
                    act.activation(dev[:, b, t, 0:D], bk(b, t)[:, 0:D], ACT.Square, bias=stat[:, b, t:t + 1],
                                   accum_out=stat[:, b, 4 + t:5 + t]).then_inc(sem("tok_sq", b), 1)
                    act.wait_ge(sem("tok_sq", b), t + 1)
                    act.activation(stat[:, b, 8 + t:9 + t], stat[:, b, 4 + t:5 + t], ACT.Sqrt,
                                   bias=eps_t[:, 0:1], scale=1.0 / D).then_inc(sem("tok_sd", b), 1)

            def tokens_out(b):
                for m in range(KT):
                    act.wait_ge(sem("tok_tr", b), m + 1)
                    act.activation(h[:, b, m, 1:S], bk(b, 2 + m)[:, 0:NTOK], ACT.Copy, scale=gamma_t[:, m:m + 1])\
                        .then_inc(sem("h_done", b), 1)

            tokens(0)
            act.wait_ge(sem("gamma_in"), 16)
            tokens_out(0)
            norm(1, 0, (0, N))
            tokens(1)
            norm2(1, 0, (0, N))
            tokens_out(1)
            norm(1, 1, (0, N))
            norm2(1, 1, (0, N))

            def high_part(par, n, e):
                at, size = PIECES[n]
                if n % 4 == 0:
                    act.wait_ge(sem("expert_in", n // 4), 64 * (e + 1) if n < 4 * KT else 32 * e + 16 * (par + 1))
                act.activation(whi[:, par, at:at + size], raw[:, at:at + size], ACT.Copy)\
                    .then_inc(sem("whi_done"), 1)

            act.wait_ge(sem("small_in"), 32)
            for b in BS:
                for m in range(2 * KT):
                    act.wait_ge(sem("qk_mm", b), m + 1)
                    act.activation(qk[:, b, m, :], bk(b, m)[:, 0:N], ACT.Identity, bias=bqkv0[:, m:m + 1])\
                        .then_inc(sem("qk_sb", b), 1)
            preload(ACT.Exp)
            for t, (_s0, rows) in enumerate(POS):
                for b in BS:
                    act.wait_ge(sem("sc_nm", b), t + 1)
                    act.activation(prob[0:rows, b, t, 0:S], bk(b, (3 + t) % 4)[0:rows, 0:S], ACT.Exp,
                                   bias=stat[0:rows, b, t:t + 1], scale=D ** -0.5,
                                   accum_out=stat[0:rows, b, 4 + t:5 + t]).then_inc(sem("sc_exp", b), 1)
            for n in range(3):
                high_part(0, n, 0)
            for b in BS:
                for j, (_s0, rows) in enumerate(POS):
                    act.wait_ge(sem("pt_mm", b), j + 1)
                    act.activation(probT[0:rows, b, j, 0:S], bk(b, (2 + j) % 4)[0:rows, 0:S], ACT.Copy)\
                        .then_inc(sem("pt_sb", b), 1)
            for n in range(3, 6):
                high_part(0, n, 0)
            for b in BS:
                for m in range(KT):
                    act.wait_ge(sem("cx_mm", b), m + 1)
                    act.activation(cT[:, b, m, 0:S], bk(b, 1 + m)[:, 0:S], ACT.Identity,
                                   bias=bqkv0[:, 2 * KT + m:2 * KT + m + 1]).then_inc(sem("cx_sb", b), 1)
            for n in range(6, STEPS):
                high_part(0, n, 0)

            preload(ACT.Sqrt)
            norms(2)
            preload(ACT.Exp)
            act.wait_ge(sem("rt_shift"), 1)
            act.activation(merged(route), merged(logit), ACT.Exp).then_inc(sem("rt_exp"), 1)
            preload(ACT.Silu)

            def x_high(par, count):
                for b in BS:
                    act.wait_ge(sem("xs_done"), count + b + 1)
                    act.activation(xhi[:, par, b, :, :], sq[:, b, :, :], ACT.Copy).then_inc(sem("xhi_done"), 1)

            x_high(0, 0)
            act.nop().then_inc(sem("silu_done"), OFF)
            act.nop().then_inc(sem("hhi_done"), OFF)

            def act_expert(i, par, prep):
                e = 2 * i + par
                for s in range(STEPS):
                    c, b = divmod(s, 2)
                    rows = hidden(c, par)
                    k = STEPS * e + s
                    act.wait_ge(sem("up_done"), k + 1)
                    act.wait_ge(sem("hmul_done"), k - 1 + OFF)
                    act.activation(sg[rows, b, :], bk(b, 0)[gates(c, par), 0:N], ACT.Silu).then_inc(sem("silu_done"), 1)
                    if prep:
                        if s == 2:
                            act.wait_ge(sem("down_done"), STEPS * e + OFF)
                        for n in range(*PREP[s]):
                            high_part(1 - par, n, e + 1)
                        if s == 4:
                            x_high(1 - par, 2 * (e + 1))
                    act.wait_ge(sem("hmul_done"), k + 1 + OFF)
                    act.wait_ge(sem("down_done"), k - 3 + OFF)
                    act.activation(hslot((hhi, hhi_tail), s)[rows, :], hid[rows, b, :], ACT.Copy)\
                        .then_inc(sem("hhi_done"), 1)

            with act.Fori(0, E // 2 - 1) as i:
                for par in range(2):
                    act_expert(i, par, True)
            act_expert(E // 2 - 1, 0, True)
            act_expert(E // 2 - 1, 1, False)

            preload(ACT.Sqrt)
            norms(3)
            preload(ACT.Exp)
            for b in BS:
                for m in range(2 * NQ):
                    act.wait_ge(sem("qk1_mm", b), m + 1)
                    if m < NQ:
                        if m >= KT:
                            act.wait_ge(sem("qk1_sb", b), m - KT + 1)
                        act.activation(dev[:, b, m % KT, :].bitcast(F32R), bk(b, m % 4)[:, 0:N], ACT.Copy,
                                       scale=qscale[:, 0:1]).then_inc(sem("qk1_hi", b), 1)
                    else:
                        act.activation(khi(b, m - NQ), bk(b, m % 4)[:, 0:N], ACT.Copy)\
                            .then_inc(sem("qk1_hi", b), 1)
            def last_exp():
                for b in BS:
                    act.wait_ge(sem("last_nm", b), 1)
                    act.activation(plast[:, b, 0:S], last_scored(b, S), ACT.Exp, bias=lstat[:, b, 1:2],
                                   scale=-1.0, accum_out=lstat[:, b, 2:3]).then_inc(sem("last_exp", b), 1)

            def head_exp(g):
                b, n = divmod(g, NH)
                if g >= 3:
                    act.wait_ge(sem("hp_mm"), g - 2)
                for t, (a, z) in enumerate(((0, P), (P, 3 * P))):
                    act.wait_ge(sem("hs_max"), 2 * g + t + 1)
                    act.activation(ph[:, g % 3, a:z], scm[:, g % 3, a:z], ACT.Exp, bias=hnm[:, g % 3, t:t + 1],
                                   scale=-1.0, accum_out=hsum[:, b, n // HPQ, t, n % HPQ:n % HPQ + 1]).then_inc(sem("hs_exp"), 1)

            for g in range(NB * NH + 2):
                if g < NB * NH:
                    head_exp(g)
                if g >= 2 and g % 2 == 0:
                    head_evac(act, g - 2)
                if g == LAST + 1:
                    last_exp()

            preload(ACT.Sqrt)
            for b in BS:
                norm(4, b, (0, N))
                norm2(4, b, (0, N))
            preload(ACT.Exp)
            for b in BS:
                act.wait_ge(sem("ln_y", b), 4)
                act.activation(xhi[:, 0, b, :, :], y[:, b, :, :], ACT.Copy).then_inc(sem("xhi_done"), 1)
            act.wait_ge(sem("rt_shift"), 2)
            act.activation(rstat[:, :, :, 3:4].rearrange("p b r a -> p (b r) a"),
                           rstat[:, :, :, 2:3].rearrange("p b r a -> p (b r) a"), ACT.Exp).then_inc(sem("rt_exp"), 1)
            preload(ACT.Silu)
            K0 = STEPS * E
            for k in range(2 * CH1):
                c, b = divmod(k, 2)
                act.wait_ge(sem("up_done"), K0 + k + 1)
                act.wait_ge(sem("hmul_done"), K0 + k - 1 + OFF)
                act.activation(sg[:, b, :], bk(b, 0)[:, 0:N], ACT.Silu).then_inc(sem("silu_done"), 1)
                act.wait_ge(sem("hmul_done"), K0 + k + 1 + OFF)
                act.wait_ge(sem("down_done"), K0 + k - 3 + OFF)
                act.activation(hhi[:, k % 4, :], hid[:, b, :], ACT.Copy).then_inc(sem("hhi_done"), 1)
            for b in BS:
                for t, rows in ((0, P), (2, 1)):
                    act.wait_ge(sem("ot_mm", b), t + 1)
                    act.activation(v[0:rows, b, t, :], bk(b, (0, 1, 3)[t])[0:rows, 0:D], ACT.Copy)\
                        .then_inc(sem("y_out_ready", b), 1)

        @block.vector
        def _(dve):
            cnt = [0]

            def link(ins):
                cnt[0] += 1
                ins.then_inc(sem("dve_chain"), 1)
                dve.wait_ge(sem("dve_chain"), cnt[0])

            link(dve.memset(f32(zero[:, :]), 0.0))
            dve.nop().then_inc(sem("zero_ready"), 1)

            def norm_dev(n, b, src, cols):
                a, z = cols
                dve.wait_ge(sem("ln_mean", b), n)
                mean = bk(b, 2)[:, a:z].unsqueeze(1).to_broadcast([P, KT, z - a])
                dve.tensor_tensor(dev[:, b, :, a:z], src[:, b, :, a:z], mean, ALU.subtract)\
                    .then_inc(sem("ln_dev", b), 1)

            def norm_out(n, b, cols):
                a, z = cols
                dve.wait_ge(sem("ln_sd", b), n)
                link(dve.reciprocal(rstd[:, b, a:z], sd[:, b, a:z]))
                r = rstd[:, b, a:z].unsqueeze(1).to_broadcast([P, KT, z - a])
                dve.tensor_tensor(y[:, b, :, a:z], dev[:, b, :, a:z], r, ALU.mult).then_inc(sem("ln_y", b), 1)

            def norms(n):
                for b in BS:
                    norm_dev(n, b, h, (0, N))
                for b in BS:
                    norm_out(n, b, (0, N))

            def tokens(b):
                for t in range(NTT):
                    dve.wait_ge(sem("tok_mm", b), t + 1)
                    link(dve.tensor_reduce(stat[:, b, 12 + t:13 + t], bk(b, t)[:, 0:D], AX, ALU.add))
                    dve.tensor_scalar(stat[:, b, t:t + 1], stat[:, b, 12 + t:13 + t], -1.0 / D, None, ALU.mult)\
                        .then_inc(sem("tok_nm", b), 1)
                for t in range(NTT):
                    dve.wait_ge(sem("tok_sd", b), t + 1)
                    link(dve.reciprocal(stat[:, b, 12 + t:13 + t], stat[:, b, 8 + t:9 + t]))
                    dve.tensor_scalar(v[:, b, t, :], bk(b, t)[:, 0:D], stat[:, b, t:t + 1],
                                      stat[:, b, 12 + t:13 + t], ALU.add, ALU.mult).then_inc(sem("tok_sb", b), 1)

            tokens(0)
            norm_dev(1, 0, h, (0, N))
            tokens(1)
            norm_out(1, 0, (0, N))
            norm_dev(1, 1, h, (0, N))
            norm_out(1, 1, (0, N))
            for b in BS:
                for t, (_s0, rows) in enumerate(POS):
                    dve.wait_ge(sem("v_mm", b), t + 1)
                    dve.tensor_copy(v[0:rows, b, t, :], bk(b, t)[0:rows, 0:D]).then_inc(sem("v_sb", b), 1)
            for t, (_s0, rows) in enumerate(POS):
                for b in BS:
                    dve.wait_ge(sem("sc_mm", b), t + 1)
                    link(dve.tensor_reduce(stat[0:rows, b, 8 + t:9 + t], bk(b, (3 + t) % 4)[0:rows, 0:S], AX,
                                           ALU.max))
                    dve.tensor_scalar(stat[0:rows, b, t:t + 1], stat[0:rows, b, 8 + t:9 + t], -D ** -0.5, None,
                                      ALU.mult).then_inc(sem("sc_nm", b), 1)
            for t, (_s0, rows) in enumerate(POS):
                for b in BS:
                    dve.wait_ge(sem("sc_exp", b), t + 1)
                    link(dve.reciprocal(stat[0:rows, b, 12 + t:13 + t], stat[0:rows, b, 4 + t:5 + t]))
                    dve.tensor_scalar(prob[0:rows, b, t, 0:S], prob[0:rows, b, t, 0:S],
                                      stat[0:rows, b, 12 + t:13 + t], None, ALU.mult).then_inc(sem("prob_ok", b), 1)
            for m in range(KT):
                for b in BS:
                    dve.wait_ge(sem("op_mm", b), m + 1)
                    dve.scalar_tensor_tensor(out=h[:, b, m, 0:S], in0=bk(b, (3 + m) % 4)[:, 0:S],
                                             scalar=bo0[:, m:m + 1], in1=h[:, b, m, 0:S],
                                             op0=ALU.add, op1=ALU.add).then_inc(sem("h_done", b), 1)
            for b in BS:
                dve.wait_ge(sem("h_done", b), 2 * KT)
            norms(2)

            R = NB * NR

            def wide(ap):
                return ap.to_broadcast([RT, R, E])

            def col(n):
                return rstat[:, :, :, n:n + 1].rearrange("p b r a -> p (b r) a")

            lg, eq_, p1, p2, rs, rt = (merged(t) for t in (logit, eq, pick1, pick2, rest, route))

            def top(src, pick, n):
                link(dve.tensor_reduce(col(n), src, AX, ALU.max))
                link(dve.tensor_tensor(eq_, src, wide(col(n)), ALU.is_equal))
                link(dve.tensor_tensor(eq_, eq_, rank8[0:RT, :, :], ALU.mult))
                link(dve.tensor_reduce(col(4), eq_, AX, ALU.max))
                link(dve.tensor_tensor(pick, eq_, wide(col(4)), ALU.is_equal))

            def top2(src):
                top(src, p1, 0)
                link(dve.scalar_tensor_tensor(out=rs, in0=p1, scalar=-HUGE, in1=src, op0=ALU.mult, op1=ALU.add))
                top(rs, p2, 1)

            def logits_in(b):
                return bk(b, 0)[0:RT, 0:NR * E].rearrange("p (r e) -> p r e", e=E)

            for b in BS:
                dve.wait_ge(sem("rt_mm", b), 1)
                link(dve.tensor_copy(rest[:, b], logits_in(b)))
            link(dve.tensor_reduce(col(0), rs, AX, ALU.max))
            dve.tensor_tensor(lg, rs, wide(col(0)), ALU.subtract).then_inc(sem("rt_shift"), 1)
            dve.wait_ge(sem("rt_exp"), 1)
            link(dve.tensor_reduce(col(5), rt, AX, ALU.add))
            link(dve.reciprocal(col(6), col(5)))
            link(dve.tensor_tensor(lg, rt, wide(col(6)), ALU.mult))
            top2(lg)
            link(dve.tensor_tensor(eq_, p1, p2, ALU.add))
            dve.tensor_tensor(rt, eq_, lg, ALU.mult).then_inc(sem("rt_done"), 1)

            def scaled_x(e):
                for b in BS:
                    dve.wait_ge(sem("rt_in", b), 16)
                    w = big[:, b, :, bass.ds(e, 1)].rearrange("p n a -> p (a n)").unsqueeze(1)
                    dve.tensor_tensor(sq[:, b, :, :], y[:, b, :, :], w.to_broadcast([P, KT, N]), ALU.mult)\
                        .then_inc(sem("xs_done"), 1)

            def x_low(par, count):
                for b in BS:
                    dve.wait_ge(sem("xhi_done"), count + b + 1)
                    dve.tensor_tensor(xlo[:, par, b, :, :], sq[:, b, :, :], f32(xhi[:, par, b, :, :]), ALU.subtract)\
                        .then_inc(sem("xlo_done"), 1)

            for b in BS:
                dve.wait_ge(sem("rb_mm", b), 1)
                dve.tensor_tensor(sq[:, b, :, :], y[:, b, :, :],
                                  bk(b, 1)[:, 0:N].unsqueeze(1).to_broadcast([P, KT, N]), ALU.mult)\
                    .then_inc(sem("xs_done"), 1)
            x_low(0, 0)
            for name in ("hmul_done", "hlo_done"):
                dve.nop().then_inc(sem(name), OFF)

            def hidden_low(k, s, b, rows):
                dve.wait_ge(sem("hhi_done"), k + 1 + OFF)
                dve.tensor_tensor(hslot((hlo, hlo_tail), s)[rows, :], hid[rows, b, :],
                                  f32(hslot((hhi, hhi_tail), s)[rows, :]),
                                  ALU.subtract).then_inc(sem("hlo_done"), 1)

            def dve_expert(i, par, prep):
                e = 2 * i + par
                for s in range(STEPS):
                    c, b = divmod(s, 2)
                    rows, ups = hidden(c, par), 1 if c < HC - 1 else 0
                    k = STEPS * e + s
                    dve.wait_ge(sem("silu_done"), k + 1 + OFF)
                    dve.wait_ge(sem("hlo_done"), k - 1 + OFF)
                    dve.tensor_tensor(hid[rows, b, :], sg[rows, b, :], bk(b, ups)[rows, 0:N], ALU.mult)\
                        .then_inc(sem("hmul_done"), 1)
                    if prep and s == 2:
                        dve.wait_ge(sem("xlo_done"), 2 * (e + 1))
                        scaled_x(e + 1)
                    if prep and s == 6:
                        x_low(1 - par, 2 * (e + 1))
                    hidden_low(k, s, b, rows)

            with dve.Fori(0, E // 2 - 1) as i:
                for par in range(2):
                    dve_expert(i, par, True)
            dve_expert(E // 2 - 1, 0, True)
            dve_expert(E // 2 - 1, 1, False)
            for b in BS:
                for m in range(KT):
                    dve.wait_ge(sem("down_done"), STEPS * E + OFF - (1 - b))
                    dve.tensor_tensor(h[:, b, m, :], h[:, b, m, :], bk(b, 2 + m)[:, 0:N], ALU.add)\
                        .then_inc(sem("h_done", b), 1)
            for b in BS:
                dve.wait_ge(sem("h_done", b), 3 * KT)
            norms(3)
            for b in BS:
                for m in range(2 * NQ):
                    dve.wait_ge(sem("qk1_hi", b), m + 1)
                    if m < NQ:
                        dve.scalar_tensor_tensor(out=qsplit(b, m), in0=bk(b, m % 4)[:, 0:N],
                                                 scalar=qscale[:, 1:2], in1=dev[:, b, m % KT, :],
                                                 op0=ALU.mult, op1=ALU.add).then_inc(sem("qk1_sb", b), 1)
                    else:
                        dve.tensor_tensor(klo(b, m - NQ), bk(b, m % 4)[:, 0:N], f32(khi(b, m - NQ)), ALU.subtract)\
                            .then_inc(sem("qk1_sb", b), 1)
                if b == 0:
                    for k in range(KT):
                        dve.wait_ge(sem("wsum_mm"), 1)
                        dve.tensor_copy(wsum[:, k:k + 1], bank[5][:, 2 * k:2 * k + 1]).then_inc(sem("wsum_sb"), 1)
                for t, (_s0, rows) in enumerate(POS):
                    dve.wait_ge(sem("v1_mm", b), t + 1)
                    dve.tensor_copy(v[0:rows, b, t, :], bk(b, t)[0:rows, 0:D]).then_inc(sem("v1_sb", b), 1)
                dve.wait_ge(sem("qk1_sb", b), NQ)
                dve.tensor_tensor(qlast[:, b, :, :], headmask[:, :, :],
                                  f32((hhi, hlo)[b][:, :, S - 1:S]).to_broadcast([P, NQ, NH]), ALU.mult)\
                    .then_inc(sem("qlast_done", b), 1)
            def last_max():
                for b in BS:
                    dve.wait_ge(sem("last_mm"), 1)
                    dve.tensor_reduce(lstat[:, b, 1:2], last_scored(b, S), AX, ALU.min).then_inc(sem("last_nm", b), 1)

            def last_turned():
                dve.wait_ge(sem("last_mm"), 2)
                for n, (rows, j0, j1) in enumerate(((P, 0, 2), (1, 2, 3))):
                    dve.tensor_copy(plT[0:rows, :, j0:j1, :], bank[7][0:rows, 0:NB * 3 * NH]
                                    .rearrange("p (b j n) -> p b j n", b=NB, j=3)[:, :, j0:j1, :])\
                        .then_inc(sem("plT_sb"), 1)

            def last_out(b):
                dve.wait_ge(sem("last_mm"), 3)
                link(dve.tensor_tensor(olm[:, b], last_valued(b).rearrange("p (n c) -> p n c", c=HD),
                                       ident[0:NH, 0:NH].unsqueeze(2).to_broadcast([NH, NH, HD]), ALU.mult))
                link(dve.tensor_reduce(ol[:, b, :], olm[:, b].rearrange("p n c -> p c n"), AX, ALU.add))
                link(dve.reciprocal(lstat[:, b, 3:4], lstat[:, b, 2:3]))
                dve.tensor_scalar(ols[:, b, :], ol[:, b, :], lstat[:, b, 3:4], None, ALU.mult)\
                    .then_inc(sem("ols_done", b), 1)

            def head_max(g):
                dve.wait_ge(sem("hs_mm"), g + 1)
                if g >= 3:
                    dve.wait_ge(sem("hs_exp"), 2 * (g - 2))
                for t, (a, z) in enumerate(((0, P), (P, 3 * P))):
                    dve.tensor_tensor_reduce(scm[:, g % 3, a:z], bank[g % 3][:, 2 * a:a + z], causal[:, a:z], 1.0, HUGE,
                                             ALU.add, ALU.min, hnm[:, g % 3, t:t + 1]).then_inc(sem("hs_max"), 1)

            def group_evac(gr):
                dve.wait_ge(sem("av_mm"), HPQ * (gr + 1))
                if gr >= 2:
                    dve.wait_ge(sem("fold_mm"), gr - 1)
                dve.tensor_copy(oT[:, gr % 2, 0:2 * P], bank[4 + gr % 2][:, 0:2 * P]).then_inc(sem("oT_sb"), 1)

            def group_out(gr):
                b, gb = divmod(gr, NG)
                link(dve.reciprocal(hinv[:, b, gb], hsum[:, b, gb]))
                dve.wait_ge(sem("fold_mm"), gr + 1)
                inv = hinv[:, b, gb].rearrange("p t (u v) -> p (t u) v", v=2).unsqueeze(3)
                dve.tensor_tensor(osb[:, b, gb].rearrange("p t (u v) c -> p (t u) v c", v=2),
                                  bank[7][:, 0:2 * P].rearrange("p (a w c) -> p a w c", w=4, c=HD)[:, :, 0:4:3, :],
                                  inv.to_broadcast([P, HPQ, 2, HD]), ALU.mult).then_inc(sem("osb_done", b), 1)

            def heads_add(b):
                for k in range(KT):
                    dve.wait_ge(sem("heads_in", b), 16 * (k + 1) * NG // KT)
                    dve.scalar_tensor_tensor(out=h[:, b, k, 0:S], in0=cT[:, b, k, 0:S], scalar=wsum[:, k:k + 1],
                                             in1=h[:, b, k, 0:S], op0=ALU.mult, op1=ALU.add)\
                        .then_inc(sem("h_done", b), 1)

            dve.wait_ge(sem("wsum_sb"), KT)
            for g in range(GEND):
                if g < NB * NH:
                    head_max(g)
                if 2 <= g < NB * NH + 2 and g % 2 == 1:
                    head_evac(dve, g - 2)
                if g == LAST:
                    last_max()
                if g == LAST + 3:
                    last_turned()
                if g in (LAST + 5, LAST + 6):
                    last_out(g - LAST - 5)
                gr, at = divmod(g - LAG - HPQ, HPQ)
                if at == 0 and gr >= 0:
                    group_evac(gr)
                if at == 2 and gr >= 0:
                    group_out(gr)
                    if gr == NG + 1:
                        heads_add(0)
            for b in BS:
                if b:
                    heads_add(b)
                dve.wait_ge(sem("h_done", b), 4 * KT)
                norm_dev(4, b, h, (0, N))
                norm_out(4, b, (0, N))
            for b in BS:
                dve.wait_ge(sem("xhi_done"), 2 * E + b + 1)
                dve.tensor_tensor(xlo[:, 0, b, :, :], y[:, b, :, :], f32(xhi[:, 0, b, :, :]), ALU.subtract)\
                    .then_inc(sem("xlo_done"), 1)
            dve.wait_ge(sem("l1_in"), 64)
            for b in BS:
                dve.wait_ge(sem("rt_mm", b), 2)
                dve.tensor_tensor(logit[:, b], logits_in(b), ebias_t[:, :].unsqueeze(1).to_broadcast([RT, NR, E]),
                                  ALU.add).then_inc(sem("rt_read", b), 1)
            for b in BS:
                dve.wait_ge(sem("rt_read", b), 1)
            top2(lg)
            dve.tensor_tensor(col(2), col(1), col(0), ALU.subtract).then_inc(sem("rt_shift"), 1)
            dve.wait_ge(sem("rt_exp"), 2)
            link(dve.tensor_scalar(col(5), col(3), 1.0, None, ALU.add))
            link(dve.reciprocal(col(6), col(5)))
            link(dve.tensor_tensor(eq_, p2, wide(col(3)), ALU.mult))
            link(dve.tensor_tensor(rs, eq_, p1, ALU.add))
            dve.wait_ge(sem("rt_out", 1), 16)
            dve.tensor_tensor(rt, rs, wide(col(6)), ALU.mult).then_inc(sem("rt_done"), 1)
            K0 = STEPS * E
            for k in range(2 * CH1):
                c, b = divmod(k, 2)
                dve.wait_ge(sem("silu_done"), K0 + k + 1 + OFF)
                dve.wait_ge(sem("hlo_done"), K0 + k - 1 + OFF)
                if c < NSH:
                    dve.tensor_tensor(hid[:, b, :], sg[:, b, :], bk(b, 1)[:, 0:N], ALU.mult)\
                        .then_inc(sem("hmul_done"), 1)
                else:
                    dve.wait_ge(sem("rt_in", b), 32)
                    link(dve.tensor_tensor(hidw[:, :], sg[:, b, :], bk(b, 1)[:, 0:N], ALU.mult))
                    dve.tensor_tensor(hid[:, b, :], hidw[:, :], big[:, b, :, c - NSH], ALU.mult)\
                        .then_inc(sem("hmul_done"), 1)
                hidden_low(K0 + k, k % 4, b, slice(0, P))
            for b in BS:
                for m in range(KT):
                    dve.wait_ge(sem("down_done"), STEPS * E + 2 * CH1 + OFF - (1 - b))
                    dve.tensor_tensor(h[:, b, m, :], h[:, b, m, :], bk(b, 2 + m)[:, 0:N], ALU.add)\
                        .then_inc(sem("h_done", b), 1)
            for b in BS:
                dve.wait_ge(sem("ot_mm", b), 2)
                dve.tensor_copy(v[:, b, 1, :], bk(b, 1)[:, 0:D]).then_inc(sem("y_odd_ready", b), 1)

        @block.tensor
        def _(pe):
            def mm(o, w, m, start, stop, **kw):
                return pe.matmul(o, w, m, start=start, stop=stop, **kw)

            def keep_warm(i, count):
                for _ in range(count):
                    mm(bank[i][:, 0:N], zero[:, 0:P], zero[:, :], True, True)

            pe.wait_ge(sem("zero_ready"), 1)
            keep_warm(0, 60)
            def norm_mean(n, b, src, cols):
                a, z = cols
                for k in range(KT):
                    last = mm(bk(b, 2)[:, a:z], avg[:, :], src[:, b, k, a:z], k == 0, k == KT - 1)
                last.then_inc(sem("ln_mean", b), 1)

            def norm_var(n, b, cols):
                a, z = cols
                pe.wait_ge(sem("ln_sq", b), n)
                for k in range(KT):
                    last = mm(bk(b, 3)[:, a:z], avg[:, :], sq[:, b, k, a:z], k == 0, k == KT - 1)
                last.then_inc(sem("ln_var", b), 1)

            pe.wait_ge(sem("wtok_in"), 16 * JG)
            def tokens(b):
                pe.wait_ge(sem("patches_in", b), 16 * JG * (C - b))
                if b:
                    pe.wait_ge(sem("patches_in_sw", b), 16 * JG)
                for t in range(NTT):
                    for g in range(NJ):
                        rows = min(JG, PS - JG * g) * CI
                        last = mm(bk(b, t)[:, 0:D],
                                  patches[0:rows, b, t * P * PS + JG * g:(t + 1) * P * PS:PS], wtok[0:rows, g, :],
                                  g == 0, g == NJ - 1)
                    last.then_inc(sem("tok_mm", b), 1)

            def tokens_turn(b):
                pe.wait_ge(sem("tok_sb", b), NTT)
                for m in range(KT):
                    for t in range(NTT):
                        last = pe.transpose(bk(b, 2 + m)[:, t * P:(t + 1) * P], v[:, b, t, m * P:(m + 1) * P],
                                            ident[:, :])
                    last.then_inc(sem("tok_tr", b), 1)

            def norms(n):
                for b in BS:
                    pe.wait_ge(sem("h_done", b), n * KT)
                    norm_mean(n, b, h, (0, N))
                for b in BS:
                    norm_var(n, b, (0, N))
                keep_warm(1, 38 if n == 2 else 18)

            def first_mean(b):
                pe.wait_ge(sem("cls_in", b), 16 * KT)
                pe.wait_ge(sem("h_done", b), KT)
                norm_mean(1, b, h, (0, N))

            def qk_tiles(b, tiles):
                for m in tiles:
                    for k in range(KT):
                        last = mm(bk(b, m)[:, 0:N], wqkv0[:, k, m * P:(m + 1) * P], y[:, b, k, :], k == 0, k == KT - 1)
                    last.then_inc(sem("qk_mm", b), 1)

            def value_tiles(b):
                for t, (s0, rows) in enumerate(POS):
                    pe.wait_ge(sem("qk_sb", b), t + 1)
                    for k in range(KT):
                        last = mm(bk(b, t)[0:rows, 0:D], y[:, b, k, s0:s0 + rows], wqkv0[:, k, 2 * D:3 * D],
                                  k == 0, k == KT - 1)
                    last.then_inc(sem("v_mm", b), 1)

            tokens(0)
            keep_warm(2, 10)
            pe.wait_ge(sem("const"), CONST)
            tokens_turn(0)
            first_mean(0)
            tokens(1)
            norm_var(1, 0, (0, N))
            tokens_turn(1)
            first_mean(1)
            pe.wait_ge(sem("wqkv0_in"), 16)
            pe.wait_ge(sem("ln_y", 0), 1)
            qk_tiles(0, range(0, 2))
            norm_var(1, 1, (0, N))
            qk_tiles(0, range(2, 2 * KT))
            value_tiles(0)
            pe.wait_ge(sem("ln_y", 1), 1)
            qk_tiles(1, range(2 * KT))
            value_tiles(1)
            for t, (s0, rows) in enumerate(POS):
                for b in BS:
                    pe.wait_ge(sem("qk_sb", b), 2 * KT)
                    if t:
                        pe.wait_ge(sem("v_sb", b), t)
                    for k in range(KT):
                        last = mm(bk(b, (3 + t) % 4)[0:rows, 0:S], qk[:, b, k, s0:s0 + rows],
                                  qk[:, b, KT + k, 0:S], k == 0, k == KT - 1)
                    last.then_inc(sem("sc_mm", b), 1)
            for b in BS:
                pe.wait_ge(sem("v_sb", b), 3)
            keep_warm(2, 20)
            for j, (k0, kn) in enumerate(POS):
                for b in BS:
                    pe.wait_ge(sem("prob_ok", b), 3)
                    for t, (s0, rows) in enumerate(POS):
                        last = pe.transpose(bk(b, (2 + j) % 4)[0:kn, s0:s0 + rows], prob[0:rows, b, t, k0:k0 + kn],
                                            ident[0:rows, 0:rows])
                    last.then_inc(sem("pt_mm", b), 1)
            for m in range(KT):
                for b in BS:
                    pe.wait_ge(sem("pt_sb", b), 3)
                    for j, (k0, kn) in enumerate(POS):
                        last = mm(bk(b, 1 + m)[:, 0:S], v[0:kn, b, j, m * P:(m + 1) * P], probT[0:kn, b, j, 0:S],
                                  j == 0, j == 2)
                    last.then_inc(sem("cx_mm", b), 1)
            pe.wait_ge(sem("wo0_in"), 16)
            for m in range(KT):
                for b in BS:
                    pe.wait_ge(sem("cx_sb", b), KT)
                    for k in range(KT):
                        last = mm(bk(b, (3 + m) % 4)[:, 0:S], wo0[:, k, m * P:(m + 1) * P], cT[:, b, k, 0:S],
                                  k == 0, k == KT - 1)
                    last.then_inc(sem("op_mm", b), 1)
            norms(2)

            def logits(layer, w):
                for b in BS:
                    pe.wait_ge(sem("ln_y", b), 2 if layer == 0 else 4)
                    for r in range(NR):
                        for k in range(KT):
                            last = mm(bk(b, 0)[0:RT, r * E:(r + 1) * E], y[:, b, k, r * RT:(r + 1) * RT], w[:, k, :],
                                      k == 0, k == KT - 1)
                    last.then_inc(sem("rt_mm", b), 1)

            pe.wait_ge(sem("gw_in"), 16 * KT)
            logits(0, gw)
            keep_warm(1, 6)
            pe.wait_ge(sem("rt_shift"), 1)
            keep_warm(1, 10)
            pe.wait_ge(sem("rt_exp"), 1)
            keep_warm(1, 14)
            pe.wait_ge(sem("rt_done"), 1)
            for b in BS:
                for r in range(NR):
                    last = mm(bk(b, 1)[:, r * RT:(r + 1) * RT], route[:, b, r, 0:1].to_broadcast([RT, P]),
                              ident[0:RT, 0:RT], True, True)
                last.then_inc(sem("rb_mm", b), 1)

            def clear_sums(layer):
                for b in BS:
                    for m in range(KT):
                        mm(bk(b, 2 + m)[:, 0:N], zero[:, 0:P], zero[:, :], True, False, skip_group_check=True)

            def split_mm(o, whi_, wlo_, mhi, mlo, start, stop):
                kw = dict(skip_group_check=True)
                mm(o, whi_, mhi, start, False, **kw)
                mm(o, whi_, mlo, False, False, **kw)
                return mm(o, wlo_, mhi, False, stop, **kw)

            def up(k, s, e_par, ready=None):
                c, b = divmod(s, 2)
                pe.wait_ge(sem("hmul_done"), k - 1 + OFF)
                for n in range(2 if c < HC - 1 else 1):
                    for kt in range(KT):
                        at = kt * WA + (c * P if n == 0 else MAIN + (c + 1) * P)
                        last = split_mm(bk(b, n)[:, 0:N], whi[:, e_par, at:at + P], wlo[:, e_par, at:at + P],
                                        xhi[:, e_par, b, kt, :], xlo[:, e_par, b, kt, :], kt == 0, kt == KT - 1)
                last.then_inc(sem("up_done"), 1)

            def down(k, s, e_par, final):
                c, b = divmod(s, 2)
                if c == HC - 1 and e_par == 0:
                    return
                pe.wait_ge(sem("hhi_done"), k + 1 + OFF)
                pe.wait_ge(sem("hlo_done"), k + 1 + OFF)
                mhi, mlo = hslot((hhi, hhi_tail), s), hslot((hlo, hlo_tail), s)
                for m in range(KT):
                    at = KT * WA + c * D + m * P
                    last = split_mm(bk(b, 2 + m)[:, 0:N], whi[:, e_par, at:at + P], wlo[:, e_par, at:at + P],
                                    mhi, mlo, False, final)
                last.then_inc(sem("down_done"), 3 if e_par == 0 and s == STEPS - 3 else 1)

            def expert_ready(e):
                pe.wait_ge(sem("wlo_done"), STEPS * (e + 1))
                pe.wait_ge(sem("whi_done"), STEPS * (e + 1))

            keep_warm(0, 8)
            clear_sums(0)
            pe.nop().then_inc(sem("down_done"), OFF)
            expert_ready(0)
            pe.wait_ge(sem("xlo_done"), 1)
            up(0, 0, 0)
            pe.wait_ge(sem("xlo_done"), 2)
            up(1, 1, 0)

            def pe_expert(i, par, more):
                e = 2 * i + par
                for s in range(STEPS):
                    k = STEPS * e + s
                    if s + 2 < STEPS:
                        up(k + 2, s + 2, par)
                    elif more:
                        if s + 2 == STEPS:
                            expert_ready(e + 1)
                            pe.wait_ge(sem("xlo_done"), 2 * (e + 2))
                        up(k + 2, s + 2 - STEPS, 1 - par)
                    down(k, s, par, (not more) and s >= STEPS - 2)

            with pe.Fori(0, E // 2 - 1) as i:
                for par in range(2):
                    pe_expert(i, par, True)
            pe_expert(E // 2 - 1, 0, True)
            pe_expert(E // 2 - 1, 1, False)

            norms(3)
            pe.wait_ge(sem("wqkv1_in"), 16 * 5 * KT)
            pe.wait_ge(sem("l1_in"), 64)
            for m in range(KT):
                for k in range(KT):
                    last = mm(bank[5][:, 2 * m:2 * m + 1], wo1[:, k, m * P:(m + 1) * P],
                              ones[:, 0:1], k == 0, k == KT - 1)
            last.then_inc(sem("wsum_mm"), 1)
            for b in BS:
                if b:
                    pe.wait_ge(sem("wsum_sb"), KT)
                pe.wait_ge(sem("ln_y", b), 3)
                for m in range(2 * NQ):
                    w = (wq1, wk1)[m // NQ][:, :, m % NQ * P:(m % NQ + 1) * P]
                    if m >= 4:
                        pe.wait_ge(sem("qk1_sb", b), m - 3)
                    for k in range(KT):
                        last = mm(bk(b, m % 4)[:, 0:N], w[:, k, :], y[:, b, k, :], k == 0, k == KT - 1)
                    last.then_inc(sem("qk1_mm", b), 1)
                for t, (s0, rows) in enumerate(POS):
                    pe.wait_ge(sem("qk1_sb", b), 2 * NQ - 3 + t)
                    for k in range(KT):
                        last = mm(bk(b, t)[0:rows, 0:D], y[:, b, k, s0:s0 + rows],
                                  wv1[:, k, :], k == 0, k == KT - 1)
                    last.then_inc(sem("v1_mm", b), 1)
            for b in BS:
                pe.wait_ge(sem("qk1_sb", b), 2 * NQ)
            pe.wait_ge(sem("v1_sb", 0), 3)
            def last_scores():
                for b in BS:
                    pe.wait_ge(sem("qlast_done", b), 1)
                    for t in range(NQ):
                        mm(last_scored(b, N), qlast[:, b, t, :], khi(b, t), t == 0, False)
                        ins = mm(last_scored(b, N), qlast[:, b, t, :], klo(b, t), False, t == NQ - 1)
                ins.then_inc(sem("last_mm"), 1)

            def last_turn():
                for b in BS:
                    pe.wait_ge(sem("last_exp", b), 1)
                for b in BS:
                    for j, (k0, kn) in enumerate(POS):
                        ins = pe.transpose(bank[7][0:kn, (3 * b + j) * NH:(3 * b + j + 1) * NH],
                                           plast[:, b, k0:k0 + kn], ident[0:NH, 0:NH])
                ins.then_inc(sem("last_mm"), 1)

            def last_values():
                pe.wait_ge(sem("plT_sb"), 2)
                for b in BS:
                    for j, (k0, kn) in enumerate(POS):
                        ins = mm(last_valued(b), plT[0:kn, b, j, :], v[0:kn, b, j, :], j == 0, j == 2)
                ins.then_inc(sem("last_mm"), 1)

            def head_scores(g):
                b, n = divmod(g, NH)
                t, p0 = n // HPQ, n % HPQ * PAIR
                if g >= 3:
                    pe.wait_ge(sem("hs_max"), 2 * (g - 2))
                keep_warm(g % 3, (3 if g < 9 else 1) if 2 <= g < 16 else 0)
                hi, lo = khi(b, t)[p0:p0 + PAIR, 0:2 * P], klo(b, t)[p0:p0 + PAIR, 0:2 * P]
                for i in range(2):
                    o, q = bank[g % 3][:, 2 * i * P:2 * (i + 1) * P], qsplit(b, t)[p0:p0 + PAIR, i * P:(i + 1) * P]
                    mm(o, q, hi, True, False)
                    last = mm(o, q, lo, False, True)
                last.then_inc(sem("hs_mm"), 1)

            def head_turn(g):
                pe.wait_ge(sem("hs_exp"), 2 * (g + 1))
                if g >= 2:
                    wait_evac(pe, g - 2)
                for j in range(3):
                    last = pe.transpose(turn_bank(g)[:, j * P:(j + 1) * P], ph[:, g % 3, j * P:(j + 1) * P],
                                        ident[:, :])
                last.then_inc(sem("hp_mm"), 1)

            def head_out(g):
                b, n = divmod(g, NH)
                wait_evac(pe, g)
                if n % HPQ == 0 and g >= 2 * HPQ:
                    pe.wait_ge(sem("oT_sb"), g // HPQ - 1)
                vn = v[:, b, :, n // 2 * PAIR:(n // 2 + 1) * PAIR]
                p0 = n % HPQ * PAIR
                o = bank[4 + g // HPQ % 2][p0:p0 + PAIR, 0:2 * P]
                mm(o[:, 0:2 * P], vn[:, 0, :], phT[:, g % 3, 0:2 * P], True, False, skip_group_check=True)
                mm(o[:, P:2 * P], vn[:, 1, :], phT[:, g % 3, 2 * P:3 * P], False, True, skip_group_check=True)\
                    .then_inc(sem("av_mm"), 1)

            def group_fold(gr):
                pe.wait_ge(sem("oT_sb"), gr + 1)
                if gr == 0:
                    pe.wait_ge(sem("ols_done", 1), 1)
                else:
                    pe.wait_ge(sem("osb_done", (gr - 1) // NG), (gr - 1) % NG + 1)
                for t in range(2):
                    last = pe.transpose(bank[7][:, t * P:(t + 1) * P], oT[:, gr % 2, t * P:(t + 1) * P], ident[:, :])
                last.then_inc(sem("fold_mm"), 1)

            for g in range(GEND):
                if g < NB * NH:
                    head_scores(g)
                if 2 <= g < NB * NH + 2:
                    head_turn(g - 2)
                if LAG <= g < NB * NH + LAG:
                    head_out(g - LAG)
                if g == LAST:
                    pe.wait_ge(sem("v1_sb", 1), 3)
                    last_scores()
                if g == LAST + 3:
                    last_turn()
                if g == LAST + 4:
                    last_values()
                gr, at = divmod(g - LAG - HPQ, HPQ)
                if at == 1 and gr >= 0:
                    group_fold(gr)

            for b in BS:
                pe.wait_ge(sem("h_done", b), 4 * KT)
                norm_mean(4, b, h, (0, N))
                norm_var(4, b, (0, N))
                keep_warm(1, 24)
            logits(1, wr1)
            clear_sums(1)
            pe.wait_ge(sem("w1split_done"), CH1)
            K0 = STEPS * E

            def up1(k):
                c, b = divmod(k, 2)
                pe.wait_ge(sem("hmul_done"), K0 + k - 1 + OFF)
                if c == 0:
                    pe.wait_ge(sem("rt_read", b), 1)
                    pe.wait_ge(sem("xlo_done"), 2 * E + b + 1)
                for n in range(2):
                    for kt in range(KT):
                        at = c * W1 + n * GU + kt * F1
                        last = split_mm(bk(b, n)[:, 0:N], whi1[:, at:at + F1], wlo1[:, at:at + F1],
                                        xhi[:, 0, b, kt, :], xlo[:, 0, b, kt, :], kt == 0, kt == KT - 1)
                last.then_inc(sem("up_done"), 1)

            def down1(k):
                c, b = divmod(k, 2)
                pe.wait_ge(sem("hhi_done"), K0 + k + 1 + OFF)
                pe.wait_ge(sem("hlo_done"), K0 + k + 1 + OFF)
                for m in range(KT):
                    at = c * W1 + 2 * GU + m * P
                    last = split_mm(bk(b, 2 + m)[:, 0:N], whi1[:, at:at + P], wlo1[:, at:at + P],
                                    hhi[:, k % 4, :], hlo[:, k % 4, :], False, c == CH1 - 1)
                last.then_inc(sem("down_done"), 1)

            for k in range(2 * CH1 + 2):
                if k < 2 * CH1:
                    up1(k)
                if k >= 2:
                    down1(k - 2)
            for b in BS:
                for t, (s0, rows) in enumerate(POS):
                    pe.wait_ge(sem("h_done", b), 5 * KT)
                    for k in range(KT):
                        last = pe.transpose(bk(b, (0, 1, 3)[t])[0:rows, k * P:(k + 1) * P], h[:, b, k, s0:s0 + rows],
                                            ident[:, :])
                    last.then_inc(sem("ot_mm", b), 1)


_INS = ['x', 'cls_tok', 'L0_tok_W', 'L0_tok_gamma', 'L0_attn_W_qkv', 'L0_attn_b_qkv', 'L0_attn_W_out',
        'L0_attn_b_out', 'L0_ffn_gate_w', 'L0_ffn_w1', 'L0_ffn_w2', 'L0_ffn_w3', 'L1_attn_W_qkv', 'L1_attn_W_out',
        'L1_ffn_Wr', 'L1_ffn_Wg', 'L1_ffn_Wu', 'L1_ffn_Wd', 'L1_ffn_Sg', 'L1_ffn_Su', 'L1_ffn_Sd',
        'L1_ffn_expert_bias']
_OUTS = [((2, 257, 256), 'float32')]


def kernel(**inputs):
    import numpy as _np
    import concourse.bacc as _bacc
    from concourse import mybir as _mybir
    from concourse.bass_utils import run_bass_kernel_spmd as _run

    nc = _bacc.Bacc("TRN2", target_bir_lowering=False, num_devices=1)
    arrays, args = {}, []
    for name in _INS:
        a = _np.ascontiguousarray(inputs[name])
        arrays[f"in_{name}_dram"] = a
        args.append(nc.dram_tensor(f"in_{name}_dram", a.shape, _mybir.dt.from_np(a.dtype), kind="ExternalInput").ap())
    for i, (shape, dtype) in enumerate(_OUTS):
        dt = _mybir.dt.from_np(_np.dtype(dtype))
        args.append(nc.dram_tensor(f"out_{i}_dram", shape, dt, kind="ExternalOutput").ap())
    vit_tower(nc, *args)
    r = _run(nc, [arrays], core_ids=[0])
    got = tuple(r.results[0][f"out_{i}_dram"] for i in range(len(_OUTS)))
    return got[0]
```
